# Optimizing a Trainium2 kernel written in Bass

```python
import numpy as np
import jax
import jax.numpy as jnp

def _softmax(x, axis=-1):
    return jax.nn.softmax(x, axis=axis)

def _gelu(x):
    return jax.nn.gelu(x, approximate=True)

def _silu(x):
    return jax.nn.silu(x)

def _sigmoid(x):
    return jax.nn.sigmoid(x)

def _layernorm(x, axis=-1, eps=1e-05):
    m = jnp.mean(x, axis=axis, keepdims=True)
    v = jnp.var(x, axis=axis, keepdims=True)
    return (x - m) / jnp.sqrt(v + eps)

def _scatter_add(tgt, idx, src, axis=0):
    return tgt.at[idx].add(src)

def _segment_sum(src, seg, n):
    return jax.ops.segment_sum(src, seg, n)
kernel_name = 'mk_seq_preln_d1_jaxref_r4_021d00'

def setup_inputs(seed: int=0):
    np.random.seed(seed)
    _w = jnp.asarray

    def _L0_attn_setup():
        import jax, jax.numpy as jnp
        import numpy as np
        B, L, D, H = (2, 512, 256, 16)
        C = D // H
        SCALE = 1.0 / np.sqrt(D).astype(np.float32)
        key = jax.random.key(seed)
        ks = jax.random.split(key, 5)
        return {'x': jax.random.normal(ks[0], (B, L, D), dtype=jnp.float32), 'w_qkv': jax.random.normal(ks[1], (3 * D, D), dtype=jnp.float32) * (1.0 / np.sqrt(D)), 'b_qkv': jax.random.normal(ks[2], (3 * D,), dtype=jnp.float32) * 0.02, 'w_o': jax.random.normal(ks[3], (D, D), dtype=jnp.float32) * (1.0 / np.sqrt(D)), 'b_o': jax.random.normal(ks[4], (D,), dtype=jnp.float32) * 0.02}
    _L0_attn_in = _L0_attn_setup()

    def _L0_ffn_setup():
        import jax, jax.numpy as jnp
        import numpy as np
        E = 8
        G = 4
        LG = 2
        TOPK = 2
        ROUTE_SCALE = 1.0

        def _grouped_mm(x, w, counts):
            counts = counts.astype(jnp.int32)
            if hasattr(jax.lax, 'ragged_dot'):
                return jax.lax.ragged_dot(x, w, counts)
            offs = jnp.cumsum(counts)
            eid = jnp.searchsorted(offs, jnp.arange(x.shape[0]), side='right')
            oh = jax.nn.one_hot(eid, w.shape[0], dtype=x.dtype)
            return jnp.einsum('nd,ne,edh->nh', x, oh, w)
        key = jax.random.key(seed)
        ks = jax.random.split(key, 8)
        bs, slen, dim, hid, shid = (2, 512, 256, 128, 256)
        std = 0.02
        return {'x': jax.random.normal(ks[0], (bs, slen, dim), jnp.float32), 'w_gate': jax.random.normal(ks[1], (E, dim), jnp.float32) * std, 'w1': jax.random.normal(ks[2], (E, dim, hid), jnp.float32) * std, 'w2': jax.random.normal(ks[3], (E, hid, dim), jnp.float32) * std, 'w3': jax.random.normal(ks[4], (E, dim, hid), jnp.float32) * std, 'sw1': jax.random.normal(ks[5], (shid, dim), jnp.float32) * std, 'sw2': jax.random.normal(ks[6], (dim, shid), jnp.float32) * std, 'sw3': jax.random.normal(ks[7], (shid, dim), jnp.float32) * std, 'expert_bias': jnp.zeros((E,), jnp.float32)}
    _L0_ffn_in = _L0_ffn_setup()
    _d = {'L0_attn_x': _L0_attn_in['x'], 'L0_attn_w_qkv': _L0_attn_in['w_qkv'], 'L0_attn_b_qkv': _L0_attn_in['b_qkv'], 'L0_attn_w_o': _L0_attn_in['w_o'], 'L0_attn_b_o': _L0_attn_in['b_o'], 'L0_ffn_w_gate': _L0_ffn_in['w_gate'], 'L0_ffn_w1': _L0_ffn_in['w1'], 'L0_ffn_w2': _L0_ffn_in['w2'], 'L0_ffn_w3': _L0_ffn_in['w3'], 'L0_ffn_sw1': _L0_ffn_in['sw1'], 'L0_ffn_sw2': _L0_ffn_in['sw2'], 'L0_ffn_sw3': _L0_ffn_in['sw3'], 'L0_ffn_expert_bias': _L0_ffn_in['expert_bias']}
    _x0 = _d['L0_attn_x']
    _d['L0_attn_x'] = jax.random.normal(jax.random.fold_in(jax.random.key(seed), 1), (4, 2048, 256), dtype=_x0.dtype)
    del _x0
    return _d

def reference(L0_attn_x, L0_attn_w_qkv, L0_attn_b_qkv, L0_attn_w_o, L0_attn_b_o, L0_ffn_w_gate, L0_ffn_w1, L0_ffn_w2, L0_ffn_w3, L0_ffn_sw1, L0_ffn_sw2, L0_ffn_sw3, L0_ffn_expert_bias):

    def _L0_attn_ref(x, w_qkv, b_qkv, w_o, b_o):
        import jax, jax.numpy as jnp
        import numpy as np
        B, L, D, H = (2, 512, 256, 16)
        C = D // H
        SCALE = 1.0 / np.sqrt(D).astype(np.float32)
        b, l, d = x.shape
        h, c = (H, d // H)
        qkv = jnp.einsum('bld,ed->ble', x, w_qkv) + b_qkv
        q, k, v = jnp.split(qkv, 3, axis=-1)
        q = q.reshape(b, l, h, c)
        k = k.reshape(b, l, h, c)
        v = v.reshape(b, l, h, c)
        attn = jax.nn.softmax(jnp.einsum('blhc,bmhc->bhlm', q, k) * SCALE, axis=-1)
        heads = jnp.einsum('bhlm,bmhc->blhc', attn, v).reshape(b, l, d)
        return jnp.einsum('bld,ed->ble', heads, w_o) + b_o + x

    def _L0_ffn_ref(x, w_gate, w1, w2, w3, sw1, sw2, sw3, expert_bias):
        import jax, jax.numpy as jnp
        import numpy as np
        E = 8
        G = 4
        LG = 2
        TOPK = 2
        ROUTE_SCALE = 1.0

        def _grouped_mm(x, w, counts):
            counts = counts.astype(jnp.int32)
            if hasattr(jax.lax, 'ragged_dot'):
                return jax.lax.ragged_dot(x, w, counts)
            offs = jnp.cumsum(counts)
            eid = jnp.searchsorted(offs, jnp.arange(x.shape[0]), side='right')
            oh = jax.nn.one_hot(eid, w.shape[0], dtype=x.dtype)
            return jnp.einsum('nd,ne,edh->nh', x, oh, w)
        bs, slen, dim = x.shape
        xf = x.reshape(-1, dim)
        N = xf.shape[0]
        logits = xf @ w_gate.T
        scores = jax.nn.softmax(logits.astype(jnp.float32), axis=-1)
        original = scores
        s = (scores + expert_bias).reshape(N, G, E // G)
        group_scores = jax.lax.top_k(s, 2)[0].sum(-1)
        top_groups = jax.lax.top_k(group_scores, LG)[1]
        keep = jnp.zeros((N, G), bool).at[jnp.arange(N)[:, None], top_groups].set(True)
        masked = jnp.where(keep[:, :, None], s, -jnp.inf).reshape(N, E)
        topk_idx = jax.lax.top_k(masked, TOPK)[1]
        weights = (jnp.take_along_axis(original, topk_idx, axis=1) * ROUTE_SCALE).astype(x.dtype)
        counts = jnp.bincount(topk_idx.reshape(-1), length=E)
        flat_idx = topk_idx.reshape(-1)
        routed_in = xf[flat_idx]
        routed_in = (routed_in.astype(jnp.float32) * weights.reshape(-1, 1)).astype(x.dtype)
        h = jax.nn.silu(_grouped_mm(routed_in, w1, counts)) * _grouped_mm(routed_in, w3, counts)
        routed_out = _grouped_mm(h, w2, counts)
        shared = jax.nn.silu(xf @ sw1.T) * (xf @ sw3.T) @ sw2.T
        out = shared.at[flat_idx].add(routed_out)
        return out.reshape(bs, slen, dim)
    x = L0_attn_x
    x = x + _L0_attn_ref(_layernorm(x, axis=-1), L0_attn_w_qkv, L0_attn_b_qkv, L0_attn_w_o, L0_attn_b_o)
    x = x + _L0_ffn_ref(_layernorm(x, axis=-1), L0_ffn_w_gate, L0_ffn_w1, L0_ffn_w2, L0_ffn_w3, L0_ffn_sw1, L0_ffn_sw2, L0_ffn_sw3, L0_ffn_expert_bias)
    return x

_drawn_inputs = setup_inputs


def setup_inputs(seed=0):
    import zlib

    import numpy as np

    out = dict(_drawn_inputs(seed))
    spreads = {'L0_ffn_expert_bias': (0.0, 0.8)}
    factors = {'L0_attn_w_qkv': 2.683,
     'L0_attn_b_qkv': 4.768,
     'L0_attn_b_o': 5.817,
     'L0_ffn_w_gate': 8.0,
     'L0_ffn_w1': 6.951,
     'L0_ffn_w2': 6.058,
     'L0_ffn_w3': 6.819,
     'L0_ffn_sw1': 6.758,
     'L0_ffn_sw2': 6.71,
     'L0_ffn_sw3': 6.699}
    for name, (base, spread) in spreads.items():
        noise = np.random.default_rng([zlib.crc32(name.encode()), seed]).standard_normal(out[name].shape)
        drawn = base * np.exp(spread * noise) if base else spread * noise
        out[name] = jnp.asarray(drawn.astype(out[name].dtype))
    for name, factor in factors.items():
        out[name] = (out[name] * factor).astype(out[name].dtype)
    return out
```

```python
from contextlib import ExitStack, nullcontext

import concourse.bass as bass
from concourse import mybir

F32, BF16, I32 = mybir.dt.float32, mybir.dt.bfloat16, mybir.dt.int32
ALU, ACT, AX = mybir.AluOpType, mybir.ActivationFunctionType, mybir.AxisListType
ds = bass.ds

B, L, D, H = 4, 2048, 256, 16
C = D // H
P = 128
TOK = B * L
TILES = TOK // P
GT = 4
GN = GT * P
GROUPS = TOK // GN
GPB = L // GN
DH = D // P
KT = L // P
HEADS = B * H
HPH = P // C
HID, NE, NG = 128, 8, 4
SCALE = 1.0 / D ** 0.5
EPS = 1e-5

Q_GROUPS = ((0, 3), (1, 2), (2, 1))
K_RUNS = ((0, 3), (0, 2), (0, 1))
SR = 6 * C
LEAST_SUM = 1e-26
NORM_UP = 1.02


def bcast(ap, pos, n):
    ap = ap.unsqueeze(pos)
    shape = list(ap.shape)
    shape[pos] = n
    return ap.broadcast_to(shape)


def wait_apart(eng, count, value, mark):
    eng.wait_ge(count, value)
    eng.sem_inc(mark, 1)


def flat(ap):
    return ap.rearrange("p a d -> p (a d)")


def qkv_stage(nc, sb, sem, ps, m):
    with ExitStack() as ctx:
        xln = sb(ctx, "xln", [P, 2, GT, D], F32)
        xT = sb(ctx, "xT", [P, 2, DH, GN], F32)
        r = sb(ctx, "r", [P, 2, GN], F32)
        r1 = sb(ctx, "r1", [P, 2, GN], F32)
        split = sb(ctx, "split", [P, 2, 4, 3, GN], BF16)
        sq = sb(ctx, "sq", [P, 4, GN], BF16)
        st6 = sb(ctx, "st6", [P, 2, GT, 6], F32)
        mv = sb(ctx, "mv", [P, 2, GT, 2], F32)
        veps = sb(ctx, "veps", [P, GT], F32)
        qn = sb(ctx, "qn", [HPH, 2, 2, GN], BF16)
        nmax = sb(ctx, "nmax", [HPH, 2, GROUPS], F32)
        kmax = sb(ctx, "kmax", [HPH, 2], F32)
        krow = xln[0:HPH, :, :, :].rearrange("h u t d -> h (u t d)").bitcast(BF16)[:, 0:2 * L].rearrange("h (a n) -> h a n", a=2)
        x_ld, kept, mark = sem("a_x_ld"), sem("a_kept"), sem("a_mark")
        bn, aggr, veps_ready, rstd_ready, xln_ready = (sem("a_bn"), sem("a_aggr"), sem("a_veps_ready"), sem("a_rstd_ready"),
                                                       sem("a_xln_ready"))
        tr_done, xT_ready, qk_done, v_done, v_evac = (sem("a_tr_done"), sem("a_xT_ready"), sem("a_qk_done"), sem("a_v_done"),
                                                      sem("a_v_evac"))
        r_ready, hi_ready, r1_ready, mid_ready, split_ready = (sem("a_r_ready"), sem("a_hi_ready"), sem("a_r1_ready"),
                                                               sem("a_mid_ready"), sem("a_split_ready"))
        stored = [sem("a_stored0"), sem("a_stored1")]
        sq_ready, nrm_done, nrm_red = sem("a_sq_ready"), sem("a_nrm_done"), sem("a_nrm_red")
        fin, v_stored, k_stored = sem("a_fin"), sem("a_v_stored"), sem("a_k_stored")
        tr = ps[:, 0:2, :]
        qkb = ps[:, 2:4, :]
        vb = ps[:, 4:6, :].rearrange("p a (t d) -> p a t d", t=2)
        nb = ps[0:HPH, 6, :]
        block = ctx.enter_context(nc.Block())

        @block.sync
        def _(sp):
            def load_x(b):
                for c in range(GPB):
                    sp.dma_start(m.x[:, ds((b * GPB + c) * GT, GT), :], m.xg[ds(b * GPB + c, 1)].rearrange("o p t d -> p (o t) d")).then_inc(x_ld, 16)

            def store_qk(b):
                for c in range(GPB):
                    for j in range(4):
                        wait_apart(sp, split_ready, b * (GPB * 4) + (c * 4 + j + 3), mark)
                        sp.dma_start(m.scr[j // 2][:, ds(b * D + (j % 2) * P, P), c * GN:(c + 1) * GN]
                                     .rearrange("s p n -> p s n"),
                                     split[:, c % 2, j, :, :]).then_inc(stored[c % 2], 16)
                    wait_apart(sp, nrm_red, b * (4 * GPB) + (4 * c + 3), mark)
                    sp.dma_start(m.qn_dram[ds(b * H, H), c * GN:(c + 1) * GN].rearrange("(j h) n -> h j n", j=2),
                                 qn[:, c % 2, :, :]).then_inc(stored[c % 2], 16)
                wait_apart(sp, v_evac, b * GPB + (GPB + 1), mark)
                sp.dma_start(m.v_dram[:, ds(b * (H * KT * C), H * KT * C)], m.vflat[:, ds(b * (H * KT * C), H * KT * C)]).then_inc(v_stored, 16)

            load_x(0)
            with sp.Fori(0, B - 1) as b:
                wait_apart(sp, x_ld, b * (16 * GPB) + 16 * GPB, mark)
                load_x(b + 1)
                store_qk(b)
            store_qk(B - 1)
            for u in range(2):
                sp.wait_ge(stored[u], 80 * (GROUPS // 2 + 1))
            sp.wait_ge(v_stored, 16 * B)
            sp.wait_ge(fin, 4)
            for b in range(B):
                sp.dma_start(m.kmax_dram[b * H:(b + 1) * H, :].rearrange("(j h) n -> h j n", j=2), krow[:, :, :]).then_inc(k_stored, 16)
            sp.wait_ge(k_stored, 16 * B)

        @block.gpsimd
        def _(pool):
            def norm(g, c):
                wait_apart(pool, aggr, g + 1, mark)
                nc.gpsimd.tensor_scalar(veps[:, :], mv[:, c % 2, :, 1], EPS, None, ALU.add).then_inc(veps_ready, 1)
                pool.wait_ge(veps_ready, g + 1)
                nc.gpsimd.tensor_tensor(m.rstd1[:, ds(g * GT, GT)], veps[:, :], m.mhalf[:, 0:GT], ALU.pow).then_inc(rstd_ready, 1)

            def project(g, b, c):
                for j in range(4):
                    n = g * 4 + j
                    pool.wait_ge(r1_ready, n + 3)
                    wait_apart(pool, stored[c % 2], b * 160 + 80 * (c // 2 + 1), mark)
                    nc.gpsimd.tensor_copy(split[:, c % 2, j, 1, :], r1[:, j % 2, :]).then_inc(mid_ready, 1)
                    pool.wait_ge(mid_ready, n + 1)
                    nc.gpsimd.tensor_tensor(split[:, c % 2, j, 2, :], r1[:, j % 2, :], split[:, c % 2, j, 1, :],
                                            ALU.subtract).then_inc(split_ready, 1)

            norm(0, 0)

            def batch(b, last):
                for c in range(GPB):
                    g = b * GPB + c
                    if not (last and c == GPB - 1):
                        norm(g + 1, (c + 1) % GPB)
                    project(g, b, c)

            with pool.Fori(0, B - 1) as b:
                batch(b, False)
            batch(B - 1, True)

        @block.vector
        def _(dve):
            for count, free in ((r_ready, 2), (r1_ready, 2), (split_ready, 2), (xT_ready, 1), (v_done, 2), (v_evac, 1),
                                (nrm_done, 4), (nrm_red, 1), (tr_done, 2), (stored[0], 80), (stored[1], 80)):
                dve.sem_inc(count, free)

            def norm(g, b, c):
                if c == 0:
                    wait_apart(dve, x_ld, b * (16 * GPB) + 16 * GPB, mark)
                for t in range(GT):
                    last = nc.vector.bn_stats(st6[:, c % 2, t, :], flat(m.x[:, ds(g * GT + t, 1), :]))
                last.then_inc(bn, 1)
                wait_apart(dve, bn, g + 1, mark)
                for t in range(GT):
                    last = nc.vector.bn_aggr(mv[:, c % 2, t, :], st6[:, c % 2, t, :])
                last.then_inc(aggr, 1)
                dve.wait_ge(aggr, g + 1)
                nc.vector.tensor_copy(m.stat1[:, ds(g * GT, GT), :], mv[:, c % 2, :, :]).then_inc(kept, 1)
                dve.wait_ge(tr_done, g + 1)
                dve.wait_ge(rstd_ready, g + 1)
                for t in range(GT):
                    nc.vector.tensor_scalar(xln[:, c % 2, t, :], flat(m.x[:, ds(g * GT + t, 1), :]),
                                            mv[:, c % 2, t, 0:1], m.rstd1[:, ds(g * GT + t, 1)],
                                            ALU.subtract, ALU.mult).then_inc(xln_ready, 1)

            def project(g, b, c):
                dve.wait_ge(stored[c % 2], b * 160 + 80 * (c // 2 + 1))
                for j in range(4):
                    n = g * 4 + j
                    dve.wait_ge(r_ready, n + 3)
                    nc.vector.tensor_copy(split[:, c % 2, j, 0, :], r[:, j % 2, :]).then_inc(hi_ready, 1)
                    dve.wait_ge(hi_ready, n + 1)
                    dve.wait_ge(split_ready, n + 1)
                    nc.vector.tensor_tensor(r1[:, j % 2, :], r[:, j % 2, :], split[:, c % 2, j, 0, :],
                                            ALU.subtract).then_inc(r1_ready, 1)
                    dve.wait_ge(nrm_done, n + 1)
                    nc.vector.tensor_tensor(sq[:, j, :], split[:, c % 2, j, 0, :], split[:, c % 2, j, 0, :],
                                            ALU.mult).then_inc(sq_ready, 1)
                dve.wait_ge(v_done, g + 3)
                for a in range(2):
                    for t in range(2):
                        last = nc.vector.tensor_tensor(
                            m.vh[:, ds(b, 1), :, c * GT + 2 * a + t, :].rearrange("p o h c -> p (o h) c"),
                            vb[:, a, t, :].rearrange("p (h c) -> p h c", c=C),
                            m.bv[:, :].rearrange("p (h c) -> p h c", c=C), ALU.add)
                last.then_inc(v_evac, 1)
                for j in range(2, 4):
                    dve.wait_ge(nrm_done, g * 4 + j + 5)
                    nc.vector.reduce_max(nmax[:, j - 2, ds(g, 1)], nb, AX.X).then_inc(nrm_red, 1)

            norm(0, 0, 0)

            def batch(b, last):
                for c in range(GPB):
                    g = b * GPB + c
                    if not (last and c == GPB - 1):
                        norm(g + 1, b + (c + 1) // GPB, (c + 1) % GPB)
                    project(g, b, c)

            with dve.Fori(0, B - 1) as b:
                batch(b, False)
            batch(B - 1, True)

            dve.wait_ge(nrm_red, GROUPS * 4 + 1)
            nc.vector.reduce_max(kmax[:, :], nmax[:, :, :], AX.X).then_inc(fin, 1)
            nc.vector.memset(krow[:, :, :], -1.0).then_inc(fin, 1)
            dve.wait_ge(fin, 3)
            nc.vector.tensor_tensor(krow[:, :, :], krow[:, :, :], bcast(kmax[:, :], 2, L), ALU.mult).then_inc(fin, 1)
            dve.wait_ge(fin, 4)
            dve.wait_ge(kept, GROUPS)

        @block.scalar
        def _(act):

            def norm(g, c):
                act.wait_ge(tr_done, g + 3)
                act.wait_ge(v_done, g + 1)
                nc.scalar.copy(xT[:, c % 2, 0, :], tr[:, 0, :])
                nc.scalar.copy(xT[:, c % 2, 1, :], tr[:, 1, :]).then_inc(xT_ready, 1)

            def project(g, b, c):
                for j in range(4):
                    n = g * 4 + j
                    act.wait_ge(qk_done, n + 1)
                    act.wait_ge(r1_ready, n + 1)
                    nc.scalar.activation(r[:, j % 2, :], qkb[:, j % 2, :], ACT.Identity,
                                         bias=m.bqk[:, j:j + 1]).then_inc(r_ready, 1)
                act.wait_ge(stored[c % 2], b * 160 + 80 * (c // 2 + 1))
                for j in range(2):
                    act.wait_ge(nrm_done, g * 4 + j + 5)
                    nc.scalar.activation(qn[:, c % 2, j, :], nb, ACT.Sqrt, scale=NORM_UP).then_inc(nrm_red, 1)

            norm(0, 0)

            def batch(b, last):
                for c in range(GPB):
                    g = b * GPB + c
                    if not (last and c == GPB - 1):
                        norm(g + 1, (c + 1) % GPB)
                    project(g, b, c)

            with act.Fori(0, B - 1) as b:
                batch(b, False)
            batch(B - 1, True)
            act.wait_ge(fin, 2)
            nc.scalar.activation(kmax[:, :], kmax[:, :], ACT.Sqrt, scale=NORM_UP).then_inc(fin, 1)

        @block.tensor
        def _(pe):

            def norm(g, c):
                pe.wait_ge(xT_ready, g + 1)
                for t in range(GT):
                    pe.wait_ge(xln_ready, g * GT + t + 1)
                    for k in range(DH):
                        last = nc.tensor.transpose(tr[:, k, t * P:(t + 1) * P], xln[:, c % 2, t, k * P:(k + 1) * P], m.ident[:, :])
                last.then_inc(tr_done, 1)

            def project(g, c):
                pe.wait_ge(xT_ready, g + 2)
                for j in range(4):
                    pe.wait_ge(r_ready, g * 4 + j + 1)
                    for k in range(DH):
                        last = nc.tensor.matmul(qkb[:, j % 2, :], m.wqkv[:, k, j * P:(j + 1) * P], xT[:, c % 2, k, :],
                                                start=(k == 0), stop=(k == DH - 1))
                    last.then_inc(qk_done, 1)
                pe.wait_ge(v_evac, g + 1)
                for t in range(GT):
                    for k in range(DH):
                        last = nc.tensor.matmul(vb[:, t // 2, t % 2, :], xT[:, c % 2, k, t * P:(t + 1) * P],
                                                m.wqkv[:, k, 2 * D:3 * D], start=(k == 0), stop=(k == DH - 1))
                last.then_inc(v_done, 1)
                for j in range(4):
                    pe.wait_ge(sq_ready, g * 4 + j + 1)
                    pe.wait_ge(nrm_red, g * 4 + j + 1)
                    nc.tensor.matmul(nb, m.headsum[:, :], sq[:, j, :], start=True, stop=True).then_inc(nrm_done, 1)

            norm(0, 0)

            def batch(b, last):
                for c in range(GPB):
                    g = b * GPB + c
                    if not (last and c == GPB - 1):
                        norm(g + 1, (c + 1) % GPB)
                    project(g, c)

            with pe.Fori(0, B - 1) as b:
                batch(b, False)
            batch(B - 1, True)

def attention_stage(nc, sb_of, sem_of, ps, m, exact):
    run = "_exact" if exact else ""

    def sem(name):
        return sem_of(name + run)

    def sb(ctx, name, shape, dt):
        return sb_of(ctx, name + run, shape, dt)

    def when_needed(eng):
        if not exact:
            return nullcontext()
        return eng.If(eng.value_load(m.flag[0:1, 0:1], min_val=0, max_val=1) == 1)

    stack = SR + (2 if exact else 1)
    with ExitStack() as ctx:
        qs = [sb(ctx, f"qs{u}", [stack, L], BF16) for u in range(2)]
        ks = [sb(ctx, f"ks{u}", [stack, L], BF16) for u in range(2)]
        probs = sb(ctx, "probs", [P, 2, L], F32)
        vs = sb(ctx, "vs", [P, 2, KT, 2 * C], F32)
        osb = sb(ctx, "osb", [P, 2, 512], F32)
        rc = sb(ctx, "rc", [P, 2, 4, 4, 1], F32)
        rcmax = sb(ctx, "rcmax", [P, 4, 4, 1], F32)
        worst = sb(ctx, "worst", [P, 1], F32)
        verdict = sb(ctx, "verdict", [1, 2], F32)
        part = sb(ctx, "part", [P, KT, 4], F32)
        rowmax = sb(ctx, "rowmax", [P, KT], F32)
        shift = sb(ctx, "shift", [KT, 2, 2, P], BF16)
        setup, mark = sem("b_setup"), sem("b_mark")
        qk_ld = [sem("b_qk_ld0"), sem("b_qk_ld1")]
        sc_done, exp_done, pv_done, v_staged = sem("b_sc_done"), sem("b_exp_done"), sem("b_pv_done"), sem("b_v_staged")
        o_evac, tr_done, rc_ready, hd_done = sem("b_o_evac"), sem("b_tr_done"), sem("b_rc_ready"), sem("b_hd_done")
        if exact:
            mx_done, mx_red, row_ready, rowT, shi, shift_ready, v_ld = (
                sem("b_mx_done"), sem("b_mx_red"), sem("b_row_ready"), sem("b_rowT"), sem("b_shi"), sem("b_shift_ready"), sem("b_v_ld"))
            shift_ld = [sem("b_shift_ld0"), sem("b_shift_ld1")]
        else:
            kept, fin, worst_turned = sem("b_kept"), sem("b_fin"), sem("b_worst_turned")
        sc = [ps[:, 0:2, :], ps[:, 2:4, :]]
        ob = [ps[:, 4, :], ps[:, 5, :]]
        trb = ps[:, 6, :]
        mxb = ps[:, 7, :]
        PAIRS = HEADS // 2
        LOADS = 6 if exact else 8
        block = ctx.enter_context(nc.Block())

        @block.sync
        def _(sp):
            def load(n, u):
                row = 0
                for s, times in Q_GROUPS:
                    src = m.scr[0][s, ds(n * C, C), :]
                    sp.dma_start(qs[u][row:row + times * C, :], bcast(src, 0, times) if times > 1 else src).then_inc(qk_ld[u], 16)
                    row += times * C
                row = 0
                for s, parts in K_RUNS:
                    sp.dma_start(ks[u][row:row + parts * C, :], m.scr[1][s:s + parts, ds(n * C, C), :]).then_inc(qk_ld[u], 16)
                    row += parts * C
                if not exact:
                    sp.dma_start(qs[u][SR:SR + 1, :], m.qn_dram[ds(n, 1), :]).then_inc(qk_ld[u], 16)
                    sp.dma_start(ks[u][SR:SR + 1, :], m.kmax_dram[ds(n, 1), :]).then_inc(qk_ld[u], 16)

            def put_shift(n, u):
                if exact:
                    wait_apart(sp, shift_ready, n + 1, mark)
                    for a in range(2):
                        sp.dma_start(qs[u][SR + a:SR + a + 1, :], shift[:, u, a, :]).then_inc(shift_ld[u], 16)

            with when_needed(sp):
                if exact:
                    sp.wait_ge(setup, 3)
                    sp.dma_start(m.vflat, m.v_dram).then_inc(v_ld, 16)
                for u in range(2):
                    load(u, u)
                with sp.Fori(1, PAIRS) as i:
                    for u in range(2):
                        put_shift(2 * i + (u - 2), u)
                        wait_apart(sp, sc_done, i * (4 * KT) + (u - 1) * 2 * KT, mark)
                        load(2 * i + u, u)
                for u in range(2):
                    put_shift(HEADS - 2 + u, u)
                sp.nop()

        @block.gpsimd
        def _(pool):
            def stage_v(n, u):
                nc.gpsimd.tensor_copy(vs[:, u, :, 0:C], m.vflat[:, ds(n * (KT * C), KT * C)]
                                      .rearrange("p (t c) -> p t c", c=C)).then_inc(v_staged, 1)

            with when_needed(pool):
                nc.gpsimd.memset(vs[:, :, :, C:2 * C], 1.0).then_inc(setup, 1)
                if exact:
                    pool.wait_ge(v_ld, 16)
                for u in range(2):
                    stage_v(u, u)
                with pool.Fori(1, PAIRS) as i:
                    for u in range(2):
                        wait_apart(pool, pv_done, i * (2 * KT) + (u - 1) * KT + 2, mark)
                        stage_v(2 * i + u, u)

        @block.vector
        def _(dve):
            def row_max(n, i, u):
                for qt in range(KT):
                    for kc in range(4):
                        dve.wait_ge(mx_done, n * (4 * KT) + qt * 4 + kc + 1)
                        nc.vector.reduce_max(part[:, qt, kc:kc + 1], mxb, AX.X).then_inc(mx_red, 1)
                dve.wait_ge(mx_red, n * (4 * KT) + 4 * KT + 1)
                nc.vector.reduce_max(rowmax[:, :], part[:, :, :], AX.X).then_inc(row_ready, 1)
                dve.wait_ge(rowT, n + 1)
                dve.wait_ge(shift_ld[u], i * 32 + 32)
                nc.vector.tensor_scalar(shift[:, u, 0, :], mxb[0:KT, 0:P], -1.0, None, ALU.mult).then_inc(shi, 1)
                dve.wait_ge(shi, n + 1)
                nc.vector.scalar_tensor_tensor(out=shift[:, u, 1, :], in0=mxb[0:KT, 0:P], scalar=-1.0,
                                               in1=shift[:, u, 0, :], op0=ALU.mult, op1=ALU.subtract).then_inc(shift_ready, 1)

            def finish(n, u):
                dve.wait_ge(pv_done, n * KT + KT + 2)
                nc.vector.tensor_copy(osb[:, u, :], ob[u]).then_inc(o_evac, 1)
                dve.wait_ge(tr_done, n + 1)
                t = trb.rearrange("p (s j c) -> p s j c", s=4, j=4)
                nc.vector.reciprocal(rc[:, u, :, :, :], t[:, :, :, C:C + 1]).then_inc(rc_ready, 1)
                dve.wait_ge(rc_ready, n + 1)
                nc.vector.tensor_tensor(m.vflat[:, ds(n * (KT * C), KT * C)].rearrange("p (j s c) -> p s j c", j=4, s=4),
                                        t[:, :, :, 0:C], rc[:, u, :, :, :].broadcast_to([P, 4, 4, C]), ALU.mult).then_inc(hd_done, 1)
                if not exact:
                    dve.wait_ge(kept, n + 1)
                    nc.vector.tensor_tensor(rcmax[:, :, :, :], rcmax[:, :, :, :], rc[:, u, :, :, :], ALU.max).then_inc(kept, 1)

            def pair(i, last):
                for u in range(2):
                    n = 2 * i + u
                    if exact and not (last and u == 1):
                        row_max(n + 1, i + u, 1 - u)
                    finish(n, u)

            with when_needed(dve):
                for count, free in ((exp_done, 2), (pv_done, 2), (o_evac, 2), (hd_done, 1)):
                    dve.sem_inc(count, free)
                if exact:
                    for u in range(2):
                        nc.vector.memset(ks[u][SR:stack, :], 1.0).then_inc(setup, 1)
                    for count, free in ((mx_red, 1), (shift_ld[0], 32), (shift_ld[1], 32)):
                        dve.sem_inc(count, free)
                    row_max(0, 0, 0)
                else:
                    nc.vector.memset(rcmax[:, :, :, :], 0.0).then_inc(kept, 1)
                with dve.Fori(0, PAIRS - 1) as i:
                    pair(i, False)
                pair(PAIRS - 1, True)
                dve.wait_ge(hd_done, HEADS + 1)
            if not exact:
                dve.wait_ge(kept, HEADS + 1)
                nc.vector.reduce_max(worst[:, :], rcmax[:, :, :, :], AX.XYZ).then_inc(fin, 1)
                dve.wait_ge(worst_turned, 1)
                nc.vector.reduce_max(verdict[:, 0:1], mxb[0:1, 0:P], AX.X).then_inc(fin, 1)
                dve.wait_ge(fin, 2)
                nc.vector.tensor_scalar(verdict[:, 1:2], verdict[:, 0:1], 1.0 / LEAST_SUM, None, ALU.is_le).then_inc(fin, 1)
                dve.wait_ge(fin, 3)
                nc.vector.tensor_scalar(m.flag[:, :], verdict[:, 1:2], -1.0, 1.0, ALU.mult, ALU.add).then_inc(fin, 1)
                dve.wait_ge(fin, 4)

        @block.scalar
        def _(act):
            with when_needed(act):
                with act.Fori(0, PAIRS) as i:
                    for k in range(2 * KT):
                        act.wait_ge(pv_done, i * (2 * KT) + k + 1)
                        for half in range(2):
                            act.wait_ge(sc_done, i * (4 * KT) + 2 * k + half + 1)
                            nc.scalar.activation(probs[:, k % 2, half * (L // 2):(half + 1) * (L // 2)], sc[half],
                                                 ACT.Exp, scale=SCALE).then_inc(exp_done, 1)

        @block.tensor
        def _(pe):
            def max_scores(n, i, u):
                pe.wait_ge(qk_ld[u], i * (16 * LOADS) + 16 * LOADS)
                for qt in range(KT):
                    for kc in range(4):
                        pe.wait_ge(mx_red, n * (4 * KT) + qt * 4 + kc + 1)
                        nc.tensor.matmul(mxb, qs[u][0:SR, qt * P:(qt + 1) * P], ks[u][0:SR, kc * 512:(kc + 1) * 512],
                                         start=True, stop=True).then_inc(mx_done, 1)
                pe.wait_ge(row_ready, n + 1)
                nc.tensor.transpose(mxb[0:KT, 0:P], rowmax[:, :], m.ident[:, :]).then_inc(rowT, 1)
                pe.wait_ge(shift_ld[u], i * 32 + 64)
                pe.wait_ge(shift_ready, n + 1)

            def scores(n, u, kt):
                for half in range(2):
                    pe.wait_ge(exp_done, n * (2 * KT) + 2 * kt + half + 1)
                    for a in range(2):
                        q0 = (2 * half + a) * 512
                        last = nc.tensor.matmul(sc[half][:, a, :], ks[u][:, kt * P:(kt + 1) * P], qs[u][:, q0:q0 + 512],
                                                start=True, stop=True)
                    last.then_inc(sc_done, 1)

            def values(n, u, kt):
                if kt == 0:
                    pe.wait_ge(v_staged, n + 1)
                    pe.wait_ge(o_evac, n + 1)
                pe.wait_ge(exp_done, n * (2 * KT) + 2 * kt + 4)
                for j in range(4):
                    last = nc.tensor.matmul(ob[u][32 * j:32 * j + 2 * C, :], vs[:, u, kt, :], probs[:, kt % 2, j * 512:(j + 1) * 512],
                                            start=(kt == 0), stop=(kt == KT - 1))
                last.then_inc(pv_done, 1)

            def back(n, u):
                pe.wait_ge(o_evac, n + 3)
                pe.wait_ge(hd_done, n + 1)
                for s in range(4):
                    last = nc.tensor.transpose(trb[:, s * P:(s + 1) * P], osb[:, u, s * P:(s + 1) * P], m.ident[:, :])
                last.then_inc(tr_done, 1)

            def start_head(n, i, u):
                if exact:
                    max_scores(n, i, u)
                pe.wait_ge(qk_ld[u], i * (16 * LOADS) + 16 * LOADS)
                scores(n, u, 0)

            def pair(i, first, last):
                for u in range(2):
                    n = 2 * i + u
                    for kt in range(KT):
                        if kt + 1 < KT:
                            scores(n, u, kt + 1)
                        elif not (last and u == 1):
                            start_head(n + 1, i + u, 1 - u)
                        values(n, u, kt)
                        if kt == 2 and not (first and u == 0):
                            back(n - 1, 1 - u)

            with when_needed(pe):
                pe.wait_ge(setup, 3 if exact else 1)
                start_head(0, 0, 0)
                pair(0, True, False)
                with pe.Fori(1, PAIRS - 1) as i:
                    pair(i, False, False)
                pair(PAIRS - 1, False, True)
                back(HEADS - 1, 1)
            if not exact:
                pe.wait_ge(fin, 1)
                nc.tensor.transpose(mxb[0:1, 0:P], worst[:, :], m.ident[:, :]).then_inc(worst_turned, 1)


def dense_stage(nc, sb, sem, ps, m):
    with ExitStack() as ctx:
        hs = sb(ctx, "hs", [P, 2, GT, D], F32)
        hT = sb(ctx, "hT", [P, DH, GN], F32)
        fT = sb(ctx, "fT", [P, DH, GN], F32)
        xb = sb(ctx, "xb", [P, GT, D], F32)
        t1 = sb(ctx, "t1", [P, GT, D], F32)
        xf = sb(ctx, "xf", [P, 2, GT, D], F32)
        st6 = sb(ctx, "st6c", [P, GT, 6], F32)
        mv = sb(ctx, "mvc", [P, 2, GT, 2], F32)
        veps = sb(ctx, "vepsc", [P, GT], F32)
        th = sb(ctx, "th", [P, DH, GN], F32)
        gT = sb(ctx, "gT", [P, DH, GN], F32)
        y = sb(ctx, "y", [P, 2, GT, D], F32)
        hs_ready, xb_ready, ln1_ready, t1_ready = sem("c_hs_ready"), sem("c_xb_ready"), sem("c_ln1_ready"), sem("c_t1_ready")
        htr_done, hT_ready, pj_done, x1_ready = sem("c_htr_done"), sem("c_hT_ready"), sem("c_pj_done"), sem("c_x1_ready")
        bn, aggr, veps_ready, rstd_ready, xf_ready = (sem("c_bn"), sem("c_aggr"), sem("c_veps_ready"), sem("c_rstd_ready"),
                                                      sem("c_xf_ready"))
        ftr_done, fT_ready, lg_done, lg_evac = sem("c_ftr_done"), sem("c_fT_ready"), sem("c_lg_done"), sem("c_lg_evac")
        ab_done, th_ready, sg_ready, g_ready = sem("c_ab_done"), sem("c_th_ready"), sem("c_sg_ready"), sem("c_g_ready")
        so_done, y_ready, stored = sem("c_so_done"), sem("c_y_ready"), sem("c_stored")
        half_ready, kept, mark = sem("c_half_ready"), sem("c_kept"), sem("c_mark")
        tr = ps[:, 0:2, :]
        pj = ps[:, 2:4, :].rearrange("p a (t d) -> p (a t) d", t=2)
        so = ps[:, 4:6, :].rearrange("p a (t d) -> p (a t) d", t=2)
        lg = ps[:, 4, 0:GT * NE].rearrange("p (t e) -> p t e", e=NE)
        ab = [ps[:, 6:8, :], ps[:, 0:2, :]]
        block = ctx.enter_context(nc.Block())

        def pipeline(eng, join, feed):
            join(0, 0)
            with eng.Fori(0, GROUPS // 2 - 1) as i:
                for u in range(2):
                    join(2 * i + (u + 1), 1 - u)
                    feed(2 * i + u, u)
            g = GROUPS - 2
            join(g + 1, 1)
            feed(g, 0)
            feed(g + 1, 1)

        @block.sync
        def _(sp):
            sp.sem_inc(stored, 32)
            with sp.Fori(0, GROUPS // 2) as i:
                for u in range(2):
                    g = 2 * i + u
                    wait_apart(sp, y_ready, g + 2, mark)
                    sp.dma_start(m.og[ds(g, 1)].rearrange("o p t d -> p (o t) d"), y[:, u, :, :]).then_inc(stored, 16)
                    wait_apart(sp, stored, g * 16 + 48, mark)

        @block.gpsimd
        def _(pool):
            for count, free in ((htr_done, 2), (hT_ready, 1), (pj_done, 1), (x1_ready, 1), (ftr_done, 2), (fT_ready, 1),
                                (lg_evac, 1), (g_ready, 2), (so_done, 1), (y_ready, 1)):
                pool.sem_inc(count, free)
            with pool.Fori(0, B) as b:
                for c in range(GPB):
                    g = b * GPB + c
                    wait_apart(pool, htr_done, g + 1, mark)
                    for t in range(GT):
                        last = nc.gpsimd.tensor_copy(hs[:, c % 2, t, :].rearrange("p (h c) -> p h c", c=C),
                                                     m.vh[:, ds(b, 1), :, c * GT + t, :].rearrange("p o h c -> p (o h) c"))
                    last.then_inc(hs_ready, 1)
                    pool.wait_ge(x1_ready, g + 1)
                    nc.gpsimd.tensor_tensor(xb[:, :, :], m.x[:, ds(g * GT, GT), :], bcast(m.bo[:, :], 1, GT), ALU.add).then_inc(xb_ready, 1)
                    wait_apart(pool, aggr, g + 1, mark)
                    nc.gpsimd.tensor_scalar(veps[:, :], mv[:, c % 2, :, 1], EPS, None, ALU.add).then_inc(veps_ready, 1)
                    pool.wait_ge(veps_ready, g + 1)
                    nc.gpsimd.tensor_tensor(m.rstd2[:, ds(g * GT, GT)], veps[:, :], m.mhalf[:, 0:GT], ALU.pow).then_inc(rstd_ready, 1)

        @block.scalar
        def _(act):
            def join(g, u):
                act.wait_ge(htr_done, g + 3)
                act.wait_ge(pj_done, g + 1)
                nc.scalar.copy(hT[:, 0, :], tr[:, 0, :])
                nc.scalar.copy(hT[:, 1, :], tr[:, 1, :]).then_inc(hT_ready, 1)

            def feed(g, u):
                act.wait_ge(ftr_done, g + 3)
                nc.scalar.copy(fT[:, 0, :], tr[:, 0, :])
                nc.scalar.copy(fT[:, 1, :], tr[:, 1, :]).then_inc(fT_ready, 1)
                for k in range(DH):
                    act.wait_ge(ab_done, g * DH + k + 1)
                    if k == 0:
                        act.wait_ge(g_ready, g + 2)
                    nc.scalar.activation(th[:, k, :], ab[k][:, 0, :], ACT.Tanh, scale=0.5).then_inc(th_ready, 1)
                act.wait_ge(lg_done, g + 1)
                nc.scalar.copy(m.logits[:, ds(g * GT, GT), :], lg).then_inc(lg_evac, 1)

            pipeline(act, join, feed)

        @block.vector
        def _(dve):
            nc.vector.tensor_scalar(m.sw2h[:, :, :], m.sw2[:, :, :], 0.5, None, ALU.mult).then_inc(half_ready, 1)

            def join(g, u):
                for t in range(GT):
                    last = nc.vector.tensor_scalar(t1[:, t, :], flat(m.x[:, ds(g * GT + t, 1), :]),
                                                   m.stat1[:, ds(g * GT + t, 1), 0], m.rstd1[:, ds(g * GT + t, 1)], ALU.subtract, ALU.mult)
                last.then_inc(ln1_ready, 1)
                dve.wait_ge(ln1_ready, g + 1)
                dve.wait_ge(xb_ready, g + 1)
                nc.vector.tensor_tensor(t1[:, :, :], t1[:, :, :], xb[:, :, :], ALU.add).then_inc(t1_ready, 1)
                dve.wait_ge(t1_ready, g + 1)
                dve.wait_ge(pj_done, g + 2)
                nc.vector.tensor_tensor(m.x[:, ds(g * GT, GT), :], t1[:, :, :], pj, ALU.add).then_inc(x1_ready, 1)
                wait_apart(dve, x1_ready, g + 2, mark)
                for t in range(GT):
                    last = nc.vector.bn_stats(st6[:, t, :], flat(m.x[:, ds(g * GT + t, 1), :]))
                last.then_inc(bn, 1)
                wait_apart(dve, bn, g + 1, mark)
                for t in range(GT):
                    last = nc.vector.bn_aggr(mv[:, u, t, :], st6[:, t, :])
                last.then_inc(aggr, 1)
                dve.wait_ge(aggr, g + 1)
                nc.vector.tensor_copy(m.stat2[:, ds(g * GT, GT), :], mv[:, u, :, :]).then_inc(kept, 1)
                dve.wait_ge(rstd_ready, g + 1)
                dve.wait_ge(ftr_done, g + 1)
                for t in range(GT):
                    last = nc.vector.tensor_scalar(xf[:, u, t, :], flat(m.x[:, ds(g * GT + t, 1), :]),
                                                   mv[:, u, t, 0:1], m.rstd2[:, ds(g * GT + t, 1)], ALU.subtract, ALU.mult)
                last.then_inc(xf_ready, 1)

            def feed(g, u):
                for k in range(DH):
                    dve.wait_ge(th_ready, g * DH + k + 1)
                    nc.vector.scalar_tensor_tensor(out=th[:, k, :], in0=th[:, k, :], scalar=1.0, in1=ab[k][:, 0, :],
                                                   op0=ALU.add, op1=ALU.mult).then_inc(sg_ready, 1)
                    dve.wait_ge(sg_ready, g * DH + k + 1)
                    if k == 0:
                        dve.wait_ge(so_done, g + 1)
                    last = nc.vector.tensor_tensor(gT[:, k, :], th[:, k, :], ab[k][:, 1, :], ALU.mult)
                last.then_inc(g_ready, 1)
                dve.wait_ge(so_done, g + 2)
                dve.wait_ge(stored, g * 16 + 16)
                nc.vector.tensor_tensor(y[:, u, :, :], m.x[:, ds(g * GT, GT), :], so, ALU.add).then_inc(y_ready, 1)

            pipeline(dve, join, feed)

        @block.tensor
        def _(pe):
            pe.wait_ge(half_ready, 1)

            def join(g, u):
                pe.wait_ge(hs_ready, g + 1)
                pe.wait_ge(g_ready, g + 1)
                for t in range(GT):
                    for k in range(DH):
                        last = nc.tensor.transpose(tr[:, k, t * P:(t + 1) * P], hs[:, u, t, k * P:(k + 1) * P], m.ident[:, :])
                last.then_inc(htr_done, 1)
                pe.wait_ge(hT_ready, g + 2)
                pe.wait_ge(x1_ready, g + 1)
                for t in range(GT):
                    for k in range(DH):
                        last = nc.tensor.matmul(pj[:, t, :], hT[:, k, t * P:(t + 1) * P], m.wo[:, k, :], start=(k == 0), stop=(k == DH - 1))
                last.then_inc(pj_done, 1)

            def feed(g, u):
                pe.wait_ge(xf_ready, g + 1)
                for t in range(GT):
                    for k in range(DH):
                        last = nc.tensor.transpose(tr[:, k, t * P:(t + 1) * P], xf[:, u, t, k * P:(k + 1) * P], m.ident[:, :])
                last.then_inc(ftr_done, 1)
                pe.wait_ge(fT_ready, g + 2)
                pe.wait_ge(g_ready, g + 2)
                for h in range(DH):
                    for o, w in ((0, m.sw1), (1, m.sw3)):
                        for k in range(DH):
                            last = nc.tensor.matmul(ab[h][:, o, :], w[:, k, h * P:(h + 1) * P], fT[:, k, :], start=(k == 0), stop=(k == DH - 1))
                    last.then_inc(ab_done, 1)
                pe.wait_ge(y_ready, g + 1)
                for t in range(GT):
                    for k in range(DH):
                        last = nc.tensor.matmul(lg[:, t, :], fT[:, k, t * P:(t + 1) * P], m.wg[:, k, :], start=(k == 0), stop=(k == DH - 1))
                last.then_inc(lg_done, 1)
                pe.wait_ge(lg_evac, g + 2)
                pe.wait_ge(g_ready, g + 3)
                for t in range(GT):
                    for k in range(DH):
                        last = nc.tensor.matmul(so[:, t, :], gT[:, k, t * P:(t + 1) * P], m.sw2h[:, k, :], start=(k == 0), stop=(k == DH - 1))
                last.then_inc(so_done, 1)

            pipeline(pe, join, feed)


def routed_stage(nc, sb, sem, ps, m):
    RT = 2 * TILES
    JE = NE * NE
    QT = 2
    STEPS = TILES // QT
    BIG = 3.0e38
    with ExitStack() as ctx:
        w1 = sb(ctx, "w1", [P, DH, NE, HID], F32)
        w3 = sb(ctx, "w3", [P, DH, NE, HID], F32)
        w2 = sb(ctx, "w2", [P, NE, D], F32)
        big = m.vh[:, :, :, :, :].rearrange("p b h t c -> p (b h t c)")
        ohw = big[:, 0:RT * JE].rearrange("p (r j e) -> p r j e", j=NE, e=NE)
        ohb = big[:, RT * JE:RT * JE * 3 // 2].bitcast(BF16).rearrange("p (r j e) -> p r j e", j=NE, e=NE)
        rest = RT * JE * 3 // 2
        s8 = [big[:, rest + i * TILES * NE:rest + (i + 1) * TILES * NE].rearrange("p (t e) -> p t e", e=NE) for i in range(5)]
        one = [sb(ctx, f"one{i}", [P, TILES], F32) for i in range(3)]
        s4 = [sb(ctx, f"s4_{i}", [P, TILES, NG], F32) for i in range(5)]
        rest += 5 * TILES * NE
        ohk = big[:, rest:rest + RT * NE].rearrange("p (t k e) -> p t k e", k=2, e=NE)
        ohkw = sb(ctx, "ohkw", [P, TILES, 2, NE], F32)
        wk = sb(ctx, "wk", [P, TILES, 2], F32)
        reached = sb(ctx, "reached", [P, RT, NE + 1], F32)
        span = sb(ctx, "span", [P, RT, NE], F32)
        cnt = sb(ctx, "cnt", [P, NE], F32)
        csum = sb(ctx, "csum", [P, NE, NE], F32)
        offs = sb(ctx, "offs", [P, NE], F32)
        x0 = sb(ctx, "x0", [NE, D], F32)
        x0T = sb(ctx, "x0T", [P, DH, NE], F32)
        arow = sb(ctx, "arow", [NE, NE * HID], F32)
        a2 = sb(ctx, "a2", [P, HID], F32)
        arest = sb(ctx, "arest", [P, HID], F32)
        ad = sb(ctx, "ad", [P, 3, 2 * HID], BF16)
        bT = sb(ctx, "bT", [HID, NE, NE], F32)
        hT = sb(ctx, "hTd", [HID, NE, NE], F32)
        ohT = sb(ctx, "ohT", [P, 2, QT, P], BF16)
        z, th, sil = (m.x[:, (i + 1) * 4:(i + 2) * 4, :].rearrange("p t d -> p (t d)").rearrange("p (u r h) -> p u r h", u=2, h=HID)
                      for i in range(3))
        rows = sb(ctx, "rows", [NE, D], F32)
        final = sb(ctx, "final", [NE, D], F32)
        w_ld, rows_ld, a_ld, out_st = sem("d_w_ld"), sem("d_rows_ld"), sem("d_a_ld"), sem("d_out_st")
        step, shifted, exped = sem("d_step"), sem("d_shifted"), sem("d_exped")
        cnt_ready, cnt_sum, x0_ready, x0_tr, x0T_ready, tabs_done, arow_ready, tabs_ready = (
            sem("d_cnt_ready"), sem("d_cnt_sum"), sem("d_x0_ready"), sem("d_x0_tr"), sem("d_x0T_ready"), sem("d_tabs_done"),
            sem("d_arow_ready"), sem("d_tabs_ready"))
        ohb_ready, ohw_ready = sem("d_ohb_ready"), sem("d_ohw_ready")
        oh_tr, ohT_ready, a_done, z_ready, th_ready, sil_ready, sum_done = (
            sem("d_oh_tr"), sem("d_ohT_ready"), sem("d_a_done"), sem("d_z_ready"), sem("d_th_ready"), sem("d_sil_ready"), sem("d_sum_done"))
        g_done, h_ready, o_done, final_ready = sem("d_g_done"), sem("d_h_ready"), sem("d_o_done"), sem("d_final_ready")
        ab = ps[0:NE, 0:2, :]
        bTb = ps[:, 2, 0:JE].rearrange("p (e j) -> p e j", j=NE)
        x0b = ps[:, 3, 0:DH * NE].rearrange("p (k j) -> p k j", j=NE)
        cb = ps[:, 4, 0:NE]
        gb = ps[:, 5, 0:JE].rearrange("p (j e) -> p j e", e=NE)
        ab2 = [ps[:, 0, :], ps[:, 1, :]]
        trb = [ps[:, 6, :].bitcast(BF16), ps[:, 7, :].bitcast(BF16)]
        ob = ps[0:NE, 2, 0:D]
        block = ctx.enter_context(nc.Block())

        @block.sync
        def _(sp):
            for dst, src in ((w1, m.w1_dram), (w3, m.w3_dram)):
                for k in range(DH):
                    sp.dma_start(dst[:, k, :, :], src[:, k * P:(k + 1) * P, :].rearrange("e p h -> p e h")).then_inc(w_ld, 16)
            sp.dma_start(w2[:, :, :], m.w2_dram.rearrange("e p d -> p e d")).then_inc(w_ld, 16)
            sp.dma_start(rows[:, :], m.out_rows).then_inc(rows_ld, 16)
            sp.wait_ge(arow_ready, 1)
            for u in range(2):
                sp.dma_start(a2[u * JE:(u + 1) * JE, :], arow[:, :].rearrange("j (e h) -> j e h", h=HID)).then_inc(a_ld, 16)
            sp.wait_ge(final_ready, 1)
            sp.dma_start(m.out_rows, final[:, :]).then_inc(out_st, 16)
            sp.wait_ge(out_st, 16)

        @block.gpsimd
        def _(pool):
            nc.gpsimd.memset(ad[:, :, :], 0.0).then_inc(tabs_ready, 1)
            pool.wait_ge(ohw_ready, 1)
            quarter = RT // 4
            for i in range(4):
                s = slice(i * quarter, (i + 1) * quarter)
                nc.gpsimd.tensor_tensor(ohw[:, s, :, :], bcast(ohkw[:, :, :, :].rearrange("p t k e -> p (t k) e")[:, s, :], 3, NE),
                                        bcast(span[:, s, :], 2, NE), ALU.mult).then_inc(ohw_ready, 1)

        @block.scalar
        def _(act):
            act.wait_ge(shifted, 1)
            nc.scalar.activation(s8[0][:, :, :], s8[0][:, :, :], ACT.Exp).then_inc(exped, 1)
            with act.Fori(0, STEPS // 2) as i:
                for u in range(2):
                    q = 2 * i + u
                    act.wait_ge(oh_tr, q + 1)
                    act.wait_ge(a_done, q + 1)
                    nc.scalar.copy(ohT[:, u, :, :].rearrange("p t n -> p (t n)"), trb[u][:, 0:QT * P]).then_inc(ohT_ready, 1)
                    act.wait_ge(z_ready, q + 1)
                    act.wait_ge(sil_ready, q + 1)
                    nc.scalar.activation(th[:, u, :, :], z[:, u, :, :], ACT.Tanh, scale=0.5).then_inc(th_ready, 1)

        @block.vector
        def _(dve):
            for count, free in ((a_done, 2), (sil_ready, 2), (sum_done, 2), (z_ready, 0), (ohT_ready, 2)):
                if free:
                    dve.sem_inc(count, free)
            steps = [0]

            def link(ins):
                steps[0] += 1
                ins.then_inc(step, 1)
                dve.wait_ge(step, steps[0])

            V = nc.vector
            V.tensor_scalar(x0[:, :], m.x[0:NE, 0, :], m.stat2[0:NE, 0, 0:1], m.rstd2[0:NE, 0:1], ALU.subtract, ALU.mult).then_inc(x0_ready, 1)
            lg = m.logits[:, :, :]
            link(V.reduce_max(one[0][:, :], lg, AX.X))
            V.tensor_tensor(s8[0][:, :, :], lg, bcast(one[0][:, :], 2, NE), ALU.subtract).then_inc(shifted, 1)
            dve.wait_ge(x0_tr, 1)
            V.tensor_copy(x0T[:, :, :], x0b).then_inc(x0T_ready, 1)
            dve.wait_ge(exped, 1)
            link(V.reduce_sum(one[1][:, :], s8[0][:, :, :], AX.X))
            link(V.reciprocal(one[1][:, :], one[1][:, :]))
            scores = s8[1]
            link(V.tensor_tensor(scores[:, :, :], s8[0][:, :, :], bcast(one[1][:, :], 2, NE), ALU.mult))
            biased = s8[2]
            link(V.tensor_tensor(biased[:, :, :], scores[:, :, :], bcast(m.ebias[:, :], 1, TILES), ALU.add))

            def first_max(vals, n, tmp, pick):
                link(V.reduce_max(one[2][:, :], vals, AX.X))
                link(V.tensor_tensor(tmp, vals, bcast(one[2][:, :], 2, n), ALU.is_equal))
                link(V.scalar_tensor_tensor(out=tmp, in0=tmp, scalar=-float(n), in1=bcast(m.iota[:, 0:n], 1, TILES), op0=ALU.mult, op1=ALU.add))
                link(V.tensor_reduce(one[2][:, :], tmp, AX.X, ALU.min))
                link(V.tensor_scalar(one[2][:, :], one[2][:, :], float(n), None, ALU.add))
                link(V.tensor_tensor(pick, bcast(m.iota[:, 0:n], 1, TILES), bcast(one[2][:, :], 2, n), ALU.is_equal))

            pairs = biased[:, :, :].rearrange("p t (g o) -> p t g o", o=2)
            link(V.tensor_tensor(s4[0][:, :, :], pairs[:, :, :, 0], pairs[:, :, :, 1], ALU.add))
            first_max(s4[0][:, :, :], NG, s4[1][:, :, :], s4[2][:, :, :])
            link(V.scalar_tensor_tensor(out=s4[0][:, :, :], in0=s4[2][:, :, :], scalar=-BIG, in1=s4[0][:, :, :], op0=ALU.mult, op1=ALU.add))
            first_max(s4[0][:, :, :], NG, s4[1][:, :, :], s4[3][:, :, :])
            link(V.tensor_tensor(s4[2][:, :, :], s4[2][:, :, :], s4[3][:, :, :], ALU.add))
            link(V.tensor_scalar(s4[4][:, :, :], s4[2][:, :, :], BIG, -BIG, ALU.mult, ALU.add))
            masked = s8[3]
            mpair = masked[:, :, :].rearrange("p t (g o) -> p t g o", o=2)
            link(V.tensor_tensor(mpair, pairs, bcast(s4[2][:, :, :], 3, 2), ALU.mult))
            link(V.tensor_tensor(mpair, mpair, bcast(s4[4][:, :, :], 3, 2), ALU.add))
            first_max(masked[:, :, :], NE, s8[4][:, :, :], ohk[:, :, 0, :])
            link(V.scalar_tensor_tensor(out=masked[:, :, :], in0=ohk[:, :, 0, :], scalar=-BIG, in1=masked[:, :, :], op0=ALU.mult, op1=ALU.add))
            first_max(masked[:, :, :], NE, s8[4][:, :, :], ohk[:, :, 1, :])
            V.reduce_sum(cnt[:, :], ohk[:, :, :, :].rearrange("p t k e -> p e (t k)"), AX.X).then_inc(cnt_ready, 1)
            for k in range(2):
                link(V.tensor_tensor(s8[4][:, :, :], scores[:, :, :], ohk[:, :, k, :], ALU.mult))
                link(V.reduce_sum(wk[:, :, k], s8[4][:, :, :], AX.X))
                link(V.scalar_tensor_tensor(out=ohkw[:, :, k, :], in0=ohk[:, :, k, :], scalar=0.5, in1=bcast(wk[:, :, k], 2, NE),
                                            op0=ALU.mult, op1=ALU.mult))
            dve.wait_ge(cnt_sum, 1)
            link(V.tensor_tensor(csum[:, :, :], m.upto[:, :, :], bcast(cb, 1, NE), ALU.mult))
            link(V.reduce_sum(offs[:, :], csum[:, :, :], AX.X))
            link(V.memset(reached[:, :, 0:1], 1.0))
            link(V.tensor_tensor(reached[:, :, 1:NE + 1], bcast(m.rowno[:, :], 2, NE), bcast(offs[:, :], 1, RT), ALU.is_ge))
            V.tensor_tensor(span[:, :, :], reached[:, :, 0:NE], reached[:, :, 1:NE + 1], ALU.subtract).then_inc(ohw_ready, 1)
            dve.wait_ge(ohw_ready, 1)
            dve.wait_ge(tabs_done, 1)
            V.tensor_copy(arow[:, :], ab.rearrange("p a n -> p (a n)")).then_inc(arow_ready, 1)
            link(V.tensor_copy(bT[:, :, :], bTb))
            quarter = RT // 4
            for i in range(4):
                s = slice(i * quarter, (i + 1) * quarter)
                V.tensor_tensor(ohb[:, s, :, :], bcast(ohk[:, :, :, :].rearrange("p t k e -> p (t k) e")[:, s, :], 3, NE),
                                bcast(span[:, s, :], 2, NE), ALU.mult).then_inc(ohb_ready, 1)
                if i == 0:
                    dve.wait_ge(a_ld, 32)
                    dve.wait_ge(tabs_ready, 1)
                    for part in range(3):
                        src = a2 if part == 0 else arest
                        for u in range(2):
                            d = ad[u * JE:(u + 1) * JE, part, u * HID:(u + 1) * HID]
                            link(V.tensor_copy(d, src[u * JE:(u + 1) * JE, :]))
                            if part < 2:
                                link(V.tensor_tensor(arest[u * JE:(u + 1) * JE, :], src[u * JE:(u + 1) * JE, :], d, ALU.subtract))
                    V.memset(reached[:, 0:1, 0:1], 0.0).then_inc(tabs_ready, 1)

            with dve.Fori(0, STEPS // 2) as i:
                for u in range(2):
                    q = 2 * i + u
                    dve.wait_ge(a_done, q + 3)
                    V.tensor_tensor(z[:, u, :, :], ab2[u].rearrange("p (r h) -> p r h", h=HID),
                                    bcast(m.flatwk(wk, q), 2, HID), ALU.mult).then_inc(z_ready, 1)
                    dve.wait_ge(th_ready, q + 1)
                    dve.wait_ge(sum_done, q + 1)
                    V.scalar_tensor_tensor(out=sil[:, u, :, :], in0=th[:, u, :, :], scalar=1.0, in1=z[:, u, :, :],
                                           op0=ALU.add, op1=ALU.mult).then_inc(sil_ready, 1)
            dve.wait_ge(g_done, 1)
            V.tensor_tensor(hT[:, :, :], gb.rearrange("p j e -> p e j"), bT[:, :, :], ALU.mult).then_inc(h_ready, 1)
            dve.wait_ge(rows_ld, 16)
            dve.wait_ge(o_done, 1)
            V.tensor_tensor(final[:, :], rows[:, :], ob, ALU.add).then_inc(final_ready, 1)

        @block.tensor
        def _(pe):
            pe.wait_ge(x0_ready, 1)
            for k in range(DH):
                last = nc.tensor.transpose(x0b[:, k, :], x0[:, k * P:(k + 1) * P], m.ident[0:NE, 0:NE])
            last.then_inc(x0_tr, 1)
            pe.wait_ge(x0T_ready, 1)
            pe.wait_ge(w_ld, 16 * (2 * DH + 1))
            for a in range(2):
                for k in range(DH):
                    nc.tensor.matmul(ab[:, a, :], x0T[:, k, :], w1[:, k, 4 * a:4 * a + 4, :].rearrange("p e h -> p (e h)"),
                                     start=(k == 0), stop=(k == DH - 1))
            for e in range(NE):
                for k in range(DH):
                    last = nc.tensor.matmul(bTb[:, e, :], w3[:, k, e, :], x0T[:, k, :], start=(k == 0), stop=(k == DH - 1))
            last.then_inc(tabs_done, 1)
            pe.wait_ge(cnt_ready, 1)
            nc.tensor.matmul(cb, m.ones[:, :], cnt[:, :], start=True, stop=True).then_inc(cnt_sum, 1)
            pe.wait_ge(tabs_ready, 2)
            pe.wait_ge(arow_ready, 1)
            pe.wait_ge(ohb_ready, 4)
            pe.wait_ge(ohw_ready, 5)
            gflat = gb.rearrange("p j e -> p (j e)")
            nc.tensor.matmul(gflat, m.zeros[:, :], m.ones[:, 0:JE], start=True, stop=False)

            def gather(q, u):
                pe.wait_ge(ohT_ready, q + 1)
                for t in range(QT):
                    last = nc.tensor.transpose(trb[u][:, t * P:(t + 1) * P], m.rowtile(ohb, q * QT + t), m.identb[:, :])
                last.then_inc(oh_tr, 1)
                pe.wait_ge(ohT_ready, q + 3)
                pe.wait_ge(z_ready, q - 1) if False else None
                for t in range(QT):
                    for part in range(3):
                        last = nc.tensor.matmul(ab2[u][:, t * 2 * HID:(t + 1) * 2 * HID], ohT[:, u, t, :], ad[:, part, :],
                                                start=(part == 0), stop=(part == 2))
                last.then_inc(a_done, 1)

            def add_up(q, u):
                pe.wait_ge(sil_ready, q + 3)
                for t in range(QT):
                    for k in range(2):
                        last = nc.tensor.matmul(gflat, sil[:, u, 2 * t + k, :], m.rowhalf(ohw, q * (2 * QT) + (2 * t + k)), start=False, stop=False)
                last.then_inc(sum_done, 1)

            gather(0, 0)
            gather(1, 1)
            with pe.Fori(0, STEPS // 2 - 1) as i:
                for u in range(2):
                    add_up(2 * i + u, u)
                    gather(2 * i + (u + 2), u)
            for u in range(2):
                add_up(STEPS - 2 + u, u)
            nc.tensor.matmul(gflat, m.zeros[:, :], m.ones[:, 0:JE], start=False, stop=True).then_inc(g_done, 1)
            pe.wait_ge(h_ready, 1)
            for e in range(NE):
                last = nc.tensor.matmul(ob, hT[:, e, :], w2[:, e, :], start=(e == 0), stop=(e == NE - 1))
            last.then_inc(o_done, 1)


class Memory:
    pass


def preln_attention_moe(nc, x, w_qkvT, b_qk, b_v, w_oT, b_o, w_gateT, w1, w2, w3, sw1T, sw2T, sw3T, expert_bias,
                        ident, headsum, iota, upto, rowno, out):
    m = Memory()
    with ExitStack() as outer:
        def sb(ctx, name, shape, dt):
            return ctx.enter_context(nc.sbuf_tensor(name, shape, dt))

        def sem(name):
            return outer.enter_context(nc.semaphore(name))

        outer_sb = lambda name, shape, dt: sb(outer, name, shape, dt)
        ps = outer.enter_context(nc.psum_tensor("ps", [P, 8, 512], F32))
        m.x = outer_sb("x_sb", [P, TILES, D], F32)
        m.vh = outer_sb("vh", [P, B, H, KT, C], F32)
        m.vflat = m.vh[:, :, :, :, :].rearrange("p b h t c -> p (b h t c)")
        m.stat1 = outer_sb("stat1", [P, TILES, 2], F32)
        m.rstd1 = outer_sb("rstd1", [P, TILES], F32)
        m.stat2 = outer_sb("stat2", [P, TILES, 2], F32)
        m.rstd2 = outer_sb("rstd2", [P, TILES], F32)
        m.logits = outer_sb("logits", [P, TILES, NE], F32)
        m.wqkv = outer_sb("wqkv", [P, DH, 3 * D], F32)
        m.wo = outer_sb("wo", [P, DH, D], F32)
        m.sw1 = outer_sb("sw1", [P, DH, D], F32)
        m.sw2 = outer_sb("sw2", [P, DH, D], F32)
        m.sw2h = m.wqkv[:, :, 0:D]
        m.sw3 = outer_sb("sw3", [P, DH, D], F32)
        m.wg = outer_sb("wg", [P, DH, NE], F32)
        m.bqk = outer_sb("bqk", [P, 4], F32)
        m.bv = outer_sb("bv", [P, D], F32)
        m.bo = outer_sb("bo", [P, D], F32)
        m.ebias = outer_sb("ebias", [P, NE], F32)
        m.ident = outer_sb("ident", [P, P], F32)
        m.identb = outer_sb("identb", [P, P], BF16)
        headsum_f = outer_sb("headsum_f", [P, HPH], F32)
        m.headsum = outer_sb("headsum", [P, HPH], BF16)
        m.ones = outer_sb("ones", [P, P], F32)
        m.zeros = outer_sb("zeros", [P, P], F32)
        m.mhalf = outer_sb("mhalf", [P, GT], F32)
        m.iota = outer_sb("iota", [P, NE], F32)
        m.upto = outer_sb("upto", [P, NE, NE], F32)
        m.rowno = outer_sb("rowno", [P, 2 * TILES], F32)
        m.flag = outer_sb("flag", [1, 1], I32)
        m.scr = [nc.dram_tensor(f"{n}_parts", [3, B * D, L], BF16, kind="Internal").ap() for n in ("q", "k")]
        m.qn_dram = nc.dram_tensor("q_norms", [B * H, L], BF16, kind="Internal").ap()
        m.kmax_dram = nc.dram_tensor("k_largest", [B * H, L], BF16, kind="Internal").ap()
        m.v_dram = nc.dram_tensor("v_copy", [P, B * H * KT * C], F32, kind="Internal").ap()
        flat_x = x.rearrange("b l d -> (b l) d")
        flat_out = out.rearrange("b l d -> (b l) d")
        m.xg = flat_x.rearrange("(g t p) d -> g p t d", t=GT, p=P)
        m.og = flat_out.rearrange("(g t p) d -> g p t d", t=GT, p=P)
        m.out_rows = flat_out[0:NE, :]
        m.w1_dram, m.w2_dram, m.w3_dram = w1, w2, w3
        halves = lambda w: w.rearrange("(k p) n -> p k n", p=P)
        m.loads = [
            (m.ident[:, :], ident), (headsum_f[:, :], headsum), (m.wqkv[:, :, :], halves(w_qkvT)),
            (m.bqk[:, :], b_qk), (m.bv[:, :], b_v.partition_broadcast(P)),
            (m.bo[:, :], b_o.partition_broadcast(P)), (m.wo[:, :, :], halves(w_oT)), (m.wg[:, :, :], halves(w_gateT)),
            (m.sw1[:, :, :], halves(sw1T)), (m.sw2[:, :, :], halves(sw2T)), (m.sw3[:, :, :], halves(sw3T)),
            (m.ebias[:, :], expert_bias.partition_broadcast(P)), (m.iota[:, :], iota.partition_broadcast(P)),
            (m.upto[:, :, :], upto.partition_broadcast(P)), (m.rowno[:, :], rowno),
        ]
        m.flatwk = lambda wk, q: wk[:, :, :].rearrange("p t k -> p (t k)")[:, ds(q * 4, 4)]
        m.rowtile = lambda ohb, t: ohb.rearrange("p r j e -> p (r j e)")[:, ds(t * P, P)]
        m.rowhalf = lambda ohw, r: ohw.rearrange("p r j e -> p (r j e)")[:, ds(r * NE * NE, NE * NE)]

        w_ld, fill = sem("w_ld"), sem("fill")
        with nc.Block() as block:
            @block.sync
            def _(sp):
                for dst, src in m.loads:
                    sp.dma_start(dst, src).then_inc(w_ld, 16)

            @block.vector
            def _(dve):
                nc.vector.memset(m.ones[:, :], 1.0)
                nc.vector.memset(m.zeros[:, :], 0.0)
                nc.vector.memset(m.mhalf[:, :], -0.5)
                dve.wait_ge(w_ld, 16 * len(m.loads))
                nc.vector.tensor_copy(m.headsum[:, :], headsum_f[:, :])
                nc.vector.tensor_copy(m.identb[:, :], m.ident[:, :]).then_inc(fill, 1)
                dve.wait_ge(fill, 1)

        qkv_stage(nc, sb, sem, ps, m)
        attention_stage(nc, sb, sem, ps, m, exact=False)
        attention_stage(nc, sb, sem, ps, m, exact=True)
        dense_stage(nc, sb, sem, ps, m)
        routed_stage(nc, sb, sem, ps, m)


def kernel(**inputs):
    import numpy as np
    import concourse.bacc as bacc
    from concourse.bass_utils import run_bass_kernel_spmd

    whole = {k: np.asarray(v) for k, v in inputs.items()}
    plain = lambda name: np.ascontiguousarray(whole[name])
    turned = lambda name: np.ascontiguousarray(whole[name].T)
    row = np.arange(P)[:, None] * 2 + np.arange(TILES * 2)[None, :] // 2 * (2 * P) + np.arange(TILES * 2)[None, :] % 2
    arrays = {
        "x": plain("L0_attn_x"), "w_qkvT": turned("L0_attn_w_qkv"), 
        "b_qk": np.ascontiguousarray(whole["L0_attn_b_qkv"][:2 * D].reshape(4, P).T), "b_v": whole["L0_attn_b_qkv"][2 * D:],
        "w_oT": turned("L0_attn_w_o"), "b_o": plain("L0_attn_b_o"), "w_gateT": turned("L0_ffn_w_gate"),
        "w1": plain("L0_ffn_w1"), "w2": plain("L0_ffn_w2"), "w3": plain("L0_ffn_w3"),
        "sw1T": turned("L0_ffn_sw1"), "sw2T": turned("L0_ffn_sw2"), "sw3T": turned("L0_ffn_sw3"),
        "expert_bias": plain("L0_ffn_expert_bias"),
        "ident": np.eye(P, dtype=np.float32),
        "headsum": np.repeat(np.eye(HPH, dtype=np.float32), C, axis=0),
        "iota": np.arange(NE, dtype=np.float32),
        "upto": np.tril(np.ones((NE, NE), dtype=np.float32)),
        "rowno": row.astype(np.float32),
    }
    nc = bacc.Bacc("TRN2", target_bir_lowering=False, num_devices=1)
    args = [nc.dram_tensor(f"in_{n}", list(a.shape), mybir.dt.from_np(a.dtype), kind="ExternalInput").ap() for n, a in arrays.items()]
    out = nc.dram_tensor("out", [B, L, D], F32, kind="ExternalOutput").ap()
    preln_attention_moe(nc, *args, out)
    r = run_bass_kernel_spmd(nc, [{f"in_{n}": a for n, a in arrays.items()}], core_ids=[0])
    return r.results[0]["out"]
```

```python
from contextlib import ExitStack, nullcontext

import concourse.bass as bass
from concourse import mybir

F32, BF16, I32 = mybir.dt.float32, mybir.dt.bfloat16, mybir.dt.int32
ALU, ACT, AX = mybir.AluOpType, mybir.ActivationFunctionType, mybir.AxisListType
ds = bass.ds

B, L, D, H = 4, 2048, 256, 16
C = D // H
P = 128
TOK = B * L
TILES = TOK // P
GT = 4
GN = GT * P
GROUPS = TOK // GN
GPB = L // GN
DH = D // P
KT = L // P
HEADS = B * H
HPH = P // C
HID, NE, NG = 128, 8, 4
SCALE = 1.0 / D ** 0.5
EPS = 1e-5

Q_GROUPS = ((0, 3), (1, 2), (2, 1))
K_RUNS = ((0, 3), (0, 2), (0, 1))
SR = 6 * C
LEAST_SUM = 1e-26
NORM_UP = 1.02


def bcast(ap, pos, n):
    ap = ap.unsqueeze(pos)
    shape = list(ap.shape)
    shape[pos] = n
    return ap.broadcast_to(shape)


def wait_apart(eng, count, value, mark):
    eng.wait_ge(count, value)
    eng.sem_inc(mark, 1)


def flat(ap):
    return ap.rearrange("p a d -> p (a d)")


def qkv_stage(nc, sb, sem, ps, m):
    with ExitStack() as ctx:
        xln = sb(ctx, "xln", [P, 2, GT, D], F32)
        xT = sb(ctx, "xT", [P, 2, DH, GN], F32)
        r = sb(ctx, "r", [P, 2, GN], F32)
        r1 = sb(ctx, "r1", [P, 2, GN], F32)
        split = sb(ctx, "split", [P, 2, 4, 3, GN], BF16)
        sq = sb(ctx, "sq", [P, 4, GN], BF16)
        vst = sb(ctx, "vst", [P, 2, H, GT, C], F32)
        st6 = sb(ctx, "st6", [P, 2, GT, 6], F32)
        mv = sb(ctx, "mv", [P, 2, GT, 2], F32)
        veps = sb(ctx, "veps", [P, GT], F32)
        qn = sb(ctx, "qn", [HPH, 2, 2, GN], BF16)
        nmax = sb(ctx, "nmax", [HPH, 2, GROUPS], F32)
        kmax = sb(ctx, "kmax", [HPH, 2], F32)
        krow = xln[0:HPH, :, :, :].rearrange("h u t d -> h (u t d)").bitcast(BF16)[:, 0:2 * L].rearrange("h (a n) -> h a n", a=2)
        x_ld, kept, mark = sem("a_x_ld"), sem("a_kept"), sem("a_mark")
        bn, aggr, veps_ready, rstd_ready, xln_ready = (sem("a_bn"), sem("a_aggr"), sem("a_veps_ready"), sem("a_rstd_ready"),
                                                       sem("a_xln_ready"))
        tr_done, xT_ready, qk_done, v_done, v_evac = (sem("a_tr_done"), sem("a_xT_ready"), sem("a_qk_done"), sem("a_v_done"),
                                                      sem("a_v_evac"))
        r_ready, hi_ready, r1_ready, mid_ready, split_ready = (sem("a_r_ready"), sem("a_hi_ready"), sem("a_r1_ready"),
                                                               sem("a_mid_ready"), sem("a_split_ready"))
        stored = [sem("a_stored0"), sem("a_stored1")]
        sq_ready, nrm_done, nrm_red = sem("a_sq_ready"), sem("a_nrm_done"), sem("a_nrm_red")
        fin, k_stored = sem("a_fin"), sem("a_k_stored")
        tr = ps[:, 0:2, :]
        qkb = ps[:, 2:4, :]
        vb = ps[:, 4:6, :].rearrange("p a (t d) -> p a t d", t=2)
        nb = ps[0:HPH, 6, :]
        block = ctx.enter_context(nc.Block())

        @block.sync
        def _(sp):
            def load_x(b):
                for c in range(GPB):
                    sp.dma_start(m.x[:, ds((b * GPB + c) * GT, GT), :], m.xg[ds(b * GPB + c, 1)].rearrange("o p t d -> p (o t) d")).then_inc(x_ld, 16)

            def store_qk(b):
                for c in range(GPB):
                    for j in range(4):
                        wait_apart(sp, split_ready, b * (GPB * 4) + (c * 4 + j + 3), mark)
                        sp.dma_start(m.scr[j // 2][:, ds(b * D + (j % 2) * P, P), c * GN:(c + 1) * GN]
                                     .rearrange("s p n -> p s n"),
                                     split[:, c % 2, j, :, :]).then_inc(stored[c % 2], 16)
                    wait_apart(sp, nrm_red, b * (4 * GPB) + (4 * c + 3), mark)
                    sp.dma_start(m.qn_dram[ds(b * H, H), c * GN:(c + 1) * GN].rearrange("(j h) n -> h j n", j=2),
                                 qn[:, c % 2, :, :]).then_inc(stored[c % 2], 16)
                    wait_apart(sp, v_evac, b * GPB + (c + 2), mark)
                    sp.dma_start(m.v_dram[:, ds(b * H, H), c * GT * C:(c + 1) * GT * C],
                                 vst[:, c % 2, :, :, :].rearrange("p h t c -> p h (t c)")).then_inc(stored[c % 2], 16)

            load_x(0)
            with sp.Fori(0, B - 1) as b:
                wait_apart(sp, x_ld, b * (16 * GPB) + 16 * GPB, mark)
                load_x(b + 1)
                store_qk(b)
            store_qk(B - 1)
            for u in range(2):
                sp.wait_ge(stored[u], 96 * (GROUPS // 2 + 1))
            sp.wait_ge(fin, 4)
            for b in range(B):
                sp.dma_start(m.kmax_dram[b * H:(b + 1) * H, :].rearrange("(j h) n -> h j n", j=2), krow[:, :, :]).then_inc(k_stored, 16)
            sp.wait_ge(k_stored, 16 * B)

        @block.gpsimd
        def _(pool):
            def norm(g, c):
                wait_apart(pool, aggr, g + 1, mark)
                nc.gpsimd.tensor_scalar(veps[:, :], mv[:, c % 2, :, 1], EPS, None, ALU.add).then_inc(veps_ready, 1)
                pool.wait_ge(veps_ready, g + 1)
                nc.gpsimd.tensor_tensor(m.rstd1[:, ds(g * GT, GT)], veps[:, :], m.mhalf[:, 0:GT], ALU.pow).then_inc(rstd_ready, 1)

            def project(g, b, c):
                for j in range(4):
                    n = g * 4 + j
                    pool.wait_ge(r1_ready, n + 3)
                    wait_apart(pool, stored[c % 2], b * 192 + 96 * (c // 2 + 1), mark)
                    nc.gpsimd.tensor_copy(split[:, c % 2, j, 1, :], r1[:, j % 2, :]).then_inc(mid_ready, 1)
                    pool.wait_ge(mid_ready, n + 1)
                    nc.gpsimd.tensor_tensor(split[:, c % 2, j, 2, :], r1[:, j % 2, :], split[:, c % 2, j, 1, :],
                                            ALU.subtract).then_inc(split_ready, 1)

            norm(0, 0)

            def batch(b, last):
                for c in range(GPB):
                    g = b * GPB + c
                    if not (last and c == GPB - 1):
                        norm(g + 1, (c + 1) % GPB)
                    project(g, b, c)

            with pool.Fori(0, B - 1) as b:
                batch(b, False)
            batch(B - 1, True)

        @block.vector
        def _(dve):
            for count, free in ((r_ready, 2), (r1_ready, 2), (split_ready, 2), (xT_ready, 1), (v_done, 2), (v_evac, 1),
                                (nrm_done, 4), (nrm_red, 1), (tr_done, 2), (stored[0], 96), (stored[1], 96)):
                dve.sem_inc(count, free)

            def norm(g, b, c):
                if c == 0:
                    wait_apart(dve, x_ld, b * (16 * GPB) + 16 * GPB, mark)
                for t in range(GT):
                    last = nc.vector.bn_stats(st6[:, c % 2, t, :], flat(m.x[:, ds(g * GT + t, 1), :]))
                last.then_inc(bn, 1)
                wait_apart(dve, bn, g + 1, mark)
                for t in range(GT):
                    last = nc.vector.bn_aggr(mv[:, c % 2, t, :], st6[:, c % 2, t, :])
                last.then_inc(aggr, 1)
                dve.wait_ge(aggr, g + 1)
                nc.vector.tensor_copy(m.stat1[:, ds(g * GT, GT), :], mv[:, c % 2, :, :]).then_inc(kept, 1)
                dve.wait_ge(tr_done, g + 1)
                dve.wait_ge(rstd_ready, g + 1)
                for t in range(GT):
                    nc.vector.tensor_scalar(xln[:, c % 2, t, :], flat(m.x[:, ds(g * GT + t, 1), :]),
                                            mv[:, c % 2, t, 0:1], m.rstd1[:, ds(g * GT + t, 1)],
                                            ALU.subtract, ALU.mult).then_inc(xln_ready, 1)

            def project(g, b, c):
                dve.wait_ge(stored[c % 2], b * 192 + 96 * (c // 2 + 1))
                for j in range(4):
                    n = g * 4 + j
                    dve.wait_ge(r_ready, n + 3)
                    nc.vector.tensor_copy(split[:, c % 2, j, 0, :], r[:, j % 2, :]).then_inc(hi_ready, 1)
                    dve.wait_ge(hi_ready, n + 1)
                    dve.wait_ge(split_ready, n + 1)
                    nc.vector.tensor_tensor(r1[:, j % 2, :], r[:, j % 2, :], split[:, c % 2, j, 0, :],
                                            ALU.subtract).then_inc(r1_ready, 1)
                    dve.wait_ge(nrm_done, n + 1)
                    nc.vector.tensor_tensor(sq[:, j, :], split[:, c % 2, j, 0, :], split[:, c % 2, j, 0, :],
                                            ALU.mult).then_inc(sq_ready, 1)
                dve.wait_ge(v_done, g + 3)
                for a in range(2):
                    for t in range(2):
                        last = nc.vector.tensor_tensor(
                            vst[:, c % 2, :, 2 * a + t, :],
                            vb[:, a, t, :].rearrange("p (h c) -> p h c", c=C),
                            m.bv[:, :].rearrange("p (h c) -> p h c", c=C), ALU.add)
                last.then_inc(v_evac, 1)
                for j in range(2, 4):
                    dve.wait_ge(nrm_done, g * 4 + j + 5)
                    nc.vector.reduce_max(nmax[:, j - 2, ds(g, 1)], nb, AX.X).then_inc(nrm_red, 1)

            norm(0, 0, 0)

            def batch(b, last):
                for c in range(GPB):
                    g = b * GPB + c
                    if not (last and c == GPB - 1):
                        norm(g + 1, b + (c + 1) // GPB, (c + 1) % GPB)
                    project(g, b, c)

            with dve.Fori(0, B - 1) as b:
                batch(b, False)
            batch(B - 1, True)

            dve.wait_ge(nrm_red, GROUPS * 4 + 1)
            nc.vector.reduce_max(kmax[:, :], nmax[:, :, :], AX.X).then_inc(fin, 1)
            nc.vector.memset(krow[:, :, :], -1.0).then_inc(fin, 1)
            dve.wait_ge(fin, 3)
            nc.vector.tensor_tensor(krow[:, :, :], krow[:, :, :], bcast(kmax[:, :], 2, L), ALU.mult).then_inc(fin, 1)
            dve.wait_ge(fin, 4)
            dve.wait_ge(kept, GROUPS)

        @block.scalar
        def _(act):

            def norm(g, c):
                act.wait_ge(tr_done, g + 3)
                act.wait_ge(v_done, g + 1)
                nc.scalar.copy(xT[:, c % 2, 0, :], tr[:, 0, :])
                nc.scalar.copy(xT[:, c % 2, 1, :], tr[:, 1, :]).then_inc(xT_ready, 1)

            def project(g, b, c):
                for j in range(4):
                    n = g * 4 + j
                    act.wait_ge(qk_done, n + 1)
                    act.wait_ge(r1_ready, n + 1)
                    nc.scalar.activation(r[:, j % 2, :], qkb[:, j % 2, :], ACT.Identity,
                                         bias=m.bqk[:, j:j + 1]).then_inc(r_ready, 1)
                act.wait_ge(stored[c % 2], b * 192 + 96 * (c // 2 + 1))
                for j in range(2):
                    act.wait_ge(nrm_done, g * 4 + j + 5)
                    nc.scalar.activation(qn[:, c % 2, j, :], nb, ACT.Sqrt, scale=NORM_UP).then_inc(nrm_red, 1)

            norm(0, 0)

            def batch(b, last):
                for c in range(GPB):
                    g = b * GPB + c
                    if not (last and c == GPB - 1):
                        norm(g + 1, (c + 1) % GPB)
                    project(g, b, c)

            with act.Fori(0, B - 1) as b:
                batch(b, False)
            batch(B - 1, True)
            act.wait_ge(fin, 2)
            nc.scalar.activation(kmax[:, :], kmax[:, :], ACT.Sqrt, scale=NORM_UP).then_inc(fin, 1)

        @block.tensor
        def _(pe):

            def norm(g, c):
                pe.wait_ge(xT_ready, g + 1)
                for t in range(GT):
                    pe.wait_ge(xln_ready, g * GT + t + 1)
                    for k in range(DH):
                        last = nc.tensor.transpose(tr[:, k, t * P:(t + 1) * P], xln[:, c % 2, t, k * P:(k + 1) * P], m.ident[:, :])
                last.then_inc(tr_done, 1)

            def project(g, c):
                pe.wait_ge(xT_ready, g + 2)
                for j in range(4):
                    pe.wait_ge(r_ready, g * 4 + j + 1)
                    for k in range(DH):
                        last = nc.tensor.matmul(qkb[:, j % 2, :], m.wqkv[:, k, j * P:(j + 1) * P], xT[:, c % 2, k, :],
                                                start=(k == 0), stop=(k == DH - 1))
                    last.then_inc(qk_done, 1)
                pe.wait_ge(v_evac, g + 1)
                for t in range(GT):
                    for k in range(DH):
                        last = nc.tensor.matmul(vb[:, t // 2, t % 2, :], xT[:, c % 2, k, t * P:(t + 1) * P],
                                                m.wqkv[:, k, 2 * D:3 * D], start=(k == 0), stop=(k == DH - 1))
                last.then_inc(v_done, 1)
                for j in range(4):
                    pe.wait_ge(sq_ready, g * 4 + j + 1)
                    pe.wait_ge(nrm_red, g * 4 + j + 1)
                    nc.tensor.matmul(nb, m.headsum[:, :], sq[:, j, :], start=True, stop=True).then_inc(nrm_done, 1)

            norm(0, 0)

            def batch(b, last):
                for c in range(GPB):
                    g = b * GPB + c
                    if not (last and c == GPB - 1):
                        norm(g + 1, (c + 1) % GPB)
                    project(g, c)

            with pe.Fori(0, B - 1) as b:
                batch(b, False)
            batch(B - 1, True)

def attention_stage(nc, sb_of, sem_of, ps, m, exact):
    run = "_exact" if exact else ""

    def sem(name):
        return sem_of(name + run)

    def sb(ctx, name, shape, dt):
        return sb_of(ctx, name + run, shape, dt)

    def when_needed(eng):
        if not exact:
            return nullcontext()
        return eng.If(eng.value_load(m.flag[0:1, 0:1], min_val=0, max_val=1) == 1)

    stack = SR + (2 if exact else 1)
    PS = 4
    STEPS = 4 * KT
    slot = [s % 3 for s in range(STEPS - 1)] + [1]
    back_to = [next(d for d in range(1, STEPS) if slot[(s - d) % STEPS] == slot[s]) for s in range(STEPS)]
    with ExitStack() as ctx:
        qs = [sb(ctx, f"qs{u}", [stack, L], BF16) for u in range(2)]
        ks = [sb(ctx, f"ks{u}", [stack, L], BF16) for u in range(2)]
        probs = sb(ctx, "probs", [P, PS, L], F32)
        vst = sb(ctx, "vst_b", [P, 2, KT * C], F32)
        vs = sb(ctx, "vs", [P, 2, KT, 2 * C], F32)
        osb = sb(ctx, "osb", [P, 512], F32)
        sums = sb(ctx, "sums", [P, 512], F32)
        rc = sb(ctx, "rc", [P, 512], F32)
        hout = sb(ctx, "hout", [P, 2, 512], F32)
        rcmax = sb(ctx, "rcmax", [P, HEADS], F32)
        worst = sb(ctx, "worst", [P, 1], F32)
        verdict = sb(ctx, "verdict", [1, 2], F32)
        part = sb(ctx, "part", [P, KT, 4], F32)
        rowmax = sb(ctx, "rowmax", [P, KT], F32)
        shift = sb(ctx, "shift", [KT, 2, 2, P], BF16)
        setup, mark = sem("b_setup"), sem("b_mark")
        qk_ld = [sem("b_qk_ld0"), sem("b_qk_ld1")]
        sc_done, exp_done, pv_done, v_staged = sem("b_sc_done"), sem("b_exp_done"), sem("b_pv_done"), sem("b_v_staged")
        v_ld = [sem("b_v_ld0"), sem("b_v_ld1")]
        o_evac, sums_ready, rc_ready, hd_done = sem("b_o_evac"), sem("b_sums_ready"), sem("b_rc_ready"), sem("b_hd_done")
        hd_stored = [sem("b_hd_stored0"), sem("b_hd_stored1")]
        if exact:
            mx_done, mx_red, row_ready, rowT, shi, shift_ready = (
                sem("b_mx_done"), sem("b_mx_red"), sem("b_row_ready"), sem("b_rowT"), sem("b_shi"), sem("b_shift_ready"))
            shift_ld = [sem("b_shift_ld0"), sem("b_shift_ld1")]
        else:
            kept, fin, worst_turned = sem("b_kept"), sem("b_fin"), sem("b_worst_turned")
        sc = [ps[:, 2 * k:2 * k + 2, :] for k in range(3)]
        ob = [ps[:, 6, :], ps[:, 7, :]]
        PAIRS = HEADS // 2
        LOADS = 6 if exact else 8
        block = ctx.enter_context(nc.Block())

        @block.sync
        def _(sp):
            def load(n, u):
                row = 0
                for s, times in Q_GROUPS:
                    src = m.scr[0][s, ds(n * C, C), :]
                    sp.dma_start(qs[u][row:row + times * C, :], bcast(src, 0, times) if times > 1 else src).then_inc(qk_ld[u], 16)
                    row += times * C
                row = 0
                for s, parts in K_RUNS:
                    sp.dma_start(ks[u][row:row + parts * C, :], m.scr[1][s:s + parts, ds(n * C, C), :]).then_inc(qk_ld[u], 16)
                    row += parts * C
                sp.dma_start(vst[:, u, :], m.v_dram[:, ds(n, 1), :].rearrange("p o c -> p (o c)")).then_inc(v_ld[u], 16)
                if not exact:
                    sp.dma_start(qs[u][SR:SR + 1, :], m.qn_dram[ds(n, 1), :]).then_inc(qk_ld[u], 16)
                    sp.dma_start(ks[u][SR:SR + 1, :], m.kmax_dram[ds(n, 1), :]).then_inc(qk_ld[u], 16)

            def put_shift(n, u):
                if exact:
                    wait_apart(sp, shift_ready, n + 1, mark)
                    for a in range(2):
                        sp.dma_start(qs[u][SR + a:SR + a + 1, :], shift[:, u, a, :]).then_inc(shift_ld[u], 16)

            def store(n, u):
                wait_apart(sp, hd_done, n + 1, mark)
                for j in range(4):
                    sp.dma_start(m.heads_dram[ds(n * C, C), j * 512:(j + 1) * 512],
                                 hout[32 * j + C:32 * (j + 1), u, :]).then_inc(hd_stored[u], 16)

            def turn(i, first):
                for u in range(2):
                    put_shift(2 * i + (u - 2), u)
                    wait_apart(sp, sc_done, i * STEPS + (u - 1) * 2 * KT, mark)
                    load(2 * i + u, u)
                    if not (first and u == 0):
                        store(2 * i + (u - 3), 1 - u)

            with when_needed(sp):
                if exact:
                    sp.wait_ge(setup, 3)
                for u in range(2):
                    load(u, u)
                turn(1, True)
                with sp.Fori(2, PAIRS) as i:
                    turn(i, False)
                put_shift(HEADS - 2, 0)
                store(HEADS - 3, 1)
                put_shift(HEADS - 1, 1)
                store(HEADS - 2, 0)
                store(HEADS - 1, 1)
                for u in range(2):
                    sp.wait_ge(hd_stored[u], 64 * (PAIRS + 1))

        @block.gpsimd
        def _(pool):
            def stage_v(i, u):
                wait_apart(pool, v_ld[u], i * 16 + 16, mark)
                nc.gpsimd.tensor_copy(vs[:, u, :, C:2 * C], vst[:, u, :].rearrange("p (t c) -> p t c", c=C)).then_inc(v_staged, 1)

            with when_needed(pool):
                nc.gpsimd.memset(vs[:, :, :, 0:C], 1.0).then_inc(setup, 1)
                for u in range(2):
                    stage_v(0, u)
                with pool.Fori(1, PAIRS) as i:
                    for u in range(2):
                        wait_apart(pool, pv_done, i * (2 * KT) + (u - 1) * KT + PS, mark)
                        stage_v(i, u)

        @block.vector
        def _(dve):
            def row_max(n, i, u):
                for qt in range(KT):
                    for kc in range(4):
                        dve.wait_ge(mx_done, n * (4 * KT) + qt * 4 + kc + 1)
                        nc.vector.reduce_max(part[:, qt, kc:kc + 1], ob[u], AX.X).then_inc(mx_red, 1)
                dve.wait_ge(mx_red, n * (4 * KT) + 4 * KT + 1)
                nc.vector.reduce_max(rowmax[:, :], part[:, :, :], AX.X).then_inc(row_ready, 1)
                dve.wait_ge(rowT, n + 1)
                dve.wait_ge(shift_ld[u], i * 32 + 32)
                nc.vector.tensor_scalar(shift[:, u, 0, :], ob[u][0:KT, 0:P], -1.0, None, ALU.mult).then_inc(shi, 1)
                dve.wait_ge(shi, n + 1)
                nc.vector.scalar_tensor_tensor(out=shift[:, u, 1, :], in0=ob[u][0:KT, 0:P], scalar=-1.0,
                                               in1=shift[:, u, 0, :], op0=ALU.mult, op1=ALU.subtract).then_inc(shift_ready, 1)

            def finish(n, i, u):
                dve.wait_ge(pv_done, n * KT + KT + PS)
                nc.vector.tensor_copy(osb[:, :], ob[u]).then_inc(o_evac, 1)
                wait_apart(dve, o_evac, n + 3, mark)
                nc.vector.stream_shuffle(sums[:, :], osb[:, :], [k % C for k in range(32)]).then_inc(sums_ready, 1)
                dve.wait_ge(sums_ready, n + 1)
                nc.vector.reciprocal(rc[:, :], sums[:, :]).then_inc(rc_ready, 1)
                dve.wait_ge(rc_ready, n + 1)
                dve.wait_ge(hd_stored[u], i * 64 + 64)
                nc.vector.tensor_tensor(hout[:, u, :], osb[:, :], rc[:, :], ALU.mult).then_inc(hd_done, 1)
                if not exact:
                    nc.vector.reduce_max(rcmax[:, ds(n, 1)], rc[:, :], AX.X).then_inc(kept, 1)
                    dve.wait_ge(kept, n + 1)
                dve.wait_ge(hd_done, n + 1)

            def pair(i, last):
                for u in range(2):
                    n = 2 * i + u
                    if exact and not (last and u == 1):
                        row_max(n + 1, i + u, 1 - u)
                    finish(n, i, u)

            with when_needed(dve):
                for count, free in ((pv_done, PS), (o_evac, 2), (hd_stored[0], 64), (hd_stored[1], 64)):
                    dve.sem_inc(count, free)
                if exact:
                    for u in range(2):
                        nc.vector.memset(ks[u][SR:stack, :], 1.0).then_inc(setup, 1)
                    for count, free in ((mx_red, 1), (shift_ld[0], 32), (shift_ld[1], 32)):
                        dve.sem_inc(count, free)
                    row_max(0, 0, 0)
                with dve.Fori(0, PAIRS - 1) as i:
                    pair(i, False)
                pair(PAIRS - 1, True)
                dve.wait_ge(hd_done, HEADS)
            if not exact:
                dve.wait_ge(kept, HEADS)
                nc.vector.reduce_max(worst[:, :], rcmax[:, :], AX.X).then_inc(fin, 1)
                dve.wait_ge(worst_turned, 1)
                nc.vector.reduce_max(verdict[:, 0:1], sc[0][0:1, 0, 0:P], AX.X).then_inc(fin, 1)
                dve.wait_ge(fin, 2)
                nc.vector.tensor_scalar(verdict[:, 1:2], verdict[:, 0:1], 1.0 / LEAST_SUM, None, ALU.is_le).then_inc(fin, 1)
                dve.wait_ge(fin, 3)
                nc.vector.tensor_scalar(m.flag[:, :], verdict[:, 1:2], -1.0, 1.0, ALU.mult, ALU.add).then_inc(fin, 1)
                dve.wait_ge(fin, 4)

        @block.scalar
        def _(act):
            with when_needed(act):
                with act.Fori(0, PAIRS) as i:
                    for s in range(STEPS):
                        if s % 2 == 0:
                            act.wait_ge(pv_done, i * (2 * KT) + s // 2 + 1)
                        act.wait_ge(sc_done, i * STEPS + s + 1)
                        half = s % 2
                        nc.scalar.activation(probs[:, s // 2 % PS, half * (L // 2):(half + 1) * (L // 2)], sc[slot[s]],
                                             ACT.Exp, scale=SCALE).then_inc(exp_done, 1)

        @block.tensor
        def _(pe):
            def max_scores(n, i, u):
                pe.wait_ge(qk_ld[u], i * (16 * LOADS) + 16 * LOADS)
                pe.wait_ge(o_evac, n + 1)
                for qt in range(KT):
                    for kc in range(4):
                        pe.wait_ge(mx_red, n * (4 * KT) + qt * 4 + kc + 1)
                        nc.tensor.matmul(ob[u], qs[u][0:SR, qt * P:(qt + 1) * P], ks[u][0:SR, kc * 512:(kc + 1) * 512],
                                         start=True, stop=True).then_inc(mx_done, 1)
                pe.wait_ge(row_ready, n + 1)
                nc.tensor.transpose(ob[u][0:KT, 0:P], rowmax[:, :], m.ident[:, :]).then_inc(rowT, 1)
                pe.wait_ge(shift_ld[u], i * 32 + 64)
                pe.wait_ge(shift_ready, n + 1)

            def scores(i, s, first):
                i, s, first = (i, s, first) if s < STEPS else (i + 1, s - STEPS, False)
                u, kt, half = s // (2 * KT), s // 2 % KT, s % 2
                if s % (2 * KT) == 0:
                    if exact:
                        max_scores(2 * i + u, i, u)
                    pe.wait_ge(qk_ld[u], i * (16 * LOADS) + 16 * LOADS)
                if not (first and s < 3):
                    pe.wait_ge(exp_done, i * STEPS + (s - back_to[s] + 1))
                for a in range(2):
                    q0 = (2 * half + a) * 512
                    last = nc.tensor.matmul(sc[slot[s]][:, a, :], ks[u][:, kt * P:(kt + 1) * P], qs[u][:, q0:q0 + 512],
                                            start=True, stop=True)
                last.then_inc(sc_done, 1)

            def values(i, u, kt):
                n = 2 * i + u
                if kt == 0:
                    pe.wait_ge(v_staged, n + 1)
                    pe.wait_ge(o_evac, n + 1)
                pe.wait_ge(exp_done, i * STEPS + (u * 2 * KT + 2 * kt + 2))
                for j in range(4):
                    last = nc.tensor.matmul(ob[u][32 * j:32 * (j + 1), :], vs[:, u, kt, :], probs[:, kt % PS, j * 512:(j + 1) * 512],
                                            start=(kt == 0), stop=(kt == KT - 1))
                last.then_inc(pv_done, 1)

            def pair(i, first, last):
                for t in range(2 * KT):
                    for s in (2 * t + 3, 2 * t + 4):
                        if not (last and s >= STEPS):
                            scores(i, s, first)
                    values(i, t // KT, t % KT)

            with when_needed(pe):
                pe.wait_ge(setup, 3 if exact else 1)
                for s in range(3):
                    scores(0, s, True)
                pair(0, True, False)
                with pe.Fori(1, PAIRS - 1) as i:
                    pair(i, False, False)
                pair(PAIRS - 1, False, True)
            if not exact:
                pe.wait_ge(fin, 1)
                nc.tensor.transpose(sc[0][0:1, 0, 0:P], worst[:, :], m.ident[:, :]).then_inc(worst_turned, 1)


def dense_stage(nc, sb, sem, ps, m):
    with ExitStack() as ctx:
        hT = sb(ctx, "hT", [P, 2, DH, GN], F32)
        fT = sb(ctx, "fT", [P, DH, GN], F32)
        xb = sb(ctx, "xb", [P, GT, D], F32)
        t1 = sb(ctx, "t1", [P, GT, D], F32)
        xf = sb(ctx, "xf", [P, 2, GT, D], F32)
        st6 = sb(ctx, "st6c", [P, GT, 6], F32)
        mv = sb(ctx, "mvc", [P, 2, GT, 2], F32)
        veps = sb(ctx, "vepsc", [P, GT], F32)
        th = sb(ctx, "th", [P, DH, GN], F32)
        gT = sb(ctx, "gT", [P, DH, GN], F32)
        y = sb(ctx, "y", [P, 2, GT, D], F32)
        hT_ld0, hT_ld1, xb_ready, ln1_ready, t1_ready = sem("c_hT_ld0"), sem("c_hT_ld1"), sem("c_xb_ready"), sem("c_ln1_ready"), sem("c_t1_ready")
        pj_done, x1_ready = sem("c_pj_done"), sem("c_x1_ready")
        bn, aggr, veps_ready, rstd_ready, xf_ready = (sem("c_bn"), sem("c_aggr"), sem("c_veps_ready"), sem("c_rstd_ready"),
                                                      sem("c_xf_ready"))
        ftr_done, fT_ready, lg_done, lg_evac = sem("c_ftr_done"), sem("c_fT_ready"), sem("c_lg_done"), sem("c_lg_evac")
        ab_done, th_ready, sg_ready, g_ready = sem("c_ab_done"), sem("c_th_ready"), sem("c_sg_ready"), sem("c_g_ready")
        so_done, y_ready, stored = sem("c_so_done"), sem("c_y_ready"), sem("c_stored")
        hT_ld = [hT_ld0, hT_ld1]
        half_ready, kept, mark = sem("c_half_ready"), sem("c_kept"), sem("c_mark")
        tr = ps[:, 0:2, :]
        pj = ps[:, 2:4, :].rearrange("p a (t d) -> p (a t) d", t=2)
        so = ps[:, 4:6, :].rearrange("p a (t d) -> p (a t) d", t=2)
        lg = ps[:, 4, 0:GT * NE].rearrange("p (t e) -> p t e", e=NE)
        ab = [ps[:, 6:8, :], ps[:, 0:2, :]]
        block = ctx.enter_context(nc.Block())

        def pipeline(eng, join, feed):
            join(0, 0)
            with eng.Fori(0, GROUPS // 2 - 1) as i:
                for u in range(2):
                    join(2 * i + (u + 1), 1 - u)
                    feed(2 * i + u, u)
            g = GROUPS - 2
            join(g + 1, 1)
            feed(g, 0)
            feed(g + 1, 1)

        @block.sync
        def _(sp):
            sp.sem_inc(stored, 32)

            def load_heads(b, c):
                sp.dma_start(hT[:, c % 2, :, :], m.heads_dram[ds(b * D, D), c * GN:(c + 1) * GN]
                             .rearrange("(k p) n -> p k n", p=P)).then_inc(hT_ld[c % 2], 16)

            def store_out(g, u):
                wait_apart(sp, y_ready, g + 2, mark)
                sp.dma_start(m.og[ds(g, 1)].rearrange("o p t d -> p (o t) d"), y[:, u, :, :]).then_inc(stored, 16)
                wait_apart(sp, stored, g * 16 + 48, mark)

            def batch(b, last):
                for c in range(GPB):
                    if not (last and c >= GPB - 2):
                        wait_apart(sp, pj_done, b * GPB + (c + 2), mark)
                        load_heads(b + (c + 2) // GPB, (c + 2) % GPB)
                    store_out(b * GPB + c, c % 2)

            load_heads(0, 0)
            load_heads(0, 1)
            with sp.Fori(0, B - 1) as b:
                batch(b, False)
            batch(B - 1, True)

        @block.gpsimd
        def _(pool):
            for count, free in ((pj_done, 1), (x1_ready, 1), (ftr_done, 2), (fT_ready, 1),
                                (lg_evac, 1), (g_ready, 2), (so_done, 1), (y_ready, 1)):
                pool.sem_inc(count, free)
            with pool.Fori(0, B) as b:
                for c in range(GPB):
                    g = b * GPB + c
                    pool.wait_ge(x1_ready, g + 1)
                    nc.gpsimd.tensor_tensor(xb[:, :, :], m.x[:, ds(g * GT, GT), :], bcast(m.bo[:, :], 1, GT), ALU.add).then_inc(xb_ready, 1)
                    wait_apart(pool, aggr, g + 1, mark)
                    nc.gpsimd.tensor_scalar(veps[:, :], mv[:, c % 2, :, 1], EPS, None, ALU.add).then_inc(veps_ready, 1)
                    pool.wait_ge(veps_ready, g + 1)
                    nc.gpsimd.tensor_tensor(m.rstd2[:, ds(g * GT, GT)], veps[:, :], m.mhalf[:, 0:GT], ALU.pow).then_inc(rstd_ready, 1)

        @block.scalar
        def _(act):
            def feed(g, u):
                act.wait_ge(ftr_done, g + 3)
                nc.scalar.copy(fT[:, 0, :], tr[:, 0, :])
                nc.scalar.copy(fT[:, 1, :], tr[:, 1, :]).then_inc(fT_ready, 1)
                for k in range(DH):
                    act.wait_ge(ab_done, g * DH + k + 1)
                    if k == 0:
                        act.wait_ge(g_ready, g + 2)
                    nc.scalar.activation(th[:, k, :], ab[k][:, 0, :], ACT.Tanh, scale=0.5).then_inc(th_ready, 1)
                act.wait_ge(lg_done, g + 1)
                nc.scalar.copy(m.logits[:, ds(g * GT, GT), :], lg).then_inc(lg_evac, 1)

            with act.Fori(0, GROUPS) as g:
                feed(g, None)

        @block.vector
        def _(dve):
            nc.vector.tensor_scalar(m.sw2h[:, :, :], m.sw2[:, :, :], 0.5, None, ALU.mult).then_inc(half_ready, 1)

            def join(g, u):
                for t in range(GT):
                    last = nc.vector.tensor_scalar(t1[:, t, :], flat(m.x[:, ds(g * GT + t, 1), :]),
                                                   m.stat1[:, ds(g * GT + t, 1), 0], m.rstd1[:, ds(g * GT + t, 1)], ALU.subtract, ALU.mult)
                last.then_inc(ln1_ready, 1)
                dve.wait_ge(ln1_ready, g + 1)
                dve.wait_ge(xb_ready, g + 1)
                nc.vector.tensor_tensor(t1[:, :, :], t1[:, :, :], xb[:, :, :], ALU.add).then_inc(t1_ready, 1)
                dve.wait_ge(t1_ready, g + 1)
                dve.wait_ge(pj_done, g + 2)
                nc.vector.tensor_tensor(m.x[:, ds(g * GT, GT), :], t1[:, :, :], pj, ALU.add).then_inc(x1_ready, 1)
                wait_apart(dve, x1_ready, g + 2, mark)
                for t in range(GT):
                    last = nc.vector.bn_stats(st6[:, t, :], flat(m.x[:, ds(g * GT + t, 1), :]))
                last.then_inc(bn, 1)
                wait_apart(dve, bn, g + 1, mark)
                for t in range(GT):
                    last = nc.vector.bn_aggr(mv[:, u, t, :], st6[:, t, :])
                last.then_inc(aggr, 1)
                dve.wait_ge(aggr, g + 1)
                nc.vector.tensor_copy(m.stat2[:, ds(g * GT, GT), :], mv[:, u, :, :]).then_inc(kept, 1)
                dve.wait_ge(rstd_ready, g + 1)
                dve.wait_ge(ftr_done, g + 1)
                for t in range(GT):
                    last = nc.vector.tensor_scalar(xf[:, u, t, :], flat(m.x[:, ds(g * GT + t, 1), :]),
                                                   mv[:, u, t, 0:1], m.rstd2[:, ds(g * GT + t, 1)], ALU.subtract, ALU.mult)
                last.then_inc(xf_ready, 1)

            def feed(g, u):
                for k in range(DH):
                    dve.wait_ge(th_ready, g * DH + k + 1)
                    nc.vector.scalar_tensor_tensor(out=th[:, k, :], in0=th[:, k, :], scalar=1.0, in1=ab[k][:, 0, :],
                                                   op0=ALU.add, op1=ALU.mult).then_inc(sg_ready, 1)
                    dve.wait_ge(sg_ready, g * DH + k + 1)
                    if k == 0:
                        dve.wait_ge(so_done, g + 1)
                    last = nc.vector.tensor_tensor(gT[:, k, :], th[:, k, :], ab[k][:, 1, :], ALU.mult)
                last.then_inc(g_ready, 1)
                dve.wait_ge(so_done, g + 2)
                dve.wait_ge(stored, g * 16 + 16)
                nc.vector.tensor_tensor(y[:, u, :, :], m.x[:, ds(g * GT, GT), :], so, ALU.add).then_inc(y_ready, 1)

            pipeline(dve, join, feed)

        @block.tensor
        def _(pe):
            pe.wait_ge(half_ready, 1)

            def join(g, u):
                pe.wait_ge(hT_ld[u], (g - u) * 8 + 16)
                pe.wait_ge(x1_ready, g + 1)
                for t in range(GT):
                    for k in range(DH):
                        last = nc.tensor.matmul(pj[:, t, :], hT[:, u, k, t * P:(t + 1) * P], m.wo[:, k, :], start=(k == 0), stop=(k == DH - 1))
                last.then_inc(pj_done, 1)

            def feed(g, u):
                pe.wait_ge(xf_ready, g + 1)
                pe.wait_ge(g_ready, g + 2)
                for t in range(GT):
                    for k in range(DH):
                        last = nc.tensor.transpose(tr[:, k, t * P:(t + 1) * P], xf[:, u, t, k * P:(k + 1) * P], m.ident[:, :])
                last.then_inc(ftr_done, 1)
                pe.wait_ge(fT_ready, g + 2)
                for h in range(DH):
                    for o, w in ((0, m.sw1), (1, m.sw3)):
                        for k in range(DH):
                            last = nc.tensor.matmul(ab[h][:, o, :], w[:, k, h * P:(h + 1) * P], fT[:, k, :], start=(k == 0), stop=(k == DH - 1))
                    last.then_inc(ab_done, 1)
                pe.wait_ge(y_ready, g + 1)
                for t in range(GT):
                    for k in range(DH):
                        last = nc.tensor.matmul(lg[:, t, :], fT[:, k, t * P:(t + 1) * P], m.wg[:, k, :], start=(k == 0), stop=(k == DH - 1))
                last.then_inc(lg_done, 1)
                pe.wait_ge(lg_evac, g + 2)
                pe.wait_ge(g_ready, g + 3)
                for t in range(GT):
                    for k in range(DH):
                        last = nc.tensor.matmul(so[:, t, :], gT[:, k, t * P:(t + 1) * P], m.sw2h[:, k, :], start=(k == 0), stop=(k == DH - 1))
                last.then_inc(so_done, 1)

            pipeline(pe, join, feed)


def routed_stage(nc, sb, sem, ps, m):
    RT = 2 * TILES
    JE = NE * NE
    QT = 2
    STEPS = TILES // QT
    BIG = 3.0e38
    with ExitStack() as ctx:
        w1 = sb(ctx, "w1", [P, DH, NE, HID], F32)
        w3 = sb(ctx, "w3", [P, DH, NE, HID], F32)
        w2 = sb(ctx, "w2", [P, NE, D], F32)
        big = sb(ctx, "big", [P, TILES * D], F32)
        ohw = big[:, 0:RT * JE].rearrange("p (r j e) -> p r j e", j=NE, e=NE)
        ohb = big[:, RT * JE:RT * JE * 3 // 2].bitcast(BF16).rearrange("p (r j e) -> p r j e", j=NE, e=NE)
        rest = RT * JE * 3 // 2
        s8 = [big[:, rest + i * TILES * NE:rest + (i + 1) * TILES * NE].rearrange("p (t e) -> p t e", e=NE) for i in range(5)]
        one = [sb(ctx, f"one{i}", [P, TILES], F32) for i in range(3)]
        s4 = [sb(ctx, f"s4_{i}", [P, TILES, NG], F32) for i in range(5)]
        rest += 5 * TILES * NE
        ohk = big[:, rest:rest + RT * NE].rearrange("p (t k e) -> p t k e", k=2, e=NE)
        ohkw = sb(ctx, "ohkw", [P, TILES, 2, NE], F32)
        wk = sb(ctx, "wk", [P, TILES, 2], F32)
        reached = sb(ctx, "reached", [P, RT, NE + 1], F32)
        span = sb(ctx, "span", [P, RT, NE], F32)
        cnt = sb(ctx, "cnt", [P, NE], F32)
        csum = sb(ctx, "csum", [P, NE, NE], F32)
        offs = sb(ctx, "offs", [P, NE], F32)
        x0 = sb(ctx, "x0", [NE, D], F32)
        x0T = sb(ctx, "x0T", [P, DH, NE], F32)
        arow = sb(ctx, "arow", [NE, NE * HID], F32)
        a2 = sb(ctx, "a2", [P, HID], F32)
        arest = sb(ctx, "arest", [P, HID], F32)
        ad = sb(ctx, "ad", [P, 3, 2 * HID], BF16)
        bT = sb(ctx, "bT", [HID, NE, NE], F32)
        hT = sb(ctx, "hTd", [HID, NE, NE], F32)
        ohT = sb(ctx, "ohT", [P, 2, QT, P], BF16)
        z, th, sil = (m.x[:, (i + 1) * 4:(i + 2) * 4, :].rearrange("p t d -> p (t d)").rearrange("p (u r h) -> p u r h", u=2, h=HID)
                      for i in range(3))
        rows = sb(ctx, "rows", [NE, D], F32)
        final = sb(ctx, "final", [NE, D], F32)
        w_ld, rows_ld, a_ld, out_st = sem("d_w_ld"), sem("d_rows_ld"), sem("d_a_ld"), sem("d_out_st")
        step, shifted, exped = sem("d_step"), sem("d_shifted"), sem("d_exped")
        cnt_ready, cnt_sum, x0_ready, x0_tr, x0T_ready, tabs_done, arow_ready, tabs_ready = (
            sem("d_cnt_ready"), sem("d_cnt_sum"), sem("d_x0_ready"), sem("d_x0_tr"), sem("d_x0T_ready"), sem("d_tabs_done"),
            sem("d_arow_ready"), sem("d_tabs_ready"))
        ohb_ready, ohw_ready = sem("d_ohb_ready"), sem("d_ohw_ready")
        oh_tr, ohT_ready, a_done, z_ready, th_ready, sil_ready, sum_done = (
            sem("d_oh_tr"), sem("d_ohT_ready"), sem("d_a_done"), sem("d_z_ready"), sem("d_th_ready"), sem("d_sil_ready"), sem("d_sum_done"))
        g_done, h_ready, o_done, final_ready = sem("d_g_done"), sem("d_h_ready"), sem("d_o_done"), sem("d_final_ready")
        ab = ps[0:NE, 0:2, :]
        bTb = ps[:, 2, 0:JE].rearrange("p (e j) -> p e j", j=NE)
        x0b = ps[:, 3, 0:DH * NE].rearrange("p (k j) -> p k j", j=NE)
        cb = ps[:, 4, 0:NE]
        gb = ps[:, 5, 0:JE].rearrange("p (j e) -> p j e", e=NE)
        ab2 = [ps[:, 0, :], ps[:, 1, :]]
        trb = [ps[:, 6, :].bitcast(BF16), ps[:, 7, :].bitcast(BF16)]
        ob = ps[0:NE, 2, 0:D]
        block = ctx.enter_context(nc.Block())

        @block.sync
        def _(sp):
            for dst, src in ((w1, m.w1_dram), (w3, m.w3_dram)):
                for k in range(DH):
                    sp.dma_start(dst[:, k, :, :], src[:, k * P:(k + 1) * P, :].rearrange("e p h -> p e h")).then_inc(w_ld, 16)
            sp.dma_start(w2[:, :, :], m.w2_dram.rearrange("e p d -> p e d")).then_inc(w_ld, 16)
            sp.dma_start(rows[:, :], m.out_rows).then_inc(rows_ld, 16)
            sp.wait_ge(arow_ready, 1)
            for u in range(2):
                sp.dma_start(a2[u * JE:(u + 1) * JE, :], arow[:, :].rearrange("j (e h) -> j e h", h=HID)).then_inc(a_ld, 16)
            sp.wait_ge(final_ready, 1)
            sp.dma_start(m.out_rows, final[:, :]).then_inc(out_st, 16)
            sp.wait_ge(out_st, 16)

        @block.gpsimd
        def _(pool):
            nc.gpsimd.memset(ad[:, :, :], 0.0).then_inc(tabs_ready, 1)
            pool.wait_ge(ohw_ready, 1)
            quarter = RT // 4
            for i in range(4):
                s = slice(i * quarter, (i + 1) * quarter)
                nc.gpsimd.tensor_tensor(ohw[:, s, :, :], bcast(ohkw[:, :, :, :].rearrange("p t k e -> p (t k) e")[:, s, :], 3, NE),
                                        bcast(span[:, s, :], 2, NE), ALU.mult).then_inc(ohw_ready, 1)

        @block.scalar
        def _(act):
            act.wait_ge(shifted, 1)
            nc.scalar.activation(s8[0][:, :, :], s8[0][:, :, :], ACT.Exp).then_inc(exped, 1)
            with act.Fori(0, STEPS // 2) as i:
                for u in range(2):
                    q = 2 * i + u
                    act.wait_ge(oh_tr, q + 1)
                    act.wait_ge(a_done, q + 1)
                    nc.scalar.copy(ohT[:, u, :, :].rearrange("p t n -> p (t n)"), trb[u][:, 0:QT * P]).then_inc(ohT_ready, 1)
                    act.wait_ge(z_ready, q + 1)
                    act.wait_ge(sil_ready, q + 1)
                    nc.scalar.activation(th[:, u, :, :], z[:, u, :, :], ACT.Tanh, scale=0.5).then_inc(th_ready, 1)

        @block.vector
        def _(dve):
            for count, free in ((a_done, 2), (sil_ready, 2), (sum_done, 2), (z_ready, 0), (ohT_ready, 2)):
                if free:
                    dve.sem_inc(count, free)
            steps = [0]

            def link(ins):
                steps[0] += 1
                ins.then_inc(step, 1)
                dve.wait_ge(step, steps[0])

            V = nc.vector
            V.tensor_scalar(x0[:, :], m.x[0:NE, 0, :], m.stat2[0:NE, 0, 0:1], m.rstd2[0:NE, 0:1], ALU.subtract, ALU.mult).then_inc(x0_ready, 1)
            lg = m.logits[:, :, :]
            link(V.reduce_max(one[0][:, :], lg, AX.X))
            V.tensor_tensor(s8[0][:, :, :], lg, bcast(one[0][:, :], 2, NE), ALU.subtract).then_inc(shifted, 1)
            dve.wait_ge(x0_tr, 1)
            V.tensor_copy(x0T[:, :, :], x0b).then_inc(x0T_ready, 1)
            dve.wait_ge(exped, 1)
            link(V.reduce_sum(one[1][:, :], s8[0][:, :, :], AX.X))
            link(V.reciprocal(one[1][:, :], one[1][:, :]))
            scores = s8[1]
            link(V.tensor_tensor(scores[:, :, :], s8[0][:, :, :], bcast(one[1][:, :], 2, NE), ALU.mult))
            biased = s8[2]
            link(V.tensor_tensor(biased[:, :, :], scores[:, :, :], bcast(m.ebias[:, :], 1, TILES), ALU.add))

            def first_max(vals, n, tmp, pick):
                link(V.reduce_max(one[2][:, :], vals, AX.X))
                link(V.tensor_tensor(tmp, vals, bcast(one[2][:, :], 2, n), ALU.is_equal))
                link(V.scalar_tensor_tensor(out=tmp, in0=tmp, scalar=-float(n), in1=bcast(m.iota[:, 0:n], 1, TILES), op0=ALU.mult, op1=ALU.add))
                link(V.tensor_reduce(one[2][:, :], tmp, AX.X, ALU.min))
                link(V.tensor_scalar(one[2][:, :], one[2][:, :], float(n), None, ALU.add))
                link(V.tensor_tensor(pick, bcast(m.iota[:, 0:n], 1, TILES), bcast(one[2][:, :], 2, n), ALU.is_equal))

            pairs = biased[:, :, :].rearrange("p t (g o) -> p t g o", o=2)
            link(V.tensor_tensor(s4[0][:, :, :], pairs[:, :, :, 0], pairs[:, :, :, 1], ALU.add))
            first_max(s4[0][:, :, :], NG, s4[1][:, :, :], s4[2][:, :, :])
            link(V.scalar_tensor_tensor(out=s4[0][:, :, :], in0=s4[2][:, :, :], scalar=-BIG, in1=s4[0][:, :, :], op0=ALU.mult, op1=ALU.add))
            first_max(s4[0][:, :, :], NG, s4[1][:, :, :], s4[3][:, :, :])
            link(V.tensor_tensor(s4[2][:, :, :], s4[2][:, :, :], s4[3][:, :, :], ALU.add))
            link(V.tensor_scalar(s4[4][:, :, :], s4[2][:, :, :], BIG, -BIG, ALU.mult, ALU.add))
            masked = s8[3]
            mpair = masked[:, :, :].rearrange("p t (g o) -> p t g o", o=2)
            link(V.tensor_tensor(mpair, pairs, bcast(s4[2][:, :, :], 3, 2), ALU.mult))
            link(V.tensor_tensor(mpair, mpair, bcast(s4[4][:, :, :], 3, 2), ALU.add))
            first_max(masked[:, :, :], NE, s8[4][:, :, :], ohk[:, :, 0, :])
            link(V.scalar_tensor_tensor(out=masked[:, :, :], in0=ohk[:, :, 0, :], scalar=-BIG, in1=masked[:, :, :], op0=ALU.mult, op1=ALU.add))
            first_max(masked[:, :, :], NE, s8[4][:, :, :], ohk[:, :, 1, :])
            V.reduce_sum(cnt[:, :], ohk[:, :, :, :].rearrange("p t k e -> p e (t k)"), AX.X).then_inc(cnt_ready, 1)
            for k in range(2):
                link(V.tensor_tensor(s8[4][:, :, :], scores[:, :, :], ohk[:, :, k, :], ALU.mult))
                link(V.reduce_sum(wk[:, :, k], s8[4][:, :, :], AX.X))
                link(V.scalar_tensor_tensor(out=ohkw[:, :, k, :], in0=ohk[:, :, k, :], scalar=0.5, in1=bcast(wk[:, :, k], 2, NE),
                                            op0=ALU.mult, op1=ALU.mult))
            dve.wait_ge(cnt_sum, 1)
            link(V.tensor_tensor(csum[:, :, :], m.upto[:, :, :], bcast(cb, 1, NE), ALU.mult))
            link(V.reduce_sum(offs[:, :], csum[:, :, :], AX.X))
            link(V.memset(reached[:, :, 0:1], 1.0))
            link(V.tensor_tensor(reached[:, :, 1:NE + 1], bcast(m.rowno[:, :], 2, NE), bcast(offs[:, :], 1, RT), ALU.is_ge))
            V.tensor_tensor(span[:, :, :], reached[:, :, 0:NE], reached[:, :, 1:NE + 1], ALU.subtract).then_inc(ohw_ready, 1)
            dve.wait_ge(ohw_ready, 1)
            dve.wait_ge(tabs_done, 1)
            V.tensor_copy(arow[:, :], ab.rearrange("p a n -> p (a n)")).then_inc(arow_ready, 1)
            link(V.tensor_copy(bT[:, :, :], bTb))
            quarter = RT // 4
            for i in range(4):
                s = slice(i * quarter, (i + 1) * quarter)
                V.tensor_tensor(ohb[:, s, :, :], bcast(ohk[:, :, :, :].rearrange("p t k e -> p (t k) e")[:, s, :], 3, NE),
                                bcast(span[:, s, :], 2, NE), ALU.mult).then_inc(ohb_ready, 1)
                if i == 0:
                    dve.wait_ge(a_ld, 32)
                    dve.wait_ge(tabs_ready, 1)
                    for part in range(3):
                        src = a2 if part == 0 else arest
                        for u in range(2):
                            d = ad[u * JE:(u + 1) * JE, part, u * HID:(u + 1) * HID]
                            link(V.tensor_copy(d, src[u * JE:(u + 1) * JE, :]))
                            if part < 2:
                                link(V.tensor_tensor(arest[u * JE:(u + 1) * JE, :], src[u * JE:(u + 1) * JE, :], d, ALU.subtract))
                    V.memset(reached[:, 0:1, 0:1], 0.0).then_inc(tabs_ready, 1)

            with dve.Fori(0, STEPS // 2) as i:
                for u in range(2):
                    q = 2 * i + u
                    dve.wait_ge(a_done, q + 3)
                    V.tensor_tensor(z[:, u, :, :], ab2[u].rearrange("p (r h) -> p r h", h=HID),
                                    bcast(m.flatwk(wk, q), 2, HID), ALU.mult).then_inc(z_ready, 1)
                    dve.wait_ge(th_ready, q + 1)
                    dve.wait_ge(sum_done, q + 1)
                    V.scalar_tensor_tensor(out=sil[:, u, :, :], in0=th[:, u, :, :], scalar=1.0, in1=z[:, u, :, :],
                                           op0=ALU.add, op1=ALU.mult).then_inc(sil_ready, 1)
            dve.wait_ge(g_done, 1)
            V.tensor_tensor(hT[:, :, :], gb.rearrange("p j e -> p e j"), bT[:, :, :], ALU.mult).then_inc(h_ready, 1)
            dve.wait_ge(rows_ld, 16)
            dve.wait_ge(o_done, 1)
            V.tensor_tensor(final[:, :], rows[:, :], ob, ALU.add).then_inc(final_ready, 1)

        @block.tensor
        def _(pe):
            pe.wait_ge(x0_ready, 1)
            for k in range(DH):
                last = nc.tensor.transpose(x0b[:, k, :], x0[:, k * P:(k + 1) * P], m.ident[0:NE, 0:NE])
            last.then_inc(x0_tr, 1)
            pe.wait_ge(x0T_ready, 1)
            pe.wait_ge(w_ld, 16 * (2 * DH + 1))
            for a in range(2):
                for k in range(DH):
                    nc.tensor.matmul(ab[:, a, :], x0T[:, k, :], w1[:, k, 4 * a:4 * a + 4, :].rearrange("p e h -> p (e h)"),
                                     start=(k == 0), stop=(k == DH - 1))
            for e in range(NE):
                for k in range(DH):
                    last = nc.tensor.matmul(bTb[:, e, :], w3[:, k, e, :], x0T[:, k, :], start=(k == 0), stop=(k == DH - 1))
            last.then_inc(tabs_done, 1)
            pe.wait_ge(cnt_ready, 1)
            nc.tensor.matmul(cb, m.ones[:, :], cnt[:, :], start=True, stop=True).then_inc(cnt_sum, 1)
            pe.wait_ge(tabs_ready, 2)
            pe.wait_ge(arow_ready, 1)
            pe.wait_ge(ohb_ready, 4)
            pe.wait_ge(ohw_ready, 5)
            gflat = gb.rearrange("p j e -> p (j e)")
            nc.tensor.matmul(gflat, m.zeros[:, :], m.ones[:, 0:JE], start=True, stop=False)

            def gather(q, u):
                pe.wait_ge(ohT_ready, q + 1)
                for t in range(QT):
                    last = nc.tensor.transpose(trb[u][:, t * P:(t + 1) * P], m.rowtile(ohb, q * QT + t), m.identb[:, :])
                last.then_inc(oh_tr, 1)
                pe.wait_ge(ohT_ready, q + 3)
                pe.wait_ge(z_ready, q - 1) if False else None
                for t in range(QT):
                    for part in range(3):
                        last = nc.tensor.matmul(ab2[u][:, t * 2 * HID:(t + 1) * 2 * HID], ohT[:, u, t, :], ad[:, part, :],
                                                start=(part == 0), stop=(part == 2))
                last.then_inc(a_done, 1)

            def add_up(q, u):
                pe.wait_ge(sil_ready, q + 3)
                for t in range(QT):
                    for k in range(2):
                        last = nc.tensor.matmul(gflat, sil[:, u, 2 * t + k, :], m.rowhalf(ohw, q * (2 * QT) + (2 * t + k)), start=False, stop=False)
                last.then_inc(sum_done, 1)

            gather(0, 0)
            gather(1, 1)
            with pe.Fori(0, STEPS // 2 - 1) as i:
                for u in range(2):
                    add_up(2 * i + u, u)
                    gather(2 * i + (u + 2), u)
            for u in range(2):
                add_up(STEPS - 2 + u, u)
            nc.tensor.matmul(gflat, m.zeros[:, :], m.ones[:, 0:JE], start=False, stop=True).then_inc(g_done, 1)
            pe.wait_ge(h_ready, 1)
            for e in range(NE):
                last = nc.tensor.matmul(ob, hT[:, e, :], w2[:, e, :], start=(e == 0), stop=(e == NE - 1))
            last.then_inc(o_done, 1)


class Memory:
    pass


def preln_attention_moe(nc, x, w_qkvT, b_qk, b_v, w_oT, b_o, w_gateT, w1, w2, w3, sw1T, sw2T, sw3T, expert_bias,
                        ident, headsum, iota, upto, rowno, out):
    m = Memory()
    with ExitStack() as outer:
        def sb(ctx, name, shape, dt):
            return ctx.enter_context(nc.sbuf_tensor(name, shape, dt))

        def sem(name):
            return outer.enter_context(nc.semaphore(name))

        outer_sb = lambda name, shape, dt: sb(outer, name, shape, dt)
        ps = outer.enter_context(nc.psum_tensor("ps", [P, 8, 512], F32))
        m.x = outer_sb("x_sb", [P, TILES, D], F32)
        m.stat1 = outer_sb("stat1", [P, TILES, 2], F32)
        m.rstd1 = outer_sb("rstd1", [P, TILES], F32)
        m.stat2 = outer_sb("stat2", [P, TILES, 2], F32)
        m.rstd2 = outer_sb("rstd2", [P, TILES], F32)
        m.logits = outer_sb("logits", [P, TILES, NE], F32)
        m.wqkv = outer_sb("wqkv", [P, DH, 3 * D], F32)
        m.wo = outer_sb("wo", [P, DH, D], F32)
        m.sw1 = outer_sb("sw1", [P, DH, D], F32)
        m.sw2 = outer_sb("sw2", [P, DH, D], F32)
        m.sw2h = m.wqkv[:, :, 0:D]
        m.sw3 = outer_sb("sw3", [P, DH, D], F32)
        m.wg = outer_sb("wg", [P, DH, NE], F32)
        m.bqk = outer_sb("bqk", [P, 4], F32)
        m.bv = outer_sb("bv", [P, D], F32)
        m.bo = outer_sb("bo", [P, D], F32)
        m.ebias = outer_sb("ebias", [P, NE], F32)
        m.ident = outer_sb("ident", [P, P], F32)
        m.identb = outer_sb("identb", [P, P], BF16)
        headsum_f = outer_sb("headsum_f", [P, HPH], F32)
        m.headsum = outer_sb("headsum", [P, HPH], BF16)
        m.ones = outer_sb("ones", [P, P], F32)
        m.zeros = outer_sb("zeros", [P, P], F32)
        m.mhalf = outer_sb("mhalf", [P, GT], F32)
        m.iota = outer_sb("iota", [P, NE], F32)
        m.upto = outer_sb("upto", [P, NE, NE], F32)
        m.rowno = outer_sb("rowno", [P, 2 * TILES], F32)
        m.flag = outer_sb("flag", [1, 1], I32)
        m.scr = [nc.dram_tensor(f"{n}_parts", [3, B * D, L], BF16, kind="Internal").ap() for n in ("q", "k")]
        m.qn_dram = nc.dram_tensor("q_norms", [B * H, L], BF16, kind="Internal").ap()
        m.kmax_dram = nc.dram_tensor("k_largest", [B * H, L], BF16, kind="Internal").ap()
        m.v_dram = nc.dram_tensor("v", [P, B * H, KT * C], F32, kind="Internal").ap()
        m.heads_dram = nc.dram_tensor("heads", [B * D, L], F32, kind="Internal").ap()
        flat_x = x.rearrange("b l d -> (b l) d")
        flat_out = out.rearrange("b l d -> (b l) d")
        m.xg = flat_x.rearrange("(g t p) d -> g p t d", t=GT, p=P)
        m.og = flat_out.rearrange("(g t p) d -> g p t d", t=GT, p=P)
        m.out_rows = flat_out[0:NE, :]
        m.w1_dram, m.w2_dram, m.w3_dram = w1, w2, w3
        halves = lambda w: w.rearrange("(k p) n -> p k n", p=P)
        m.loads = [
            (m.ident[:, :], ident), (headsum_f[:, :], headsum), (m.wqkv[:, :, :], halves(w_qkvT)),
            (m.bqk[:, :], b_qk), (m.bv[:, :], b_v.partition_broadcast(P)),
            (m.bo[:, :], b_o.partition_broadcast(P)), (m.wo[:, :, :], halves(w_oT)), (m.wg[:, :, :], halves(w_gateT)),
            (m.sw1[:, :, :], halves(sw1T)), (m.sw2[:, :, :], halves(sw2T)), (m.sw3[:, :, :], halves(sw3T)),
            (m.ebias[:, :], expert_bias.partition_broadcast(P)), (m.iota[:, :], iota.partition_broadcast(P)),
            (m.upto[:, :, :], upto.partition_broadcast(P)), (m.rowno[:, :], rowno),
        ]
        m.flatwk = lambda wk, q: wk[:, :, :].rearrange("p t k -> p (t k)")[:, ds(q * 4, 4)]
        m.rowtile = lambda ohb, t: ohb.rearrange("p r j e -> p (r j e)")[:, ds(t * P, P)]
        m.rowhalf = lambda ohw, r: ohw.rearrange("p r j e -> p (r j e)")[:, ds(r * NE * NE, NE * NE)]

        w_ld, fill = sem("w_ld"), sem("fill")
        with nc.Block() as block:
            @block.sync
            def _(sp):
                for dst, src in m.loads:
                    sp.dma_start(dst, src).then_inc(w_ld, 16)

            @block.vector
            def _(dve):
                nc.vector.memset(m.ones[:, :], 1.0)
                nc.vector.memset(m.zeros[:, :], 0.0)
                nc.vector.memset(m.mhalf[:, :], -0.5)
                dve.wait_ge(w_ld, 16 * len(m.loads))
                nc.vector.tensor_copy(m.headsum[:, :], headsum_f[:, :])
                nc.vector.tensor_copy(m.identb[:, :], m.ident[:, :]).then_inc(fill, 1)
                dve.wait_ge(fill, 1)

        qkv_stage(nc, sb, sem, ps, m)
        attention_stage(nc, sb, sem, ps, m, exact=False)
        attention_stage(nc, sb, sem, ps, m, exact=True)
        dense_stage(nc, sb, sem, ps, m)
        routed_stage(nc, sb, sem, ps, m)


def kernel(**inputs):
    import numpy as np
    import concourse.bacc as bacc
    from concourse.bass_utils import run_bass_kernel_spmd

    whole = {k: np.asarray(v) for k, v in inputs.items()}
    plain = lambda name: np.ascontiguousarray(whole[name])
    turned = lambda name: np.ascontiguousarray(whole[name].T)
    row = np.arange(P)[:, None] * 2 + np.arange(TILES * 2)[None, :] // 2 * (2 * P) + np.arange(TILES * 2)[None, :] % 2
    arrays = {
        "x": plain("L0_attn_x"), "w_qkvT": turned("L0_attn_w_qkv"), 
        "b_qk": np.ascontiguousarray(whole["L0_attn_b_qkv"][:2 * D].reshape(4, P).T), "b_v": whole["L0_attn_b_qkv"][2 * D:],
        "w_oT": turned("L0_attn_w_o"), "b_o": plain("L0_attn_b_o"), "w_gateT": turned("L0_ffn_w_gate"),
        "w1": plain("L0_ffn_w1"), "w2": plain("L0_ffn_w2"), "w3": plain("L0_ffn_w3"),
        "sw1T": turned("L0_ffn_sw1"), "sw2T": turned("L0_ffn_sw2"), "sw3T": turned("L0_ffn_sw3"),
        "expert_bias": plain("L0_ffn_expert_bias"),
        "ident": np.eye(P, dtype=np.float32),
        "headsum": np.repeat(np.eye(HPH, dtype=np.float32), C, axis=0),
        "iota": np.arange(NE, dtype=np.float32),
        "upto": np.tril(np.ones((NE, NE), dtype=np.float32)),
        "rowno": row.astype(np.float32),
    }
    nc = bacc.Bacc("TRN2", target_bir_lowering=False, num_devices=1)
    args = [nc.dram_tensor(f"in_{n}", list(a.shape), mybir.dt.from_np(a.dtype), kind="ExternalInput").ap() for n, a in arrays.items()]
    out = nc.dram_tensor("out", [B, L, D], F32, kind="ExternalOutput").ap()
    preln_attention_moe(nc, *args, out)
    r = run_bass_kernel_spmd(nc, [{f"in_{n}": a for n, a in arrays.items()}], core_ids=[0])
    return r.results[0]["out"]
```

```python
from contextlib import ExitStack, nullcontext

import concourse.bass as bass
from concourse import mybir

F32, BF16, I32 = mybir.dt.float32, mybir.dt.bfloat16, mybir.dt.int32
ALU, ACT, AX = mybir.AluOpType, mybir.ActivationFunctionType, mybir.AxisListType
ds = bass.ds

B, L, D, H = 4, 2048, 256, 16
C = D // H
P = 128
TOK = B * L
TILES = TOK // P
GT = 4
GN = GT * P
GROUPS = TOK // GN
GPB = L // GN
DH = D // P
KT = L // P
HEADS = B * H
HPH = P // C
HID, NE, NG = 128, 8, 4
SCALE = 1.0 / D ** 0.5
EPS = 1e-5

Q_GROUPS = ((0, 3), (1, 2), (2, 1))
K_RUNS = ((0, 3), (0, 2), (0, 1))
SR = 6 * C
LEAST_SUM = 1e-26
NORM_UP = 1.02
NORM_LEAST = 1e-30


def bcast(ap, pos, n):
    ap = ap.unsqueeze(pos)
    shape = list(ap.shape)
    shape[pos] = n
    return ap.broadcast_to(shape)


def wait_apart(eng, count, value, mark):
    eng.wait_ge(count, value)
    eng.sem_inc(mark, 1)


def flat(ap):
    return ap.rearrange("p a d -> p (a d)")


NPB = H * P // HEADS


def by_partition(rows):
    return rows.rearrange("n (a l) -> (n a) l", a=P // HEADS)


def turn_norms(nc, sp, m, nmax, b0, b1):
    for b in range(b0, b1):
        for j in range(2):
            sp.dma_start(m.k2_dram[b * H + j * HPH:b * H + (j + 1) * HPH, :], nmax[:, j, b * GPB:(b + 1) * GPB]).then_inc(m.k2_stored, 16)
    sp.dma_start(m.q2_all[b0 * NPB:b1 * NPB, :], by_partition(m.q2_dram)[b0 * NPB:b1 * NPB, :]).then_inc(m.n_ld, 16)
    sp.wait_ge(m.k2_stored, 2 * 16 * b1)
    sp.dma_start(m.k2_all[b0 * NPB:b1 * NPB, :], bcast(m.k2_dram[b0 * H:b1 * H, :], 1, P // HEADS)).then_inc(m.n_ld, 16)


def largest_norms(nc, dve, m, b0, b1):
    parts = slice(b0 * NPB, b1 * NPB)
    turn = 0 if b0 == 0 else 1
    dve.wait_ge(m.n_ld, 32 * (turn + 1))
    nc.vector.reduce_max(m.k2_max[parts, :], m.k2_all[parts, :], AX.X).then_inc(m.k2_step, 1)
    dve.wait_ge(m.k2_step, 2 * turn + 1)
    nc.vector.tensor_scalar(m.k2_max[parts, :], m.k2_max[parts, :], NORM_UP, NORM_LEAST, ALU.mult, ALU.max).then_inc(m.k2_step, 1)


def root_norms(nc, act, m, b0, b1, ready):
    parts = slice(b0 * NPB, b1 * NPB)
    turn = 0 if b0 == 0 else 1
    act.wait_ge(m.n_ld, 32 * (turn + 1))
    act.wait_ge(m.k2_step, 2 * turn + 2)
    nc.scalar.activation(m.shift_all[parts, :], m.q2_all[parts, :], ACT.Sqrt, scale=m.k2_max[parts, 0:1]).then_inc(ready, 1)


def qkv_stage(nc, sb, sem, ps, m):
    with ExitStack() as ctx:
        xln = sb(ctx, "xln", [P, 2, GT, D], F32)
        xT = sb(ctx, "xT", [P, 2, DH, GN], F32)
        r = sb(ctx, "r", [P, 4, GN], F32)
        r1 = sb(ctx, "r1", [P, 4, GN], F32)
        split = sb(ctx, "split", [P, 2, 4, 3, GN], BF16)
        sq = sb(ctx, "sq", [P, 4, GN], BF16)
        vst = sb(ctx, "vst", [P, 2, H, GT, C], F32)
        st6 = sb(ctx, "st6", [P, 2, GT, 6], F32)
        mv = sb(ctx, "mv", [P, 2, GT, 2], F32)
        veps = sb(ctx, "veps", [P, GT], F32)
        q2 = sb(ctx, "q2", [HPH, 2, 2, GN], F32)
        nmax = sb(ctx, "nmax", [HPH, 2, GROUPS], F32)
        loaded = sb(ctx, "loaded_a", [P, 1], F32)
        kept, mark, cast = sem("a_kept"), sem("a_mark"), sem("a_cast")
        bn, aggr, veps_ready, rstd_ready, xln_ready = (sem("a_bn"), sem("a_aggr"), sem("a_veps_ready"), sem("a_rstd_ready"),
                                                       sem("a_xln_ready"))
        tr_done, xT_ready, qk_done, v_done, v_evac = (sem("a_tr_done"), sem("a_xT_ready"), sem("a_qk_done"), sem("a_v_done"),
                                                      sem("a_v_evac"))
        r_ready, r1_ready, mid_ready, split_ready = sem("a_r_ready"), sem("a_r1_ready"), sem("a_mid_ready"), sem("a_split_ready")
        stored = [sem("a_stored0"), sem("a_stored1")]
        sq_ready, nrm_done, nrm_red = sem("a_sq_ready"), sem("a_nrm_done"), sem("a_nrm_red")
        shift_ready, shift_stored = sem("a_shift_ready"), sem("a_shift_stored")
        tr = ps[:, 0:2, :]
        qkb = ps[:, 2:4, :]
        vb = ps[:, 4:6, :].rearrange("p a (t d) -> p a t d", t=2)
        nb = [ps[0:HPH, 6, :], ps[0:HPH, 7, :]]
        block = ctx.enter_context(nc.Block())

        @block.sync
        def _(sp):
            def load_x(b):
                for c in range(GPB):
                    sp.dma_start(m.x[:, ds((b * GPB + c) * GT, GT), :], m.xg[ds(b * GPB + c, 1)].rearrange("o p t d -> p (o t) d")).then_inc(m.x_ld, 16)

            def store_qk(b):
                for c in range(GPB):
                    for j in range(4):
                        wait_apart(sp, split_ready, b * (GPB * 4) + (c * 4 + j + 5), mark)
                        sp.dma_start(m.scr[j // 2][:, ds(b * D + (j % 2) * P, P), c * GN:(c + 1) * GN]
                                     .rearrange("s p n -> p s n"),
                                     split[:, c % 2, j, :, :]).then_inc(stored[c % 2], 16)
                    wait_apart(sp, v_evac, b * GPB + (c + 2), mark)
                    sp.dma_start(m.v_dram[:, ds(b * H, H), c * GT * C:(c + 1) * GT * C],
                                 vst[:, c % 2, :, :, :].rearrange("p h t c -> p h (t c)")).then_inc(stored[c % 2], 16)
                    wait_apart(sp, nrm_red, b * (4 * GPB) + (4 * c + 4), mark)
                    sp.dma_start(m.q2_dram[ds(b * H, H), c * GN:(c + 1) * GN].rearrange("(j h) n -> h j n", j=2),
                                 q2[:, c % 2, :, :]).then_inc(stored[c % 2], 16)

            sp.dma_start(m.x[:, 0:GT, :], m.xg[0]).then_inc(m.x_first, 16)
            for dst, src in m.first_loads:
                sp.dma_start(dst, src).then_inc(m.w_ld, 16)
            for g in range(1, GPB):
                sp.dma_start(m.x[:, g * GT:(g + 1) * GT, :], m.xg[g]).then_inc(m.x_ld, 16)
            for dst, src in m.late_loads:
                sp.dma_start(dst, src).then_inc(m.late_ld, 16)
            with sp.Fori(0, B - 1) as b:
                wait_apart(sp, m.x_ld, b * (16 * GPB) + 16 * (GPB - 1), mark)
                load_x(b + 1)
                store_qk(b)
            for u in range(2):
                sp.wait_ge(stored[u], 96 * ((B - 1) * GPB // 2 + 1))
            sp.wait_ge(nrm_red, (B - 1) * GPB * 4 + 2)
            turn_norms(nc, sp, m, nmax, 0, B - 1)
            store_qk(B - 1)
            sp.wait_ge(shift_ready, 1)
            sp.dma_start(by_partition(m.shift_dram)[0:(B - 1) * NPB, :], m.shift_all[0:(B - 1) * NPB, :]).then_inc(shift_stored, 16)
            for u in range(2):
                sp.wait_ge(stored[u], 96 * (GROUPS // 2 + 1))
            sp.wait_ge(nrm_red, GROUPS * 4 + 2)
            turn_norms(nc, sp, m, nmax, B - 1, B)
            sp.wait_ge(shift_stored, 16)
            sp.wait_ge(m.late_ld, 16 * len(m.late_loads))

        @block.gpsimd
        def _(pool):
            def norm(g, c):
                wait_apart(pool, aggr, g + 1, mark)
                nc.gpsimd.tensor_scalar(veps[:, :], mv[:, c % 2, :, 1], EPS, None, ALU.add).then_inc(veps_ready, 1)
                pool.wait_ge(veps_ready, g + 1)
                nc.gpsimd.tensor_tensor(m.rstd1[:, ds(g * GT, GT)], veps[:, :], m.mhalf[:, 0:GT], ALU.pow).then_inc(rstd_ready, 1)

            def low_parts(g, c):
                for j in range(4):
                    pool.wait_ge(mid_ready, g * 4 + j + 1)
                    nc.gpsimd.tensor_tensor(split[:, c % 2, j, 2, :], r1[:, j, :], split[:, c % 2, j, 1, :],
                                            ALU.subtract).then_inc(split_ready, 1)

            norm(0, 0)
            norm(1, 1)

            def batch(b, last):
                for c in range(GPB):
                    g = b * GPB + c
                    low_parts(g, c)
                    if not (last and c >= GPB - 2):
                        norm(g + 2, (c + 2) % GPB)

            with pool.Fori(0, B - 1) as b:
                batch(b, False)
            batch(B - 1, True)

        @block.vector
        def _(dve):
            for count, free in ((r_ready, 4), (r1_ready, 4), (split_ready, 4), (xT_ready, 1), (v_done, 2), (v_evac, 1),
                                (nrm_done, 4), (nrm_red, 2), (tr_done, 2), (stored[0], 96), (stored[1], 96)):
                dve.sem_inc(count, free)

            def statistics(g, b, c):
                if c == 0 and b is not None:
                    wait_apart(dve, m.x_ld, b * (16 * GPB) + 16 * (GPB - 1), mark)
                for t in range(GT):
                    last = nc.vector.bn_stats(st6[:, c % 2, t, :], flat(m.x[:, ds(g * GT + t, 1), :]))
                last.then_inc(bn, 1)
                wait_apart(dve, bn, g + 1, mark)
                for t in range(GT):
                    last = nc.vector.bn_aggr(mv[:, c % 2, t, :], st6[:, c % 2, t, :])
                last.then_inc(aggr, 1)
                dve.wait_ge(aggr, g + 1)
                nc.vector.tensor_copy(m.stat1[:, ds(g * GT, GT), :], mv[:, c % 2, :, :]).then_inc(kept, 1)

            def normalise(g, c):
                dve.wait_ge(tr_done, g + 1)
                dve.wait_ge(rstd_ready, g + 1)
                for t in range(GT):
                    nc.vector.tensor_scalar(xln[:, c % 2, t, :], flat(m.x[:, ds(g * GT + t, 1), :]),
                                            mv[:, c % 2, t, 0:1], m.rstd1[:, ds(g * GT + t, 1)],
                                            ALU.subtract, ALU.mult).then_inc(xln_ready, 1)

            def parts(g, c, chunks):
                for j in chunks:
                    n = g * 4 + j
                    dve.wait_ge(r_ready, n + 5)
                    dve.wait_ge(split_ready, n + 1)
                    nc.vector.tensor_tensor(r1[:, j, :], r[:, j, :], split[:, c % 2, j, 0, :],
                                            ALU.subtract).then_inc(r1_ready, 1)
                    dve.wait_ge(nrm_done, n + 1)
                    nc.vector.tensor_tensor(sq[:, j, :], split[:, c % 2, j, 0, :], split[:, c % 2, j, 0, :],
                                            ALU.mult).then_inc(sq_ready, 1)

            def values(g, b, c):
                dve.wait_ge(v_done, g + 3)
                dve.wait_ge(stored[c % 2], b * 192 + 96 * (c // 2 + 1))
                nc.vector.tensor_tensor(vst[:, c % 2, :, :, :], vb.rearrange("p a t (h c) -> p h (a t) c", c=C),
                                        bcast(m.bv[:, :].rearrange("p (h c) -> p h c", c=C), 2, GT), ALU.add).then_inc(v_evac, 1)

            def norms(g, b, c, chunks):
                for j in chunks:
                    dve.wait_ge(nrm_done, g * 4 + j + 5)
                    if j < 2:
                        dve.wait_ge(stored[c % 2], b * 192 + 96 * (c // 2 + 1))
                        nc.vector.tensor_scalar(q2[:, c % 2, j, :], nb[j % 2], NORM_UP, NORM_LEAST, ALU.mult, ALU.max).then_inc(nrm_red, 1)
                    else:
                        nc.vector.reduce_max(nmax[:, j - 2, ds(g, 1)], nb[j % 2], AX.X).then_inc(nrm_red, 1)

            dve.wait_ge(m.x_first, 16)
            statistics(0, None, 0)
            normalise(0, 0)
            dve.wait_ge(m.w_ld, 16 * len(m.first_loads))
            nc.vector.tensor_copy(m.headsum[:, :], m.headsum_f[:, :])
            nc.vector.tensor_copy(m.identb[:, :], m.ident[:, :]).then_inc(cast, 1)
            dve.wait_ge(m.x_ld, 16 * (GPB - 1))
            statistics(1, 0, 1)

            def batch(b, last):
                for c in range(GPB):
                    g = b * GPB + c
                    parts(g, c, (0, 1))
                    if not (last and c == GPB - 1):
                        normalise(g + 1, (c + 1) % GPB)
                    parts(g, c, (2, 3))
                    norms(g, b, c, (0, 1))
                    values(g, b, c)
                    norms(g, b, c, (2, 3))
                    if not (last and c >= GPB - 2):
                        statistics(g + 2, b + (c + 2) // GPB, (c + 2) % GPB)
                    if last and c == 1:
                        largest_norms(nc, dve, m, 0, B - 1)

            with dve.Fori(0, B - 1) as b:
                batch(b, False)
            batch(B - 1, True)
            dve.wait_ge(nrm_red, GROUPS * 4 + 2)
            dve.wait_ge(kept, GROUPS)
            dve.wait_ge(cast, 1)

        @block.scalar
        def _(act):
            def turned(g, c):
                act.wait_ge(tr_done, g + 3)
                act.wait_ge(v_done, g + 1)
                nc.scalar.copy(xT[:, c % 2, 0, :], tr[:, 0, :])
                nc.scalar.copy(xT[:, c % 2, 1, :], tr[:, 1, :]).then_inc(xT_ready, 1)

            def biased(g, b, c):
                act.wait_ge(stored[c % 2], b * 192 + 96 * (c // 2 + 1))
                def middle(j):
                    act.wait_ge(r1_ready, g * 4 + j + 5)
                    nc.scalar.copy(split[:, c % 2, j, 1, :], r1[:, j, :]).then_inc(mid_ready, 1)

                for j in range(4):
                    n = g * 4 + j
                    act.wait_ge(qk_done, n + 1)
                    act.wait_ge(r1_ready, n + 1)
                    nc.scalar.activation(split[:, c % 2, j, 0, :], qkb[:, j % 2, :], ACT.Identity, bias=m.bqk[:, j:j + 1])
                    nc.scalar.activation(r[:, j, :], qkb[:, j % 2, :], ACT.Identity, bias=m.bqk[:, j:j + 1]).then_inc(r_ready, 1)
                    if j > 0:
                        middle(j - 1)
                middle(3)

            nc.scalar.activation(loaded[:, :], m.zeros[:, 0:1], ACT.Identity)
            act.wait_ge(m.w_ld, 16 * len(m.first_loads))
            turned(0, 0)

            def batch(b, last):
                for c in range(GPB):
                    g = b * GPB + c
                    biased(g, b, c)
                    if not (last and c == GPB - 1):
                        turned(g + 1, (c + 1) % GPB)
                    if last and c == 1:
                        root_norms(nc, act, m, 0, B - 1, shift_ready)

            with act.Fori(0, B - 1) as b:
                batch(b, False)
            batch(B - 1, True)

        @block.tensor
        def _(pe):
            pe.wait_ge(m.w_ld, 16 * len(m.first_loads))

            def turn(g, c):
                pe.wait_ge(xT_ready, g + 1)
                for t in range(GT):
                    pe.wait_ge(xln_ready, g * GT + t + 1)
                    for k in range(DH):
                        last = nc.tensor.transpose(tr[:, k, t * P:(t + 1) * P], xln[:, c % 2, t, k * P:(k + 1) * P], m.ident[:, :])
                last.then_inc(tr_done, 1)

            def qk(g, c):
                pe.wait_ge(xT_ready, g + 2)
                for j in range(4):
                    pe.wait_ge(r_ready, g * 4 + j + 3)
                    for k in range(DH):
                        last = nc.tensor.matmul(qkb[:, j % 2, :], m.wqkv[:, k, j * P:(j + 1) * P], xT[:, c % 2, k, :],
                                                start=(k == 0), stop=(k == DH - 1))
                    last.then_inc(qk_done, 1)

            def v(g, c):
                pe.wait_ge(v_evac, g + 1)
                for t in range(GT):
                    for k in range(DH):
                        last = nc.tensor.matmul(vb[:, t // 2, t % 2, :], xT[:, c % 2, k, t * P:(t + 1) * P],
                                                m.wqkv[:, k, 2 * D:3 * D], start=(k == 0), stop=(k == DH - 1))
                last.then_inc(v_done, 1)

            def norms(g, chunks):
                for j in chunks:
                    pe.wait_ge(sq_ready, g * 4 + j + 1)
                    pe.wait_ge(nrm_red, g * 4 + j + 1)
                    nc.tensor.matmul(nb[j % 2], m.headsum[:, :], sq[:, j, :], start=True, stop=True).then_inc(nrm_done, 1)

            turn(0, 0)
            pe.wait_ge(cast, 1)

            def batch(b, last):
                for c in range(GPB):
                    g = b * GPB + c
                    qk(g, c)
                    norms(g, (0, 1))
                    if not (last and c == GPB - 1):
                        turn(g + 1, (c + 1) % GPB)
                    v(g, c)
                    norms(g, (2, 3))

            with pe.Fori(0, B - 1) as b:
                batch(b, False)
            batch(B - 1, True)


def attention_stage(nc, sb_of, sem_of, ps, m, exact):
    run = "_exact" if exact else ""

    def sem(name):
        return sem_of(name + run)

    def sb(ctx, name, shape, dt):
        return sb_of(ctx, name + run, shape, dt)

    def when_needed(eng):
        if not exact:
            return nullcontext()
        return eng.If(eng.value_load(m.flag[0:1, 0:1], min_val=0, max_val=1) == 1)

    stack = SR + (2 if exact else 1)
    PS = 4
    STEPS = 4 * KT
    slot = [s % 3 for s in range(STEPS - 1)] + [1]
    back_to = [next(d for d in range(1, STEPS) if slot[(s - d) % STEPS] == slot[s]) for s in range(STEPS)]
    with ExitStack() as ctx:
        qs = [sb(ctx, f"qs{u}", [stack, L], BF16) for u in range(2)]
        ks = [sb(ctx, f"ks{u}", [stack, L], BF16) for u in range(2)]
        probs = sb(ctx, "probs", [P, PS, L], F32)
        vst = sb(ctx, "vst_b", [P, 2, KT * C], F32)
        vs = sb(ctx, "vs", [P, 2, KT, 2 * C], F32)
        osb = sb(ctx, "osb", [P, 512], F32)
        sums = sb(ctx, "sums", [P, 512], F32)
        rc = sb(ctx, "rc", [P, 512], F32)
        hout = sb(ctx, "hout", [P, 2, 512], F32)
        loaded = sb(ctx, "loaded", [P, 1], F32)
        rcmax = sb(ctx, "rcmax", [P, HEADS], F32)
        worst = sb(ctx, "worst", [P, 1], F32)
        verdict = sb(ctx, "verdict", [1, 2], F32)
        part = sb(ctx, "part", [P, KT, 4], F32)
        rowmax = sb(ctx, "rowmax", [P, KT], F32)
        shift = sb(ctx, "shift", [KT, 2, 2, P], BF16)
        setup, mark = sem("b_setup"), sem("b_mark")
        qk_ld = [sem("b_qk_ld0"), sem("b_qk_ld1")]
        sc_done, exp_done, pv_done, v_staged = sem("b_sc_done"), sem("b_exp_done"), sem("b_pv_done"), sem("b_v_staged")
        v_ld = [sem("b_v_ld0"), sem("b_v_ld1")]
        o_evac, sums_ready, rc_ready, hd_done = sem("b_o_evac"), sem("b_sums_ready"), sem("b_rc_ready"), sem("b_hd_done")
        hd_stored = [sem("b_hd_stored0"), sem("b_hd_stored1")]
        if exact:
            mx_done, mx_red, row_ready, rowT, shi, shift_ready = (
                sem("b_mx_done"), sem("b_mx_red"), sem("b_row_ready"), sem("b_rowT"), sem("b_shi"), sem("b_shift_ready"))
            shift_ld = [sem("b_shift_ld0"), sem("b_shift_ld1")]
        else:
            kept, fin, worst_turned = sem("b_kept"), sem("b_fin"), sem("b_worst_turned")
            shift_ready, shift_stored = sem("b_bound_ready"), sem("b_bound_stored")
        sc = [ps[:, 2 * k:2 * k + 2, :] for k in range(3)]
        ob = [ps[:, 6, :], ps[:, 7, :]]
        PAIRS = HEADS // 2
        LOADS = 6 if exact else 7
        block = ctx.enter_context(nc.Block())

        @block.sync
        def _(sp):
            def load(n, u):
                row = 0
                for s, times in Q_GROUPS:
                    src = m.scr[0][s, ds(n * C, C), :]
                    sp.dma_start(qs[u][row:row + times * C, :], bcast(src, 0, times) if times > 1 else src).then_inc(qk_ld[u], 16)
                    row += times * C
                row = 0
                for s, parts in K_RUNS:
                    sp.dma_start(ks[u][row:row + parts * C, :], m.scr[1][s:s + parts, ds(n * C, C), :]).then_inc(qk_ld[u], 16)
                    row += parts * C
                sp.dma_start(vst[:, u, :], m.v_dram[:, ds(n, 1), :].rearrange("p o c -> p (o c)")).then_inc(v_ld[u], 16)
                if not exact:
                    sp.dma_start(qs[u][SR:SR + 1, :], m.shift_dram[ds(n, 1), :]).then_inc(qk_ld[u], 16)

            def put_shift(n, u):
                if exact:
                    wait_apart(sp, shift_ready, n + 1, mark)
                    for a in range(2):
                        sp.dma_start(qs[u][SR + a:SR + a + 1, :], shift[:, u, a, :]).then_inc(shift_ld[u], 16)

            def store(n, u):
                wait_apart(sp, hd_done, n + 1, mark)
                for j in range(4):
                    sp.dma_start(m.heads_dram[ds(n * C, C), j * 512:(j + 1) * 512],
                                 hout[32 * j + C:32 * (j + 1), u, :]).then_inc(hd_stored[u], 16)

            def turn(i, first):
                for u in range(2):
                    put_shift(2 * i + (u - 2), u)
                    wait_apart(sp, sc_done, i * STEPS + (u - 1) * 2 * KT, mark)
                    load(2 * i + u, u)
                    if not (first and u == 0):
                        store(2 * i + (u - 3), 1 - u)

            with when_needed(sp):
                if exact:
                    sp.wait_ge(setup, 3)
                for u in range(2):
                    load(u, u)
                if not exact:
                    sp.wait_ge(shift_ready, 1)
                    sp.dma_start(by_partition(m.shift_dram)[(B - 1) * NPB:, :], m.shift_all[(B - 1) * NPB:, :]).then_inc(shift_stored, 16)
                    sp.wait_ge(shift_stored, 16)
                turn(1, True)
                with sp.Fori(2, PAIRS) as i:
                    turn(i, False)
                put_shift(HEADS - 2, 0)
                store(HEADS - 3, 1)
                put_shift(HEADS - 1, 1)
                store(HEADS - 2, 0)
                store(HEADS - 1, 1)
                for u in range(2):
                    sp.wait_ge(hd_stored[u], 64 * (PAIRS + 1))

        @block.gpsimd
        def _(pool):
            def stage_v(i, u):
                wait_apart(pool, v_ld[u], i * 16 + 16, mark)
                nc.gpsimd.tensor_copy(vs[:, u, :, C:2 * C], vst[:, u, :].rearrange("p (t c) -> p t c", c=C)).then_inc(v_staged, 1)

            with when_needed(pool):
                nc.gpsimd.memset(vs[:, :, :, 0:C], 1.0).then_inc(setup, 1)
                for u in range(2):
                    stage_v(0, u)
                with pool.Fori(1, PAIRS) as i:
                    for u in range(2):
                        wait_apart(pool, pv_done, i * (2 * KT) + (u - 1) * KT + PS, mark)
                        stage_v(i, u)

        @block.vector
        def _(dve):
            def row_max(n, i, u):
                for qt in range(KT):
                    for kc in range(4):
                        dve.wait_ge(mx_done, n * (4 * KT) + qt * 4 + kc + 1)
                        nc.vector.reduce_max(part[:, qt, kc:kc + 1], ob[u], AX.X).then_inc(mx_red, 1)
                dve.wait_ge(mx_red, n * (4 * KT) + 4 * KT + 1)
                nc.vector.reduce_max(rowmax[:, :], part[:, :, :], AX.X).then_inc(row_ready, 1)
                dve.wait_ge(rowT, n + 1)
                dve.wait_ge(shift_ld[u], i * 32 + 32)
                nc.vector.tensor_scalar(shift[:, u, 0, :], ob[u][0:KT, 0:P], -1.0, None, ALU.mult).then_inc(shi, 1)
                dve.wait_ge(shi, n + 1)
                nc.vector.scalar_tensor_tensor(out=shift[:, u, 1, :], in0=ob[u][0:KT, 0:P], scalar=-1.0,
                                               in1=shift[:, u, 0, :], op0=ALU.mult, op1=ALU.subtract).then_inc(shift_ready, 1)

            def finish(n, i, u):
                dve.wait_ge(pv_done, n * KT + KT + PS)
                nc.vector.tensor_copy(osb[:, :], ob[u]).then_inc(o_evac, 1)
                wait_apart(dve, o_evac, n + 3, mark)
                nc.vector.stream_shuffle(sums[:, :], osb[:, :], [k % C for k in range(32)]).then_inc(sums_ready, 1)
                dve.wait_ge(sums_ready, n + 1)
                nc.vector.reciprocal(rc[:, :], sums[:, :]).then_inc(rc_ready, 1)
                dve.wait_ge(rc_ready, n + 1)
                dve.wait_ge(hd_stored[u], i * 64 + 64)
                nc.vector.tensor_tensor(hout[:, u, :], osb[:, :], rc[:, :], ALU.mult).then_inc(hd_done, 1)
                if not exact:
                    nc.vector.reduce_max(rcmax[:, ds(n, 1)], rc[:, :], AX.X).then_inc(kept, 1)
                    dve.wait_ge(kept, n + 1)
                dve.wait_ge(hd_done, n + 1)

            def pair(i, last):
                for u in range(2):
                    n = 2 * i + u
                    if exact and not (last and u == 1):
                        row_max(n + 1, i + u, 1 - u)
                    finish(n, i, u)

            with when_needed(dve):
                for count, free in ((pv_done, PS), (o_evac, 2), (hd_stored[0], 64), (hd_stored[1], 64)):
                    dve.sem_inc(count, free)
                for u in range(2):
                    nc.vector.memset(ks[u][SR:stack, :], 1.0 if exact else -1.0).then_inc(setup, 1)
                if not exact:
                    largest_norms(nc, dve, m, B - 1, B)
                if exact:
                    for count, free in ((mx_red, 1), (shift_ld[0], 32), (shift_ld[1], 32)):
                        dve.sem_inc(count, free)
                    row_max(0, 0, 0)
                with dve.Fori(0, PAIRS - 1) as i:
                    pair(i, False)
                pair(PAIRS - 1, True)
                dve.wait_ge(hd_done, HEADS)
            if not exact:
                dve.wait_ge(kept, HEADS)
                nc.vector.reduce_max(worst[:, :], rcmax[:, :], AX.X).then_inc(fin, 1)
                dve.wait_ge(worst_turned, 1)
                nc.vector.reduce_max(verdict[:, 0:1], sc[0][0:1, 0, 0:P], AX.X).then_inc(fin, 1)
                dve.wait_ge(fin, 2)
                nc.vector.tensor_scalar(verdict[:, 1:2], verdict[:, 0:1], 1.0 / LEAST_SUM, None, ALU.is_le).then_inc(fin, 1)
                dve.wait_ge(fin, 3)
                nc.vector.tensor_scalar(m.flag[:, :], verdict[:, 1:2], -1.0, 1.0, ALU.mult, ALU.add).then_inc(fin, 1)
                dve.wait_ge(fin, 4)

        @block.scalar
        def _(act):
            with when_needed(act):
                if not exact:
                    root_norms(nc, act, m, B - 1, B, shift_ready)
                nc.scalar.activation(loaded[:, :], m.zeros[:, 0:1], ACT.Exp)
                with act.Fori(0, PAIRS) as i:
                    for s in range(STEPS):
                        if s % 2 == 0:
                            act.wait_ge(pv_done, i * (2 * KT) + s // 2 + 1)
                        act.wait_ge(sc_done, i * STEPS + s + 1)
                        half = s % 2
                        nc.scalar.activation(probs[:, s // 2 % PS, half * (L // 2):(half + 1) * (L // 2)], sc[slot[s]],
                                             ACT.Exp, scale=SCALE).then_inc(exp_done, 1)

        @block.tensor
        def _(pe):
            def max_scores(n, i, u):
                pe.wait_ge(qk_ld[u], i * (16 * LOADS) + 16 * LOADS)
                pe.wait_ge(o_evac, n + 1)
                for qt in range(KT):
                    for kc in range(4):
                        pe.wait_ge(mx_red, n * (4 * KT) + qt * 4 + kc + 1)
                        nc.tensor.matmul(ob[u], qs[u][0:SR, qt * P:(qt + 1) * P], ks[u][0:SR, kc * 512:(kc + 1) * 512],
                                         start=True, stop=True).then_inc(mx_done, 1)
                pe.wait_ge(row_ready, n + 1)
                nc.tensor.transpose(ob[u][0:KT, 0:P], rowmax[:, :], m.ident[:, :]).then_inc(rowT, 1)
                pe.wait_ge(shift_ld[u], i * 32 + 64)
                pe.wait_ge(shift_ready, n + 1)

            def scores(i, s, first):
                i, s, first = (i, s, first) if s < STEPS else (i + 1, s - STEPS, False)
                u, kt, half = s // (2 * KT), s // 2 % KT, s % 2
                if s % (2 * KT) == 0:
                    if exact:
                        max_scores(2 * i + u, i, u)
                    pe.wait_ge(qk_ld[u], i * (16 * LOADS) + 16 * LOADS)
                if not (first and s < 3):
                    pe.wait_ge(exp_done, i * STEPS + (s - back_to[s] + 1))
                for a in range(2):
                    q0 = (2 * half + a) * 512
                    last = nc.tensor.matmul(sc[slot[s]][:, a, :], ks[u][:, kt * P:(kt + 1) * P], qs[u][:, q0:q0 + 512],
                                            start=True, stop=True)
                last.then_inc(sc_done, 1)

            def values(i, u, kt):
                n = 2 * i + u
                if kt == 0:
                    pe.wait_ge(v_staged, n + 1)
                    pe.wait_ge(o_evac, n + 1)
                pe.wait_ge(exp_done, i * STEPS + (u * 2 * KT + 2 * kt + 2))
                for j in range(4):
                    last = nc.tensor.matmul(ob[u][32 * j:32 * (j + 1), :], vs[:, u, kt, :], probs[:, kt % PS, j * 512:(j + 1) * 512],
                                            start=(kt == 0), stop=(kt == KT - 1))
                last.then_inc(pv_done, 1)

            def pair(i, first, last):
                for t in range(2 * KT):
                    for s in (2 * t + 3, 2 * t + 4):
                        if not (last and s >= STEPS):
                            scores(i, s, first)
                    values(i, t // KT, t % KT)

            with when_needed(pe):
                pe.wait_ge(setup, 3)
                for s in range(3):
                    scores(0, s, True)
                pair(0, True, False)
                with pe.Fori(1, PAIRS - 1) as i:
                    pair(i, False, False)
                pair(PAIRS - 1, False, True)
            if not exact:
                pe.wait_ge(fin, 1)
                nc.tensor.transpose(sc[0][0:1, 0, 0:P], worst[:, :], m.ident[:, :]).then_inc(worst_turned, 1)


def dense_stage(nc, sb, sem, ps, m):
    with ExitStack() as ctx:
        hT = sb(ctx, "hT", [P, 2, DH, GN], F32)
        fT = sb(ctx, "fT", [P, DH, GN], F32)
        xb = sb(ctx, "xb", [P, GT, D], F32)
        t1 = sb(ctx, "t1", [P, GT, D], F32)
        xf = sb(ctx, "xf", [P, GT, D], F32)
        st6 = sb(ctx, "st6c", [P, GT, 6], F32)
        mv = sb(ctx, "mvc", [P, 2, GT, 2], F32)
        veps = sb(ctx, "vepsc", [P, GT], F32)
        th = sb(ctx, "th", [P, DH, GN], F32)
        gT = sb(ctx, "gT", [P, DH, GN], F32)
        y = sb(ctx, "y", [P, 2, GT, D], F32)
        hT_ld0, hT_ld1, xb_ready, ln1_ready, t1_ready = sem("c_hT_ld0"), sem("c_hT_ld1"), sem("c_xb_ready"), sem("c_ln1_ready"), sem("c_t1_ready")
        pj_done, x1_ready = sem("c_pj_done"), sem("c_x1_ready")
        bn, aggr, veps_ready, rstd_ready, xf_ready = (sem("c_bn"), sem("c_aggr"), sem("c_veps_ready"), sem("c_rstd_ready"),
                                                      sem("c_xf_ready"))
        ftr_done, fT_ready, lg_done, lg_evac = sem("c_ftr_done"), sem("c_fT_ready"), sem("c_lg_done"), sem("c_lg_evac")
        ab_done, th_ready, sg_ready, g_ready = sem("c_ab_done"), sem("c_th_ready"), sem("c_sg_ready"), sem("c_g_ready")
        so_done, y_ready, stored = sem("c_so_done"), sem("c_y_ready"), sem("c_stored")
        hT_ld = [hT_ld0, hT_ld1]
        half_ready, kept, mark = sem("c_half_ready"), sem("c_kept"), sem("c_mark")
        pj = ps[:, 0:2, :].rearrange("p a (t d) -> p (a t) d", t=2)
        tr = ps[:, 0:2, :]
        so = ps[:, 2:4, :].rearrange("p a (t d) -> p (a t) d", t=2)
        lg = ps[:, 2, 0:GT * NE].rearrange("p (t e) -> p t e", e=NE)
        ab = [ps[:, 4:6, :], ps[:, 6:8, :]]
        block = ctx.enter_context(nc.Block())

        @block.sync
        def _(sp):
            sp.sem_inc(stored, 32)

            def load_heads(b, c):
                sp.dma_start(hT[:, c % 2, :, :], m.heads_dram[ds(b * D, D), c * GN:(c + 1) * GN]
                             .rearrange("(k p) n -> p k n", p=P)).then_inc(hT_ld[c % 2], 16)

            def store_out(g, u):
                wait_apart(sp, y_ready, g + 2, mark)
                sp.dma_start(m.og[ds(g, 1)].rearrange("o p t d -> p (o t) d"), y[:, u, :, :]).then_inc(stored, 16)
                wait_apart(sp, stored, g * 16 + 48, mark)

            def batch(b, last):
                for c in range(GPB):
                    if not (last and c >= GPB - 2):
                        wait_apart(sp, pj_done, b * GPB + (c + 2), mark)
                        load_heads(b + (c + 2) // GPB, (c + 2) % GPB)
                    store_out(b * GPB + c, c % 2)

            load_heads(0, 0)
            load_heads(0, 1)
            for dst, src in ((m.w1, m.w1_dram), (m.w3, m.w3_dram)):
                for k in range(DH):
                    sp.dma_start(dst[:, k, :, :], src[:, k * P:(k + 1) * P, :].rearrange("e p h -> p e h")).then_inc(m.experts_ld, 16)
            sp.dma_start(m.w2[:, :, :], m.w2_dram.rearrange("e p d -> p e d")).then_inc(m.experts_ld, 16)
            with sp.Fori(0, B - 1) as b:
                batch(b, False)
            batch(B - 1, True)

        @block.gpsimd
        def _(pool):
            for count, free in ((pj_done, 1), (x1_ready, 1), (ftr_done, 1), (fT_ready, 1), (lg_evac, 1), (g_ready, 2),
                                (so_done, 1), (y_ready, 1)):
                pool.sem_inc(count, free)
            with pool.Fori(0, B) as b:
                for c in range(GPB):
                    g = b * GPB + c
                    pool.wait_ge(x1_ready, g + 1)
                    nc.gpsimd.tensor_tensor(xb[:, :, :], m.x[:, ds(g * GT, GT), :], bcast(m.bo[:, :], 1, GT), ALU.add).then_inc(xb_ready, 1)
                    wait_apart(pool, aggr, g + 1, mark)
                    nc.gpsimd.tensor_scalar(veps[:, :], mv[:, c % 2, :, 1], EPS, None, ALU.add).then_inc(veps_ready, 1)
                    pool.wait_ge(veps_ready, g + 1)
                    nc.gpsimd.tensor_tensor(m.rstd2[:, ds(g * GT, GT)], veps[:, :], m.mhalf[:, 0:GT], ALU.pow).then_inc(rstd_ready, 1)

        @block.scalar
        def _(act):
            def feed(g):
                act.wait_ge(ftr_done, g + 2)
                nc.scalar.copy(fT[:, 0, :], tr[:, 0, :])
                nc.scalar.copy(fT[:, 1, :], tr[:, 1, :]).then_inc(fT_ready, 1)
                for k in range(DH):
                    act.wait_ge(ab_done, g * DH + k + 1)
                    act.wait_ge(g_ready, g * DH + k + 1)
                    nc.scalar.activation(th[:, k, :], ab[k][:, 0, :], ACT.Tanh, scale=0.5).then_inc(th_ready, 1)
                act.wait_ge(lg_done, g + 1)
                nc.scalar.copy(m.logits[:, ds(g * GT, GT), :], lg).then_inc(lg_evac, 1)

            with act.Fori(0, GROUPS) as g:
                feed(g)

        @block.vector
        def _(dve):
            nc.vector.tensor_scalar(m.sw2h[:, :, :], m.sw2[:, :, :], 0.5, None, ALU.mult).then_inc(half_ready, 1)

            def join(g, u):
                for t in range(GT):
                    last = nc.vector.tensor_scalar(t1[:, t, :], flat(m.x[:, ds(g * GT + t, 1), :]),
                                                   m.stat1[:, ds(g * GT + t, 1), 0], m.rstd1[:, ds(g * GT + t, 1)], ALU.subtract, ALU.mult)
                last.then_inc(ln1_ready, 1)
                dve.wait_ge(ln1_ready, g + 1)
                dve.wait_ge(xb_ready, g + 1)
                nc.vector.tensor_tensor(t1[:, :, :], t1[:, :, :], xb[:, :, :], ALU.add).then_inc(t1_ready, 1)
                dve.wait_ge(t1_ready, g + 1)
                dve.wait_ge(pj_done, g + 2)
                nc.vector.tensor_tensor(m.x[:, ds(g * GT, GT), :], t1[:, :, :], pj, ALU.add).then_inc(x1_ready, 1)
                wait_apart(dve, x1_ready, g + 2, mark)
                for t in range(GT):
                    last = nc.vector.bn_stats(st6[:, t, :], flat(m.x[:, ds(g * GT + t, 1), :]))
                last.then_inc(bn, 1)
                wait_apart(dve, bn, g + 1, mark)
                for t in range(GT):
                    last = nc.vector.bn_aggr(mv[:, u, t, :], st6[:, t, :])
                last.then_inc(aggr, 1)
                dve.wait_ge(aggr, g + 1)
                nc.vector.tensor_copy(m.stat2[:, ds(g * GT, GT), :], mv[:, u, :, :]).then_inc(kept, 1)

            def normalise(g, u):
                dve.wait_ge(rstd_ready, g + 1)
                dve.wait_ge(ftr_done, g + 1)
                for t in range(GT):
                    last = nc.vector.tensor_scalar(xf[:, t, :], flat(m.x[:, ds(g * GT + t, 1), :]),
                                                   mv[:, u, t, 0:1], m.rstd2[:, ds(g * GT + t, 1)], ALU.subtract, ALU.mult)
                last.then_inc(xf_ready, 1)

            def gate(g, k):
                dve.wait_ge(th_ready, g * DH + k + 1)
                nc.vector.scalar_tensor_tensor(out=th[:, k, :], in0=th[:, k, :], scalar=1.0, in1=ab[k][:, 0, :],
                                               op0=ALU.add, op1=ALU.mult).then_inc(sg_ready, 1)
                dve.wait_ge(sg_ready, g * DH + k + 1)
                if k == 0:
                    dve.wait_ge(so_done, g + 1)
                nc.vector.tensor_tensor(gT[:, k, :], th[:, k, :], ab[k][:, 1, :], ALU.mult).then_inc(g_ready, 1)

            def put_out(g, u):
                dve.wait_ge(so_done, g + 2)
                dve.wait_ge(stored, g * 16 + 16)
                nc.vector.tensor_tensor(y[:, u, :, :], m.x[:, ds(g * GT, GT), :], so, ALU.add).then_inc(y_ready, 1)

            def pair(i, first, last):
                for u in range(2):
                    g = 2 * i + u
                    if not (first and u == 0):
                        put_out(2 * i + (u - 1), 1 - u)
                    more = not (last and u == 1)
                    if more:
                        join(2 * i + (u + 1), 1 - u)
                    gate(g, 0)
                    if more:
                        normalise(2 * i + (u + 1), 1 - u)
                    gate(g, 1)

            join(0, 0)
            normalise(0, 0)
            pair(0, True, False)
            with dve.Fori(1, GROUPS // 2 - 1) as i:
                pair(i, False, False)
            pair(GROUPS // 2 - 1, False, True)
            put_out(GROUPS - 1, 1)

        @block.tensor
        def _(pe):
            pe.wait_ge(half_ready, 1)

            def project(g, u):
                pe.wait_ge(hT_ld[u], (g - u) * 8 + 16)
                pe.wait_ge(fT_ready, g + 1)
                for t in range(GT):
                    for k in range(DH):
                        last = nc.tensor.matmul(pj[:, t, :], hT[:, u, k, t * P:(t + 1) * P], m.wo[:, k, :], start=(k == 0), stop=(k == DH - 1))
                last.then_inc(pj_done, 1)

            def turn(g):
                pe.wait_ge(x1_ready, g + 2)
                pe.wait_ge(xf_ready, g + 1)
                for t in range(GT):
                    for k in range(DH):
                        last = nc.tensor.transpose(tr[:, k, t * P:(t + 1) * P], xf[:, t, k * P:(k + 1) * P], m.ident[:, :])
                last.then_inc(ftr_done, 1)

            def add_shared(g):
                pe.wait_ge(lg_evac, g + 2)
                pe.wait_ge(g_ready, g * DH + 4)
                for t in range(GT):
                    for k in range(DH):
                        last = nc.tensor.matmul(so[:, t, :], gT[:, k, t * P:(t + 1) * P], m.sw2h[:, k, :], start=(k == 0), stop=(k == DH - 1))
                last.then_inc(so_done, 1)

            def widen(g):
                pe.wait_ge(fT_ready, g + 2)
                for h in range(DH):
                    pe.wait_ge(g_ready, g * DH + h + 1)
                    for o, w in ((0, m.sw1), (1, m.sw3)):
                        for k in range(DH):
                            last = nc.tensor.matmul(ab[h][:, o, :], w[:, k, h * P:(h + 1) * P], fT[:, k, :], start=(k == 0), stop=(k == DH - 1))
                    last.then_inc(ab_done, 1)
                pe.wait_ge(y_ready, g + 1)
                for t in range(GT):
                    for k in range(DH):
                        last = nc.tensor.matmul(lg[:, t, :], fT[:, k, t * P:(t + 1) * P], m.wg[:, k, :], start=(k == 0), stop=(k == DH - 1))
                last.then_inc(lg_done, 1)

            def pair(i, first, last):
                for u in range(2):
                    g = 2 * i + u
                    turn(g)
                    if not (first and u == 0):
                        add_shared(2 * i + (u - 1))
                    if not (last and u == 1):
                        project(2 * i + (u + 1), 1 - u)
                    widen(g)

            project(0, 0)
            pair(0, True, False)
            with pe.Fori(1, GROUPS // 2 - 1) as i:
                pair(i, False, False)
            pair(GROUPS // 2 - 1, False, True)
            add_shared(GROUPS - 1)


def routed_stage(nc, sb, sem, ps, m):
    RT = 2 * TILES
    JE = NE * NE
    QT = 2
    STEPS = TILES // QT
    OS = 4
    BIG = 3.0e38
    with ExitStack() as ctx:
        s8 = [sb(ctx, f"s8_{i}", [P, TILES, NE], F32) for i in range(5)]
        scores = s8[1][:, :, :]
        one = [sb(ctx, f"one{i}", [P, TILES], F32) for i in range(3)]
        s4 = [sb(ctx, f"s4_{i}", [P, TILES, NG], F32) for i in range(5)]
        ohk = sb(ctx, "ohk", [P, TILES, 2, NE], F32)
        kscore = sb(ctx, "kscore", [P, TILES, 2, NE], F32)
        ohkw = sb(ctx, "ohkw", [P, TILES, 2, NE], F32)
        wk = sb(ctx, "wk", [P, TILES, 2], F32)
        reached = sb(ctx, "reached", [P, RT, NE + 1], F32)
        span = sb(ctx, "span", [P, RT, NE], F32)
        cnt = sb(ctx, "cnt", [P, NE], F32)
        csum = sb(ctx, "csum", [P, NE, NE], F32)
        offs = sb(ctx, "offs", [P, NE], F32)
        x0 = sb(ctx, "x0", [NE, D], F32)
        x0T = sb(ctx, "x0T", [P, DH, NE], F32)
        arow = sb(ctx, "arow", [NE, NE * HID], F32)
        a2 = sb(ctx, "a2", [P, HID], F32)
        arest = sb(ctx, "arest", [P, HID], F32)
        ad = sb(ctx, "ad", [P, 3, 2 * HID], BF16)
        bT = sb(ctx, "bT", [HID, NE, NE], F32)
        hT = sb(ctx, "hTd", [HID, NE, NE], F32)
        ohw = sb(ctx, "ohw", [P, OS, 2 * QT, NE, NE], F32)
        ohb = sb(ctx, "ohb", [P, OS, 2 * QT, NE, NE], BF16)
        gsum = sb(ctx, "gsum", [P, HID], F32)
        g2 = sb(ctx, "g2", [HID, NE, NE], F32)
        ohT = sb(ctx, "ohT", [P, 2, QT, P], BF16)
        z, th, sil = (m.x[:, (i + 1) * 4:(i + 2) * 4, :].rearrange("p t d -> p (t d)").rearrange("p (u r h) -> p u r h", u=2, h=HID)
                      for i in range(3))
        rows = sb(ctx, "rows", [NE, D], F32)
        final = sb(ctx, "final", [NE, D], F32)
        rows_ld, a_ld, out_st = sem("d_rows_ld"), sem("d_a_ld"), sem("d_out_st")
        step, shifted, exped = sem("d_step"), sem("d_shifted"), sem("d_exped")
        bT_ready, cnt_ready, cnt_sum, x0_ready, x0_tr, x0T_ready, tabs_done, arow_ready, tabs_ready = (
            sem("d_bT_ready"), sem("d_cnt_ready"), sem("d_cnt_sum"), sem("d_x0_ready"), sem("d_x0_tr"), sem("d_x0T_ready"), sem("d_tabs_done"),
            sem("d_arow_ready"), sem("d_tabs_ready"))
        rows_ready, ohb_ready, ohw_ready, parted = sem("d_rows_ready"), sem("d_ohb_ready"), sem("d_ohw_ready"), sem("d_parted")
        wk_ready = sem("d_wk_ready")
        gsum_ready, g_turned, g2_ready = sem("d_gsum_ready"), sem("d_g_turned"), sem("d_g2_ready")
        oh_tr, ohT_ready, a_done, z_ready, th_ready, sil_ready, sum_done = (
            sem("d_oh_tr"), sem("d_ohT_ready"), sem("d_a_done"), sem("d_z_ready"), sem("d_th_ready"), sem("d_sil_ready"), sem("d_sum_done"))
        g_done, h_ready, o_done, final_ready = sem("d_g_done"), sem("d_h_ready"), sem("d_o_done"), sem("d_final_ready")
        ab = ps[0:NE, 0:2, :]
        bTb = ps[:, 2, 0:JE].rearrange("p (e j) -> p e j", j=NE)
        x0b = ps[:, 3, 0:DH * NE].rearrange("p (k j) -> p k j", j=NE)
        cb = ps[:, 4, 0:NE]
        gb = ps[:, 5, 0:HID]
        gT = ps[:, 3, 0:2 * JE].rearrange("p (k j e) -> p k j e", j=NE, e=NE)
        ab2 = [ps[:, 0, :], ps[:, 1, :]]
        trb = [ps[:, 6, :].bitcast(BF16), ps[:, 7, :].bitcast(BF16)]
        ob = ps[0:NE, 2, 0:D]
        block = ctx.enter_context(nc.Block())

        @block.sync
        def _(sp):
            sp.dma_start(rows[:, :], m.out_rows).then_inc(rows_ld, 16)
            sp.wait_ge(arow_ready, 1)
            for u in range(2):
                sp.dma_start(a2[u * JE:(u + 1) * JE, :], arow[:, :].rearrange("j (e h) -> j e h", h=HID)).then_inc(a_ld, 16)
            sp.wait_ge(final_ready, 1)
            sp.dma_start(m.out_rows, final[:, :]).then_inc(out_st, 16)
            sp.wait_ge(out_st, 16)

        @block.gpsimd
        def _(pool):
            nc.gpsimd.memset(ad[:, :, :], 0.0).then_inc(tabs_ready, 1)
            pool.wait_ge(a_ld, 32)
            pool.wait_ge(tabs_ready, 1)
            cuts = [0]

            def link(ins):
                cuts[0] += 1
                ins.then_inc(parted, 1)
                pool.wait_ge(parted, cuts[0])

            for part in range(3):
                src = a2 if part == 0 else arest
                for u in range(2):
                    rows_u = slice(u * JE, (u + 1) * JE)
                    d = ad[rows_u, part, u * HID:(u + 1) * HID]
                    link(nc.gpsimd.tensor_copy(d, src[rows_u, :]))
                    if part < 2:
                        link(nc.gpsimd.tensor_tensor(arest[rows_u, :], src[rows_u, :], d, ALU.subtract))
            pool.sem_inc(tabs_ready, 1)
            pool.wait_ge(wk_ready, 1)
            nc.gpsimd.tensor_tensor(ohkw[:, :, :, :], ohk[:, :, :, :], bcast(wk[:, :, :], 3, NE), ALU.mult).then_inc(parted, 1)
            pool.wait_ge(parted, cuts[0] + 1)
            pool.wait_ge(rows_ready, 1)
            by_row = lambda oh: oh[:, :, :, :].rearrange("p t k e -> p (t k) e")

            def one_hots(q, u):
                pool.wait_ge(oh_tr, q + 1)
                nc.gpsimd.tensor_tensor(ohb[:, u, :, :, :], bcast(by_row(ohk)[:, ds(q * (2 * QT), 2 * QT), :], 3, NE),
                                        bcast(span[:, ds(q * (2 * QT), 2 * QT), :], 2, NE), ALU.mult).then_inc(ohb_ready, 1)

            def weights(q, u):
                pool.wait_ge(sum_done, q + 1)
                nc.gpsimd.tensor_tensor(ohw[:, u, :, :, :], bcast(by_row(ohkw)[:, ds(q * (2 * QT), 2 * QT), :], 3, NE),
                                        bcast(span[:, ds(q * (2 * QT), 2 * QT), :], 2, NE), ALU.mult).then_inc(ohw_ready, 1)

            with pool.Fori(0, STEPS // OS) as i:
                for u in range(OS):
                    one_hots(OS * i + u, u)
                    weights(OS * i + u, u)

        @block.scalar
        def _(act):
            act.wait_ge(x0_tr, 1)
            nc.scalar.copy(x0T[:, :, :], x0b).then_inc(x0T_ready, 1)
            act.wait_ge(shifted, 1)
            nc.scalar.activation(s8[0][:, :, :], s8[0][:, :, :], ACT.Exp).then_inc(exped, 1)
            act.wait_ge(tabs_done, 1)
            nc.scalar.copy(arow[:, :], ab.rearrange("p a n -> p (a n)")).then_inc(arow_ready, 1)
            nc.scalar.copy(bT[:, :, :], bTb).then_inc(bT_ready, 1)

            def turned(q, u):
                act.wait_ge(oh_tr, q + (OS + 1))
                act.wait_ge(a_done, q + 1)
                nc.scalar.copy(ohT[:, u, :, :].rearrange("p t n -> p (t n)"), trb[u][:, 0:QT * P]).then_inc(ohT_ready, 1)

            def tanh(q, u):
                act.wait_ge(z_ready, q + 3)
                act.wait_ge(sil_ready, q + 1)
                nc.scalar.activation(th[:, u, :, :], z[:, u, :, :], ACT.Tanh, scale=0.5).then_inc(th_ready, 1)

            turned(0, 0)
            turned(1, 1)
            with act.Fori(0, STEPS // 2 - 1) as i:
                for u in range(2):
                    turned(2 * i + (u + 2), u)
                    tanh(2 * i + u, u)
            for u in range(2):
                tanh(STEPS - 2 + u, u)

        @block.vector
        def _(dve):
            for count, free in ((a_done, 2), (sil_ready, 2), (z_ready, 2), (ohT_ready, 2), (sum_done, OS), (oh_tr, OS)):
                dve.sem_inc(count, free)
            steps = [0]

            def link(ins):
                steps[0] += 1
                ins.then_inc(step, 1)
                dve.wait_ge(step, steps[0])

            V = nc.vector
            link(V.memset(reached[:, :, 0:1], 1.0))
            V.tensor_scalar(x0[:, :], m.x[0:NE, 0, :], m.stat2[0:NE, 0, 0:1], m.rstd2[0:NE, 0:1], ALU.subtract, ALU.mult).then_inc(x0_ready, 1)
            lg = m.logits[:, :, :]
            link(V.reduce_max(one[0][:, :], lg, AX.X))
            V.tensor_tensor(s8[0][:, :, :], lg, bcast(one[0][:, :], 2, NE), ALU.subtract).then_inc(shifted, 1)
            dve.wait_ge(exped, 1)
            link(V.reduce_sum(one[1][:, :], s8[0][:, :, :], AX.X))
            link(V.reciprocal(one[1][:, :], one[1][:, :]))
            link(V.tensor_tensor(scores, s8[0][:, :, :], bcast(one[1][:, :], 2, NE), ALU.mult))
            biased = s8[2]
            link(V.tensor_tensor(biased[:, :, :], scores, bcast(m.ebias[:, :], 1, TILES), ALU.add))

            def first_max(vals, n, tmp, pick):
                link(V.reduce_max(one[2][:, :], vals, AX.X))
                link(V.tensor_tensor(tmp, vals, bcast(one[2][:, :], 2, n), ALU.is_equal))
                link(V.scalar_tensor_tensor(out=tmp, in0=tmp, scalar=-float(n), in1=bcast(m.iota[:, 0:n], 1, TILES), op0=ALU.mult, op1=ALU.add))
                link(V.tensor_reduce(one[2][:, :], tmp, AX.X, ALU.min))
                link(V.tensor_tensor(pick, tmp, bcast(one[2][:, :], 2, n), ALU.is_equal))

            pairs = biased[:, :, :].rearrange("p t (g o) -> p t g o", o=2)
            link(V.tensor_tensor(s4[0][:, :, :], pairs[:, :, :, 0], pairs[:, :, :, 1], ALU.add))
            first_max(s4[0][:, :, :], NG, s4[1][:, :, :], s4[2][:, :, :])
            link(V.scalar_tensor_tensor(out=s4[0][:, :, :], in0=s4[2][:, :, :], scalar=-BIG, in1=s4[0][:, :, :], op0=ALU.mult, op1=ALU.add))
            first_max(s4[0][:, :, :], NG, s4[1][:, :, :], s4[3][:, :, :])
            link(V.tensor_tensor(s4[2][:, :, :], s4[2][:, :, :], s4[3][:, :, :], ALU.add))
            link(V.tensor_scalar(s4[4][:, :, :], s4[2][:, :, :], BIG, -BIG, ALU.mult, ALU.add))
            masked = s8[3]
            mpair = masked[:, :, :].rearrange("p t (g o) -> p t g o", o=2)
            link(V.tensor_tensor(mpair, pairs, bcast(s4[4][:, :, :], 3, 2), ALU.add))
            first_max(masked[:, :, :], NE, s8[4][:, :, :], ohk[:, :, 0, :])
            link(V.scalar_tensor_tensor(out=masked[:, :, :], in0=ohk[:, :, 0, :], scalar=-BIG, in1=masked[:, :, :], op0=ALU.mult, op1=ALU.add))
            first_max(masked[:, :, :], NE, s8[4][:, :, :], ohk[:, :, 1, :])
            V.reduce_sum(cnt[:, :], ohk[:, :, :, :].rearrange("p t k e -> p e (t k)"), AX.X).then_inc(cnt_ready, 1)
            link(V.tensor_tensor(kscore[:, :, :, :], ohk[:, :, :, :], bcast(scores, 2, 2), ALU.mult))
            V.reduce_sum(wk[:, :, :], kscore[:, :, :, :], AX.X).then_inc(wk_ready, 1)
            dve.wait_ge(cnt_sum, 1)
            link(V.tensor_tensor(csum[:, :, :], m.upto[:, :, :], bcast(cb, 1, NE), ALU.mult))
            link(V.reduce_sum(offs[:, :], csum[:, :, :], AX.X))
            link(V.tensor_tensor(reached[:, :, 1:NE + 1], bcast(m.rowno[:, :], 2, NE), bcast(offs[:, :], 1, RT), ALU.is_ge))
            V.tensor_tensor(span[:, :, :], reached[:, :, 0:NE], reached[:, :, 1:NE + 1], ALU.subtract).then_inc(rows_ready, 1)

            def weigh(q, u):
                dve.wait_ge(a_done, q + 3)
                V.tensor_tensor(z[:, u, :, :], ab2[u].rearrange("p (r h) -> p r h", h=HID),
                                bcast(wk[:, :, :].rearrange("p t k -> p (t k)")[:, ds(q * (2 * QT), 2 * QT)], 2, HID), ALU.mult).then_inc(z_ready, 1)

            def gate(q, u):
                dve.wait_ge(th_ready, q + 1)
                dve.wait_ge(sum_done, q + (OS - 1))
                V.scalar_tensor_tensor(out=sil[:, u, :, :], in0=th[:, u, :, :], scalar=1.0, in1=z[:, u, :, :],
                                       op0=ALU.add, op1=ALU.mult).then_inc(sil_ready, 1)

            dve.wait_ge(wk_ready, 1)
            weigh(0, 0)
            weigh(1, 1)
            gate(0, 0)
            with dve.Fori(1, STEPS // 2) as i:
                for u in range(2):
                    dve.wait_ge(sil_ready, 2 * i + (u + 1))
                    weigh(2 * i + u, u)
                    gate(2 * i + (u - 1), 1 - u)
            gate(STEPS - 1, 1)
            dve.wait_ge(g_done, 1)
            V.tensor_copy(gsum[:, :], gb).then_inc(gsum_ready, 1)
            dve.wait_ge(g_turned, 1)
            dve.wait_ge(bT_ready, 1)
            for k, to in ((0, g2), (1, hT)):
                V.scalar_tensor_tensor(out=to[:, :, :], in0=gT[:, k, :, :].rearrange("p j e -> p e j"), scalar=0.5, in1=bT[:, :, :],
                                       op0=ALU.mult, op1=ALU.mult).then_inc(g2_ready, 1)
            dve.wait_ge(g2_ready, 2)
            V.tensor_tensor(hT[:, :, :], hT[:, :, :], g2[:, :, :], ALU.add).then_inc(h_ready, 1)
            dve.wait_ge(rows_ld, 16)
            dve.wait_ge(o_done, 1)
            V.tensor_tensor(final[:, :], rows[:, :], ob, ALU.add).then_inc(final_ready, 1)

        @block.tensor
        def _(pe):
            pe.wait_ge(x0_ready, 1)
            for k in range(DH):
                last = nc.tensor.transpose(x0b[:, k, :], x0[:, k * P:(k + 1) * P], m.ident[0:NE, 0:NE])
            last.then_inc(x0_tr, 1)
            pe.wait_ge(x0T_ready, 1)
            pe.wait_ge(m.experts_ld, 16 * (2 * DH + 1))
            for a in range(2):
                for k in range(DH):
                    nc.tensor.matmul(ab[:, a, :], x0T[:, k, :], m.w1[:, k, 4 * a:4 * a + 4, :].rearrange("p e h -> p (e h)"),
                                     start=(k == 0), stop=(k == DH - 1))
            for e in range(NE):
                for k in range(DH):
                    last = nc.tensor.matmul(bTb[:, e, :], m.w3[:, k, e, :], x0T[:, k, :], start=(k == 0), stop=(k == DH - 1))
            last.then_inc(tabs_done, 1)
            pe.wait_ge(cnt_ready, 1)
            nc.tensor.matmul(cb, m.ones[:, :], cnt[:, :], start=True, stop=True).then_inc(cnt_sum, 1)
            pe.wait_ge(tabs_ready, 2)
            pe.wait_ge(arow_ready, 1)
            nc.tensor.matmul(gb, m.zeros[:, :], m.ones[:, :], start=True, stop=False)

            def turn(q, u, o):
                pe.wait_ge(ohb_ready, q + 1)
                pe.wait_ge(ohT_ready, q + 1)
                for t in range(QT):
                    last = nc.tensor.transpose(trb[u][:, t * P:(t + 1) * P], ohb[:, o, 2 * t:2 * t + 2, :, :].rearrange("p r j e -> p (r j e)"),
                                               m.identb[:, :])
                last.then_inc(oh_tr, 1)

            def gather(q, u):
                pe.wait_ge(ohT_ready, q + 3)
                pe.wait_ge(z_ready, q + 1)
                for t in range(QT):
                    for part in range(3):
                        last = nc.tensor.matmul(ab2[u][:, t * 2 * HID:(t + 1) * 2 * HID], ohT[:, u, t, :], ad[:, part, :],
                                                start=(part == 0), stop=(part == 2))
                last.then_inc(a_done, 1)

            def add_up(q, u, o):
                pe.wait_ge(ohw_ready, q + 1)
                pe.wait_ge(sil_ready, q + 3)
                for t in range(QT):
                    for k in range(2):
                        last = nc.tensor.matmul(gb[k * JE:(k + 1) * JE, :], ohw[:, o, 2 * t + k, :, :].rearrange("p j e -> p (j e)"),
                                                sil[:, u, 2 * t + k, :], start=False, stop=False)
                last.then_inc(sum_done, 1)

            turn(0, 0, 0)
            turn(1, 1, 1)
            gather(0, 0)
            gather(1, 1)
            turn(2, 0, 2)
            with pe.Fori(0, STEPS // OS - 1) as i:
                for o in range(OS):
                    gather(OS * i + (o + 2), o % 2)
                    turn(OS * i + (o + 3), (o + 1) % 2, (o + 3) % OS)
                    add_up(OS * i + o, o % 2, o)
            for q in range(STEPS - OS, STEPS):
                if q + 2 < STEPS:
                    gather(q + 2, q % 2)
                if q + 3 < STEPS:
                    turn(q + 3, (q + 1) % 2, (q + 3) % OS)
                add_up(q, q % 2, q % OS)
            nc.tensor.matmul(gb, m.zeros[:, :], m.ones[:, :], start=False, stop=True).then_inc(g_done, 1)
            pe.wait_ge(gsum_ready, 1)
            nc.tensor.transpose(ps[:, 3, 0:2 * JE], gsum[:, :], m.ident[:, :]).then_inc(g_turned, 1)
            pe.wait_ge(h_ready, 1)
            for e in range(NE):
                last = nc.tensor.matmul(ob, hT[:, e, :], m.w2[:, e, :], start=(e == 0), stop=(e == NE - 1))
            last.then_inc(o_done, 1)


class Memory:
    pass


def preln_attention_moe(nc, x, w_qkvT, b_qk, b_v, w_oT, b_o, w_gateT, w1, w2, w3, sw1T, sw2T, sw3T, expert_bias,
                        ident, headsum, iota, upto, rowno, out):
    m = Memory()
    with ExitStack() as outer:
        def sb(ctx, name, shape, dt):
            return ctx.enter_context(nc.sbuf_tensor(name, shape, dt))

        def sem(name):
            return outer.enter_context(nc.semaphore(name))

        outer_sb = lambda name, shape, dt: sb(outer, name, shape, dt)
        ps = outer.enter_context(nc.psum_tensor("ps", [P, 8, 512], F32))
        m.x = outer_sb("x_sb", [P, TILES, D], F32)
        m.stat1 = outer_sb("stat1", [P, TILES, 2], F32)
        m.rstd1 = outer_sb("rstd1", [P, TILES], F32)
        m.stat2 = outer_sb("stat2", [P, TILES, 2], F32)
        m.rstd2 = outer_sb("rstd2", [P, TILES], F32)
        m.logits = outer_sb("logits", [P, TILES, NE], F32)
        m.wqkv = outer_sb("wqkv", [P, DH, 3 * D], F32)
        m.wo = outer_sb("wo", [P, DH, D], F32)
        m.sw1 = outer_sb("sw1", [P, DH, D], F32)
        m.sw2 = outer_sb("sw2", [P, DH, D], F32)
        m.sw2h = m.wqkv[:, :, 0:D]
        m.sw3 = outer_sb("sw3", [P, DH, D], F32)
        m.wg = outer_sb("wg", [P, DH, NE], F32)
        m.bqk = outer_sb("bqk", [P, 4], F32)
        m.bv = outer_sb("bv", [P, D], F32)
        m.bo = outer_sb("bo", [P, D], F32)
        m.ebias = outer_sb("ebias", [P, NE], F32)
        m.ident = outer_sb("ident", [P, P], F32)
        m.identb = outer_sb("identb", [P, P], BF16)
        m.headsum_f = outer_sb("headsum_f", [P, HPH], F32)
        m.headsum = outer_sb("headsum", [P, HPH], BF16)
        m.ones = outer_sb("ones", [P, P], F32)
        m.zeros = outer_sb("zeros", [P, P], F32)
        m.mhalf = outer_sb("mhalf", [P, GT], F32)
        m.iota = outer_sb("iota", [P, NE], F32)
        m.upto = outer_sb("upto", [P, NE, NE], F32)
        m.rowno = outer_sb("rowno", [P, 2 * TILES], F32)
        m.flag = outer_sb("flag", [1, 1], I32)
        m.scr = [nc.dram_tensor(f"{n}_parts", [3, B * D, L], BF16, kind="Internal").ap() for n in ("q", "k")]
        m.q2_dram = nc.dram_tensor("q_norms_squared", [B * H, L], F32, kind="Internal").ap()
        m.k2_dram = nc.dram_tensor("k_norms_squared", [B * H, GPB], F32, kind="Internal").ap()
        m.shift_dram = nc.dram_tensor("bounds", [B * H, L], BF16, kind="Internal").ap()
        m.n_ld, m.k2_stored, m.k2_step = sem("n_ld"), sem("k2_stored"), sem("k2_step")
        m.v_dram = nc.dram_tensor("v", [P, B * H, KT * C], F32, kind="Internal").ap()
        m.heads_dram = nc.dram_tensor("heads", [B * D, L], F32, kind="Internal").ap()
        flat_x = x.rearrange("b l d -> (b l) d")
        flat_out = out.rearrange("b l d -> (b l) d")
        m.xg = flat_x.rearrange("(g t p) d -> g p t d", t=GT, p=P)
        m.og = flat_out.rearrange("(g t p) d -> g p t d", t=GT, p=P)
        m.out_rows = flat_out[0:NE, :]
        m.w1_dram, m.w2_dram, m.w3_dram = w1, w2, w3
        halves = lambda w: w.rearrange("(k p) n -> p k n", p=P)
        m.first_loads = [
            (m.ident[:, :], ident), (m.wqkv[:, :, :], halves(w_qkvT)), (m.headsum_f[:, :], headsum),
            (m.bqk[:, :], b_qk), (m.bv[:, :], b_v.partition_broadcast(P)),
        ]
        m.late_loads = [
            (m.bo[:, :], b_o.partition_broadcast(P)), (m.wo[:, :, :], halves(w_oT)), (m.wg[:, :, :], halves(w_gateT)),
            (m.sw1[:, :, :], halves(sw1T)), (m.sw2[:, :, :], halves(sw2T)), (m.sw3[:, :, :], halves(sw3T)),
            (m.ebias[:, :], expert_bias.partition_broadcast(P)), (m.iota[:, :], iota.partition_broadcast(P)),
            (m.upto[:, :, :], upto.partition_broadcast(P)), (m.rowno[:, :], rowno),
        ]

        m.x_first, m.x_ld, m.w_ld, m.late_ld = sem("x_first"), sem("x_ld"), sem("w_ld"), sem("late_ld")
        with nc.Block() as block:
            @block.gpsimd
            def _(pool):
                nc.gpsimd.memset(m.mhalf[:, :], -0.5)

            @block.vector
            def _(dve):
                nc.vector.memset(m.ones[:, :], 1.0)
                nc.vector.memset(m.zeros[:, :], 0.0)

        with ExitStack() as ctx:
            m.q2_all = sb(ctx, "q2_all", [P, HEADS * L // P], F32)
            m.k2_all = sb(ctx, "k2_all", [P, GPB], F32)
            m.k2_max = sb(ctx, "k2_max", [P, 1], F32)
            m.shift_all = sb(ctx, "shift_all", [P, HEADS * L // P], BF16)
            qkv_stage(nc, sb, sem, ps, m)
            attention_stage(nc, sb, sem, ps, m, exact=False)
        attention_stage(nc, sb, sem, ps, m, exact=True)
        m.w1 = outer_sb("w1", [P, DH, NE, HID], F32)
        m.w3 = outer_sb("w3", [P, DH, NE, HID], F32)
        m.w2 = outer_sb("w2", [P, NE, D], F32)
        m.experts_ld = sem("experts_ld")
        dense_stage(nc, sb, sem, ps, m)
        routed_stage(nc, sb, sem, ps, m)


def kernel(**inputs):
    import numpy as np
    import concourse.bacc as bacc
    from concourse.bass_utils import run_bass_kernel_spmd

    whole = {k: np.asarray(v) for k, v in inputs.items()}
    plain = lambda name: np.ascontiguousarray(whole[name])
    turned = lambda name: np.ascontiguousarray(whole[name].T)
    row = np.arange(P)[:, None] * 2 + np.arange(TILES * 2)[None, :] // 2 * (2 * P) + np.arange(TILES * 2)[None, :] % 2
    arrays = {
        "x": plain("L0_attn_x"), "w_qkvT": turned("L0_attn_w_qkv"),
        "b_qk": np.ascontiguousarray(whole["L0_attn_b_qkv"][:2 * D].reshape(4, P).T), "b_v": whole["L0_attn_b_qkv"][2 * D:],
        "w_oT": turned("L0_attn_w_o"), "b_o": plain("L0_attn_b_o"), "w_gateT": turned("L0_ffn_w_gate"),
        "w1": plain("L0_ffn_w1"), "w2": plain("L0_ffn_w2"), "w3": plain("L0_ffn_w3"),
        "sw1T": turned("L0_ffn_sw1"), "sw2T": turned("L0_ffn_sw2"), "sw3T": turned("L0_ffn_sw3"),
        "expert_bias": plain("L0_ffn_expert_bias"),
        "ident": np.eye(P, dtype=np.float32),
        "headsum": np.repeat(np.eye(HPH, dtype=np.float32), C, axis=0),
        "iota": np.arange(NE, dtype=np.float32),
        "upto": np.tril(np.ones((NE, NE), dtype=np.float32)),
        "rowno": row.astype(np.float32),
    }
    nc = bacc.Bacc("TRN2", target_bir_lowering=False, num_devices=1)
    args = [nc.dram_tensor(f"in_{n}", list(a.shape), mybir.dt.from_np(a.dtype), kind="ExternalInput").ap() for n, a in arrays.items()]
    out = nc.dram_tensor("out", [B, L, D], F32, kind="ExternalOutput").ap()
    preln_attention_moe(nc, *args, out)
    r = run_bass_kernel_spmd(nc, [{f"in_{n}": a for n, a in arrays.items()}], core_ids=[0])
    return r.results[0]["out"]
```
